# Optimizing a Trainium2 kernel written in Bass

```python
import numpy as np
import jax
import jax.numpy as jnp

def _softmax(x, axis=-1):
    return jax.nn.softmax(x, axis=axis)

def _gelu(x):
    return jax.nn.gelu(x, approximate=True)

def _silu(x):
    return jax.nn.silu(x)

def _sigmoid(x):
    return jax.nn.sigmoid(x)

def _layernorm(x, axis=-1, eps=1e-05):
    m = jnp.mean(x, axis=axis, keepdims=True)
    v = jnp.var(x, axis=axis, keepdims=True)
    return (x - m) / jnp.sqrt(v + eps)

def _scatter_add(tgt, idx, src, axis=0):
    return tgt.at[idx].add(src)

def _segment_sum(src, seg, n):
    return jax.ops.segment_sum(src, seg, n)
kernel_name = 'mk_adaln_attn_ffn_d2_seqx_r4_dc7b98'

def setup_inputs(seed: int=0):
    np.random.seed(seed)
    _w = jnp.asarray

    def _rec_inputs():
        import jax
        import jax.numpy as jnp
        _rk = jax.random.key(seed)
        x = 7.22e-05 + 1 * jax.random.normal(jax.random.fold_in(_rk, 1), (2, 1024, 256), jnp.float32)
        _lenS = 1024 - jax.random.randint(jax.random.fold_in(_rk, 7), (2,), 0, max(1, 1024 // 4) + 1, jnp.int32)
        _lenS2 = 1024 - jax.random.randint(jax.random.fold_in(_rk, 8), (2,), 0, max(1, 1024 // 4) + 1, jnp.int32)
        condB_tauraws = -5.74692 + 0.777674 * jax.random.normal(jax.random.fold_in(_rk, 11), (2,), jnp.float32)
        cond_256 = -0.000235209 + 0.019331 * jax.random.normal(jax.random.fold_in(_rk, 12), (2, 64), jnp.float32)
        condB_bn2 = jnp.zeros((2,), jnp.float32)
        cond_1024 = -4.10585e-05 + 0.0199478 * jax.random.normal(jax.random.fold_in(_rk, 14), (2, 256), jnp.float32)
        itok_B_0_2 = jax.random.randint(jax.random.fold_in(_rk, 15), (2,), 0, 3, jnp.int32)
        condB_zX = jax.random.uniform(jax.random.fold_in(_rk, 16), (2,), jnp.float32, 0.0, 0.983423)
        condB_zY = jax.random.uniform(jax.random.fold_in(_rk, 17), (2,), jnp.float32, 0.0, 0.979075)
        condB_zR = jax.random.uniform(jax.random.fold_in(_rk, 18), (2,), jnp.float32, 0.0, 0.9968)
        itok_B_0_7 = jax.random.randint(jax.random.fold_in(_rk, 19), (2,), 0, 8, jnp.int32)
        return (x, condB_tauraws, cond_256, condB_bn2, cond_1024, itok_B_0_2, condB_zX, condB_zY, condB_zR, itok_B_0_7)
    x, condB_tauraws, cond_256, condB_bn2, cond_1024, itok_B_0_2, condB_zX, condB_zY, condB_zR, itok_B_0_7 = _rec_inputs()

    def _L0_cond_setup():
        import jax, jax.numpy as jnp
        import numpy as np
        import math
        B, T, E, D = (4, 512, 256, 4)

        def _tau_init(t):
            a = 0.1 ** (1.0 / max(t - 1, 1))
            tt = -math.log(max(a, 1e-10))
            return math.log(math.exp(tt) - 1 + 1e-10)

        def causal_ema(b, tau_raw):
            alpha = jnp.exp(-jax.nn.softplus(tau_raw)).astype(b.dtype)

            def step(h, bt):
                h = alpha * h + bt
                return (h, h)
            h0 = jnp.zeros((b.shape[0], b.shape[2]), b.dtype)
            _, hs = jax.lax.scan(step, h0, jnp.swapaxes(b, 0, 1))
            return jnp.swapaxes(hs, 0, 1)
        key = jax.random.key(seed)
        ks = jax.random.split(key, 10)
        s = 0.02
        return {'x': jax.random.normal(ks[0], (B, T, E), jnp.float32), 'tau_ctx': jnp.float32(_tau_init(max(T // 2, 4))), 'tau_raws': jnp.array([_tau_init(max(T // 2 ** i, 2)) for i in range(D)], jnp.float32), 'Wg': jax.random.normal(ks[1], (E, 2 * E), jnp.float32) * s, 'bg': jnp.full((E,), -0.5, jnp.float32), 'Wn1': jax.random.normal(ks[2], (E // 4, E), jnp.float32) * s, 'bn1': jnp.zeros((E // 4,), jnp.float32), 'Wn2': jax.random.normal(ks[3], (D, E // 4), jnp.float32) * s, 'bn2': jnp.zeros((D,), jnp.float32), 'blend': jax.random.normal(ks[4], (D, E), jnp.float32) * s, 'Wsoma': jax.random.normal(ks[5], (E, E), jnp.float32) * s, 'bsoma': jnp.zeros((E,), jnp.float32), 'Wtemp': jax.random.normal(ks[6], (E, E), jnp.float32) * s, 'btemp': jnp.zeros((E,), jnp.float32), 'Wout': jax.random.normal(ks[7], (E, E), jnp.float32) * s, 'gamma': jnp.ones((E,), jnp.float32), 'beta': jnp.zeros((E,), jnp.float32)}
    _L0_cond_all = _L0_cond_setup()
    _L0_cond_in = {k: v for k, v in _L0_cond_all.items() if k in ('tau_ctx', 'Wg', 'bg', 'Wn1', 'bn1', 'Wsoma', 'bsoma', 'Wtemp', 'btemp', 'Wout', 'gamma', 'beta')}
    del _L0_cond_all

    def _L0_attn_setup():
        import jax, jax.numpy as jnp
        import numpy as np
        D_MODEL, EXPAND, D_STATE, D_CONV, HEADDIM = (256, 2, 64, 4, 64)
        D_INNER = EXPAND * D_MODEL
        NHEADS = D_INNER // HEADDIM
        CONV_DIM = D_INNER + 2 * D_STATE
        D_IN_PROJ = 2 * D_INNER + 2 * D_STATE + NHEADS
        EPS = 1e-05

        def _layernorm(x, w, b):
            mu = jnp.mean(x, axis=-1, keepdims=True)
            var = jnp.mean(jnp.square(x - mu), axis=-1, keepdims=True)
            return (x - mu) * jax.lax.rsqrt(var + EPS) * w + b

        def _mamba2(x, in_proj_w, conv_w, conv_b, dt_bias, A_log, D, norm_w, out_proj_w):
            Bt, L, _ = x.shape
            zxbcdt = x @ in_proj_w.T
            z = zxbcdt[..., :D_INNER]
            xBC = zxbcdt[..., D_INNER:D_INNER + CONV_DIM]
            dt = jax.nn.softplus(zxbcdt[..., D_INNER + CONV_DIM:] + dt_bias)
            xp = jnp.pad(xBC, ((0, 0), (D_CONV - 1, 0), (0, 0)))
            conv = conv_b
            for k in range(D_CONV):
                conv = conv + xp[:, k:k + L, :] * conv_w[:, k]
            xBC = jax.nn.silu(conv)
            xs = xBC[..., :D_INNER].reshape(Bt, L, NHEADS, HEADDIM)
            Bm = xBC[..., D_INNER:D_INNER + D_STATE]
            Cm = xBC[..., D_INNER + D_STATE:]
            A = -jnp.exp(A_log)

            def step(h, inp):
                x_t, dt_t, B_t, C_t = inp
                dA = jnp.exp(dt_t * A)
                h = h * dA[:, :, None, None] + (dt_t[:, :, None] * x_t)[..., None] * B_t[:, None, None, :]
                y = jnp.einsum('bhpn,bn->bhp', h, C_t)
                return (h, y)
            h0 = jnp.zeros((Bt, NHEADS, HEADDIM, D_STATE), x.dtype)
            xsT = jnp.moveaxis(xs, 1, 0)
            dtT = jnp.moveaxis(dt, 1, 0)
            BT = jnp.moveaxis(Bm, 1, 0)
            CT = jnp.moveaxis(Cm, 1, 0)
            _, ys = jax.lax.scan(step, h0, (xsT, dtT, BT, CT))
            y = jnp.moveaxis(ys, 0, 1) + xs * D[None, None, :, None]
            y = y.reshape(Bt, L, D_INNER)
            y = y * jax.nn.silu(z)
            y = y * jax.lax.rsqrt(jnp.mean(jnp.square(y), axis=-1, keepdims=True) + EPS) * norm_w
            return y @ out_proj_w.T
        key = jax.random.key(seed)
        ks = jax.random.split(key, 16)
        s = 0.02
        inp = {'x': jax.random.normal(ks[0], (2, 512, D_MODEL), jnp.float32), 'ln1_w': jnp.ones((D_MODEL,), jnp.float32), 'ln1_b': jnp.zeros((D_MODEL,), jnp.float32), 'in_proj_w': jax.random.normal(ks[1], (D_IN_PROJ, D_MODEL), jnp.float32) * s, 'conv_w': jax.random.normal(ks[2], (CONV_DIM, D_CONV), jnp.float32) * 0.3, 'conv_b': jnp.zeros((CONV_DIM,), jnp.float32), 'dt_bias': jnp.log(jnp.expm1(jnp.exp(jax.random.uniform(ks[3], (NHEADS,), jnp.float32, jnp.log(0.001), jnp.log(0.1))))), 'A_log': jnp.log(jax.random.uniform(ks[4], (NHEADS,), jnp.float32, 1.0, 16.0)), 'D': jnp.ones((NHEADS,), jnp.float32), 'norm_w': jnp.ones((D_INNER,), jnp.float32), 'out_proj_w': jax.random.normal(ks[5], (D_MODEL, D_INNER), jnp.float32) * s, 'ln2_w': jnp.ones((D_MODEL,), jnp.float32), 'ln2_b': jnp.zeros((D_MODEL,), jnp.float32), 'mlp_w1': jax.random.normal(ks[6], (4 * D_MODEL, D_MODEL), jnp.float32) * s, 'mlp_b1': jnp.zeros((4 * D_MODEL,), jnp.float32), 'mlp_w2': jax.random.normal(ks[7], (D_MODEL, 4 * D_MODEL), jnp.float32) * s, 'mlp_b2': jnp.zeros((D_MODEL,), jnp.float32)}
        return inp
    _L0_attn_all = _L0_attn_setup()
    _L0_attn_in = {k: v for k, v in _L0_attn_all.items() if k in ('ln1_w', 'ln1_b', 'in_proj_w', 'conv_w', 'conv_b', 'dt_bias', 'A_log', 'D', 'norm_w', 'out_proj_w', 'ln2_w', 'ln2_b', 'mlp_w1', 'mlp_b1', 'mlp_w2', 'mlp_b2')}
    del _L0_attn_all

    def _L0_cond2_setup():
        import jax, jax.numpy as jnp
        import numpy as np
        NEG_INF = -1e+30
        key = jax.random.key(seed)
        k1, k2, k3, k4, k5 = jax.random.split(key, 5)
        B, S, D, A = (16, 256, 256, 64)
        hidden = jax.random.normal(k1, (B, S, D), dtype=jnp.float32)
        W1 = jax.random.normal(k2, (D, A), dtype=jnp.float32) / np.sqrt(D)
        b1 = jax.random.normal(k3, (A,), dtype=jnp.float32) * 0.01
        v = jax.random.normal(k4, (A,), dtype=jnp.float32) / np.sqrt(A)
        prompt_type_ids = jax.random.randint(k5, (B,), 0, 3, dtype=jnp.int32)
        return {'hidden': hidden, 'W1': W1, 'b1': b1, 'v': v, 'prompt_type_ids': prompt_type_ids}
    _L0_cond2_all = _L0_cond2_setup()
    _L0_cond2_in = {k: v for k, v in _L0_cond2_all.items() if k in ('W1', 'b1', 'v')}
    del _L0_cond2_all

    def _L0_ffn_setup():
        import jax, jax.numpy as jnp
        import numpy as np
        B, L, D = (4, 128, 256)
        E, TOP_K = (16, 4)
        F = 4 * D
        key = jax.random.key(seed)
        ks = jax.random.split(key, 6)
        scale = 0.02
        return {'x': jax.random.normal(ks[0], (B, L, D), jnp.float32), 'keys': jax.random.normal(ks[1], (E, D), jnp.float32), 'w1': jax.random.normal(ks[2], (E, F, D), jnp.float32) * scale, 'b1': jnp.zeros((E, F), jnp.float32), 'w2': jax.random.normal(ks[3], (E, D, F), jnp.float32) * scale, 'b2': jnp.zeros((E, D), jnp.float32), 'rw': jax.random.normal(ks[4], (E, D), jnp.float32) * scale, 'rb': jnp.zeros((E,), jnp.float32)}
    _L0_ffn_all = _L0_ffn_setup()
    _L0_ffn_in = {k: v for k, v in _L0_ffn_all.items() if k in ('keys', 'w1', 'b1', 'w2', 'b2', 'rw', 'rb')}
    del _L0_ffn_all

    def _L1_cond_setup():
        import jax, jax.numpy as jnp
        import numpy as np
        key = jax.random.key(seed)
        k1, k2, k3, k4 = jax.random.split(key, 4)
        B, H, W = (64, 256, 256)
        return {'y': jax.random.uniform(k1, (B, H, W), dtype=jnp.float32), 'zX': jax.random.uniform(k2, (B, 1), dtype=jnp.float32), 'zY': jax.random.uniform(k3, (B, 1), dtype=jnp.float32), 'zR': jax.random.uniform(k4, (B, 1), dtype=jnp.float32), 'dx': 1, 'dy': 1}
    _L1_cond_all = _L1_cond_setup()
    _L1_cond_in = {k: v for k, v in _L1_cond_all.items() if k in ()}
    del _L1_cond_all

    def _L1_attn_setup():
        import jax, jax.numpy as jnp
        import numpy as np
        import math
        LAMBDA_INIT = 0.8 - 0.6 * math.exp(-0.3 * 2)
        key = jax.random.key(seed)
        ks = jax.random.split(key, 10)
        B, T, E, hd = (1, 512, 256, 32)
        s = 0.02
        return {'x': jax.random.normal(ks[0], (B, T, E), jnp.float32), 'Wq': jax.random.normal(ks[1], (E, E), jnp.float32) * s, 'Wk': jax.random.normal(ks[2], (E, E), jnp.float32) * s, 'Wv': jax.random.normal(ks[3], (E, E), jnp.float32) * s, 'Wo': jax.random.normal(ks[4], (E, E), jnp.float32) * s, 'lambda_q1': jax.random.normal(ks[5], (hd,), jnp.float32) * 0.1, 'lambda_k1': jax.random.normal(ks[6], (hd,), jnp.float32) * 0.1, 'lambda_q2': jax.random.normal(ks[7], (hd,), jnp.float32) * 0.1, 'lambda_k2': jax.random.normal(ks[8], (hd,), jnp.float32) * 0.1, 'gamma': jnp.ones((2 * hd,), jnp.float32)}
    _L1_attn_all = _L1_attn_setup()
    _L1_attn_in = {k: v for k, v in _L1_attn_all.items() if k in ('Wq', 'Wk', 'Wv', 'Wo', 'lambda_q1', 'lambda_k1', 'lambda_q2', 'lambda_k2', 'gamma')}
    del _L1_attn_all

    def _L1_cond2_setup():
        import jax, jax.numpy as jnp
        import numpy as np
        S, O, H = (8, 256, 256)
        B, N = (32, 128)
        key = jax.random.key(seed)
        k1, k2, k3, k4 = jax.random.split(key, 4)
        x = jax.random.normal(k1, (B, N, H), dtype=jnp.float32)
        subject_id = jax.random.randint(k2, (B,), 0, S)
        wbound = jnp.sqrt(2.0 / 6.0) * jnp.sqrt(3.0 / H)
        weight = jax.random.uniform(k3, (S, O, H), minval=-wbound, maxval=wbound, dtype=jnp.float32)
        bbound = 1.0 / jnp.sqrt(H)
        bias = jax.random.uniform(k4, (S, O), minval=-bbound, maxval=bbound, dtype=jnp.float32)
        return {'x': x, 'subject_id': subject_id, 'weight': weight, 'bias': bias}
    _L1_cond2_all = _L1_cond2_setup()
    _L1_cond2_in = {k: v for k, v in _L1_cond2_all.items() if k in ('weight', 'bias')}
    del _L1_cond2_all

    def _L1_ffn_setup():
        import jax, jax.numpy as jnp
        import numpy as np
        B, S, M, E, DFF = (4, 512, 256, 8, 1024)
        CAPACITY_FACTOR = 1.25

        def _top1_gate(tokens, wg, capacity):
            gates = jax.nn.softmax(tokens @ wg)
            expert_idx = jnp.argmax(gates, axis=-1)
            mask1 = jax.nn.one_hot(expert_idx, gates.shape[-1], dtype=gates.dtype)
            pos = jnp.sum(jnp.cumsum(mask1, axis=0) * mask1, axis=-1).astype(jnp.int32) - 1
            keep = (pos < capacity).astype(gates.dtype)
            mask1c = mask1 * keep[:, None]
            gates1 = jnp.sum(gates * mask1c, axis=-1)
            loc_oh = jax.nn.one_hot(pos, capacity, dtype=gates.dtype)
            combine = gates1[:, None, None] * mask1c[:, :, None] * loc_oh[:, None, :]
            dispatch = (combine > 0).astype(tokens.dtype)
            return (combine, dispatch)
        key = jax.random.key(seed)
        k = jax.random.split(key, 5)
        x = jax.random.normal(k[0], (B, S, M), dtype=jnp.float32)
        wg = jax.random.normal(k[1], (M, E), dtype=jnp.float32) * 0.02
        w1 = jax.random.normal(k[2], (E, M, DFF), dtype=jnp.float32) * 0.02
        b1 = jnp.zeros((E, DFF), dtype=jnp.float32)
        w2 = jax.random.normal(k[3], (E, DFF, M), dtype=jnp.float32) * 0.02
        b2 = jnp.zeros((E, M), dtype=jnp.float32)
        return {'x': x, 'wg': wg, 'w1': w1, 'b1': b1, 'w2': w2, 'b2': b2}
    _L1_ffn_all = _L1_ffn_setup()
    _L1_ffn_in = {k: v for k, v in _L1_ffn_all.items() if k in ('wg', 'w1', 'b1', 'w2', 'b2')}
    del _L1_ffn_all
    return {'x': x, 'condB_tauraws': condB_tauraws, 'cond_256': cond_256, 'condB_bn2': condB_bn2, 'cond_1024': cond_1024, 'itok_B_0_2': itok_B_0_2, 'condB_zX': condB_zX, 'condB_zY': condB_zY, 'condB_zR': condB_zR, 'itok_B_0_7': itok_B_0_7, 'L0_cond_tau_ctx': _L0_cond_in['tau_ctx'], 'L0_cond_Wg': _L0_cond_in['Wg'], 'L0_cond_bg': _L0_cond_in['bg'], 'L0_cond_Wn1': _L0_cond_in['Wn1'], 'L0_cond_bn1': _L0_cond_in['bn1'], 'L0_cond_Wsoma': _L0_cond_in['Wsoma'], 'L0_cond_bsoma': _L0_cond_in['bsoma'], 'L0_cond_Wtemp': _L0_cond_in['Wtemp'], 'L0_cond_btemp': _L0_cond_in['btemp'], 'L0_cond_Wout': _L0_cond_in['Wout'], 'L0_cond_gamma': _L0_cond_in['gamma'], 'L0_cond_beta': _L0_cond_in['beta'], 'L0_attn_ln1_w': _L0_attn_in['ln1_w'], 'L0_attn_ln1_b': _L0_attn_in['ln1_b'], 'L0_attn_in_proj_w': _L0_attn_in['in_proj_w'], 'L0_attn_conv_w': _L0_attn_in['conv_w'], 'L0_attn_conv_b': _L0_attn_in['conv_b'], 'L0_attn_dt_bias': _L0_attn_in['dt_bias'], 'L0_attn_A_log': _L0_attn_in['A_log'], 'L0_attn_D': _L0_attn_in['D'], 'L0_attn_norm_w': _L0_attn_in['norm_w'], 'L0_attn_out_proj_w': _L0_attn_in['out_proj_w'], 'L0_attn_ln2_w': _L0_attn_in['ln2_w'], 'L0_attn_ln2_b': _L0_attn_in['ln2_b'], 'L0_attn_mlp_w1': _L0_attn_in['mlp_w1'], 'L0_attn_mlp_b1': _L0_attn_in['mlp_b1'], 'L0_attn_mlp_w2': _L0_attn_in['mlp_w2'], 'L0_attn_mlp_b2': _L0_attn_in['mlp_b2'], 'L0_cond2_W1': _L0_cond2_in['W1'], 'L0_cond2_b1': _L0_cond2_in['b1'], 'L0_cond2_v': _L0_cond2_in['v'], 'L0_ffn_keys': _L0_ffn_in['keys'], 'L0_ffn_w1': _L0_ffn_in['w1'], 'L0_ffn_b1': _L0_ffn_in['b1'], 'L0_ffn_w2': _L0_ffn_in['w2'], 'L0_ffn_b2': _L0_ffn_in['b2'], 'L0_ffn_rw': _L0_ffn_in['rw'], 'L0_ffn_rb': _L0_ffn_in['rb'], 'L1_attn_Wq': _L1_attn_in['Wq'], 'L1_attn_Wk': _L1_attn_in['Wk'], 'L1_attn_Wv': _L1_attn_in['Wv'], 'L1_attn_Wo': _L1_attn_in['Wo'], 'L1_attn_lambda_q1': _L1_attn_in['lambda_q1'], 'L1_attn_lambda_k1': _L1_attn_in['lambda_k1'], 'L1_attn_lambda_q2': _L1_attn_in['lambda_q2'], 'L1_attn_lambda_k2': _L1_attn_in['lambda_k2'], 'L1_attn_gamma': _L1_attn_in['gamma'], 'L1_cond2_weight': _L1_cond2_in['weight'], 'L1_cond2_bias': _L1_cond2_in['bias'], 'L1_ffn_wg': _L1_ffn_in['wg'], 'L1_ffn_w1': _L1_ffn_in['w1'], 'L1_ffn_b1': _L1_ffn_in['b1'], 'L1_ffn_w2': _L1_ffn_in['w2'], 'L1_ffn_b2': _L1_ffn_in['b2']}

def reference(x, condB_tauraws, cond_256, condB_bn2, cond_1024, itok_B_0_2, condB_zX, condB_zY, condB_zR, itok_B_0_7, L0_cond_tau_ctx, L0_cond_Wg, L0_cond_bg, L0_cond_Wn1, L0_cond_bn1, L0_cond_Wsoma, L0_cond_bsoma, L0_cond_Wtemp, L0_cond_btemp, L0_cond_Wout, L0_cond_gamma, L0_cond_beta, L0_attn_ln1_w, L0_attn_ln1_b, L0_attn_in_proj_w, L0_attn_conv_w, L0_attn_conv_b, L0_attn_dt_bias, L0_attn_A_log, L0_attn_D, L0_attn_norm_w, L0_attn_out_proj_w, L0_attn_ln2_w, L0_attn_ln2_b, L0_attn_mlp_w1, L0_attn_mlp_b1, L0_attn_mlp_w2, L0_attn_mlp_b2, L0_cond2_W1, L0_cond2_b1, L0_cond2_v, L0_ffn_keys, L0_ffn_w1, L0_ffn_b1, L0_ffn_w2, L0_ffn_b2, L0_ffn_rw, L0_ffn_rb, L1_attn_Wq, L1_attn_Wk, L1_attn_Wv, L1_attn_Wo, L1_attn_lambda_q1, L1_attn_lambda_k1, L1_attn_lambda_q2, L1_attn_lambda_k2, L1_attn_gamma, L1_cond2_weight, L1_cond2_bias, L1_ffn_wg, L1_ffn_w1, L1_ffn_b1, L1_ffn_w2, L1_ffn_b2):
    import jax
    import jax.numpy as jnp

    def _L0_cond_ref(x, tau_ctx, tau_raws, Wg, bg, Wn1, bn1, Wn2, bn2, blend, Wsoma, bsoma, Wtemp, btemp, Wout, gamma, beta):
        import jax, jax.numpy as jnp
        import numpy as np
        import math
        B, T, E, D = (4, 512, 256, 4)

        def _tau_init(t):
            a = 0.1 ** (1.0 / max(t - 1, 1))
            tt = -math.log(max(a, 1e-10))
            return math.log(math.exp(tt) - 1 + 1e-10)

        def causal_ema(b, tau_raw):
            alpha = jnp.exp(-jax.nn.softplus(tau_raw)).astype(b.dtype)

            def step(h, bt):
                h = alpha * h + bt
                return (h, h)
            h0 = jnp.zeros((b.shape[0], b.shape[2]), b.dtype)
            _, hs = jax.lax.scan(step, h0, jnp.swapaxes(b, 0, 1))
            return jnp.swapaxes(hs, 0, 1)
        ctx = causal_ema(x, tau_ctx)
        gate_in = jnp.concatenate([x, ctx], axis=-1)
        wg = jax.nn.sigmoid(jnp.einsum('btc,ec->bte', gate_in, Wg) + bg)
        gated = x * wg
        h1 = jax.nn.gelu(jnp.einsum('btc,hc->bth', x, Wn1) + bn1, approximate=False)
        mod = 0.5 + jax.nn.sigmoid(jnp.einsum('bth,dh->btd', h1, Wn2) + bn2)
        traces = jax.vmap(lambda tau, m: causal_ema(gated * m[..., None], tau))(tau_raws, jnp.moveaxis(mod, -1, 0))
        blend_w = jax.nn.softmax(blend, axis=0)
        temporal = jnp.einsum('dbtc,dc->btc', traces, blend_w)
        gate = jax.nn.sigmoid(jnp.einsum('btc,ec->bte', temporal, Wtemp) + btemp)
        soma = jax.nn.gelu(jnp.einsum('btc,ec->bte', x, Wsoma) + bsoma, approximate=False)
        out = jnp.einsum('btc,ec->bte', soma * gate, Wout)
        mu = out.mean(-1, keepdims=True)
        var = out.var(-1, keepdims=True)
        return (out - mu) / jnp.sqrt(var + 1e-05) * gamma + beta

    def _L0_attn_ref(x, ln1_w, ln1_b, in_proj_w, conv_w, conv_b, dt_bias, A_log, D, norm_w, out_proj_w, ln2_w, ln2_b, mlp_w1, mlp_b1, mlp_w2, mlp_b2):
        import jax, jax.numpy as jnp
        import numpy as np
        D_MODEL, EXPAND, D_STATE, D_CONV, HEADDIM = (256, 2, 64, 4, 64)
        D_INNER = EXPAND * D_MODEL
        NHEADS = D_INNER // HEADDIM
        CONV_DIM = D_INNER + 2 * D_STATE
        D_IN_PROJ = 2 * D_INNER + 2 * D_STATE + NHEADS
        EPS = 1e-05

        def _layernorm(x, w, b):
            mu = jnp.mean(x, axis=-1, keepdims=True)
            var = jnp.mean(jnp.square(x - mu), axis=-1, keepdims=True)
            return (x - mu) * jax.lax.rsqrt(var + EPS) * w + b

        def _mamba2(x, in_proj_w, conv_w, conv_b, dt_bias, A_log, D, norm_w, out_proj_w):
            Bt, L, _ = x.shape
            zxbcdt = x @ in_proj_w.T
            z = zxbcdt[..., :D_INNER]
            xBC = zxbcdt[..., D_INNER:D_INNER + CONV_DIM]
            dt = jax.nn.softplus(zxbcdt[..., D_INNER + CONV_DIM:] + dt_bias)
            xp = jnp.pad(xBC, ((0, 0), (D_CONV - 1, 0), (0, 0)))
            conv = conv_b
            for k in range(D_CONV):
                conv = conv + xp[:, k:k + L, :] * conv_w[:, k]
            xBC = jax.nn.silu(conv)
            xs = xBC[..., :D_INNER].reshape(Bt, L, NHEADS, HEADDIM)
            Bm = xBC[..., D_INNER:D_INNER + D_STATE]
            Cm = xBC[..., D_INNER + D_STATE:]
            A = -jnp.exp(A_log)

            def step(h, inp):
                x_t, dt_t, B_t, C_t = inp
                dA = jnp.exp(dt_t * A)
                h = h * dA[:, :, None, None] + (dt_t[:, :, None] * x_t)[..., None] * B_t[:, None, None, :]
                y = jnp.einsum('bhpn,bn->bhp', h, C_t)
                return (h, y)
            h0 = jnp.zeros((Bt, NHEADS, HEADDIM, D_STATE), x.dtype)
            xsT = jnp.moveaxis(xs, 1, 0)
            dtT = jnp.moveaxis(dt, 1, 0)
            BT = jnp.moveaxis(Bm, 1, 0)
            CT = jnp.moveaxis(Cm, 1, 0)
            _, ys = jax.lax.scan(step, h0, (xsT, dtT, BT, CT))
            y = jnp.moveaxis(ys, 0, 1) + xs * D[None, None, :, None]
            y = y.reshape(Bt, L, D_INNER)
            y = y * jax.nn.silu(z)
            y = y * jax.lax.rsqrt(jnp.mean(jnp.square(y), axis=-1, keepdims=True) + EPS) * norm_w
            return y @ out_proj_w.T
        res = x
        h = _layernorm(x, ln1_w, ln1_b)
        h = _mamba2(h, in_proj_w, conv_w, conv_b, dt_bias, A_log, D, norm_w, out_proj_w)
        x = res + h
        res = x
        h = _layernorm(x, ln2_w, ln2_b)
        h = jax.nn.gelu(h @ mlp_w1.T + mlp_b1, approximate=False) @ mlp_w2.T + mlp_b2
        return res + h

    def _L0_cond2_ref(hidden, W1, b1, v, prompt_type_ids):
        import jax, jax.numpy as jnp
        import numpy as np
        NEG_INF = -1e+30
        B, S, D = hidden.shape
        attn_in = jnp.tanh(jnp.einsum('bsd,da->bsa', hidden, W1) + b1)
        scores = jnp.einsum('bsa,a->bs', attn_in, v)
        idx = jnp.arange(S)
        j = idx[:, None]
        l = idx[None, :]
        prefix_m = l <= j
        postfix_m = l >= j
        cloze_m = l != j
        pt = prompt_type_ids[:, None, None]
        mask = jnp.where(pt == 0, prefix_m[None], jnp.where(pt == 1, postfix_m[None], cloze_m[None]))
        masked_scores = jnp.where(mask, scores[:, None, :], NEG_INF)
        p = jax.nn.softmax(masked_scores, axis=-1)
        cnt = jnp.sum(mask, axis=-1).astype(hidden.dtype)
        pooled = jnp.einsum('bjl,bld->bjd', p, hidden) / cnt[..., None]
        return pooled

    def _L0_ffn_ref(x, keys, w1, b1, w2, b2, rw, rb):
        import jax, jax.numpy as jnp
        import numpy as np
        B, L, D = (4, 128, 256)
        E, TOP_K = (16, 4)
        F = 4 * D
        diff = x[:, :, None, :] - keys
        dist2 = jnp.sum(diff * diff, axis=-1)
        logits = -dist2 + jnp.einsum('bld,ed->ble', x, rw) + rb
        topv, topi = jax.lax.top_k(logits, TOP_K)
        w = jax.nn.softmax(topv, axis=-1)
        hidden = jax.nn.gelu(jnp.einsum('bld,efd->blef', x, w1) + b1, approximate=False)
        exp_out = jnp.einsum('blef,edf->bled', hidden, w2) + b2
        sel = jnp.take_along_axis(exp_out, topi[..., None], axis=2)
        fused = jnp.sum(w[..., None] * sel, axis=2)
        return fused

    def _L1_cond_ref(y, zX, zY, zR, dx, dy):
        import jax, jax.numpy as jnp
        import numpy as np
        yp_x = jnp.pad(y, ((0, 0), (0, 0), (1, 1)), mode='reflect')
        lap_x = (yp_x[:, :, :-2] - 2.0 * y + yp_x[:, :, 2:]) / (dx * dx)
        yp_y = jnp.pad(y, ((0, 0), (1, 1), (0, 0)), mode='reflect')
        lap_y = (yp_y[:, :-2, :] - 2.0 * y + yp_y[:, 2:, :]) / (dy * dy)
        du_dt = zX[:, :, None] * lap_x + zY[:, :, None] * lap_y + zR[:, :, None] * y * (1.0 - y)
        return du_dt

    def _L1_attn_ref(x, Wq, Wk, Wv, Wo, lambda_q1, lambda_k1, lambda_q2, lambda_k2, gamma):
        import jax, jax.numpy as jnp
        import numpy as np
        import math
        LAMBDA_INIT = 0.8 - 0.6 * math.exp(-0.3 * 2)
        B, T, E = x.shape
        hd = gamma.shape[0] // 2
        H = E // (2 * hd)
        scaling = hd ** (-0.5)
        q = (x @ Wq.T).reshape(B, T, 2 * H, hd).transpose(0, 2, 1, 3)
        k = (x @ Wk.T).reshape(B, T, 2 * H, hd).transpose(0, 2, 1, 3)
        v = (x @ Wv.T).reshape(B, T, H, 2 * hd).transpose(0, 2, 1, 3)
        mask = jnp.triu(jnp.full((T, T), -jnp.inf, jnp.float32), k=1)
        attn_weights = jnp.einsum('bhtd,bhsd->bhts', q * scaling, k) + mask
        attn_weights = jax.nn.softmax(attn_weights.astype(jnp.float32), axis=-1).astype(x.dtype)
        lambda_1 = jnp.exp(jnp.sum(lambda_q1 * lambda_k1).astype(jnp.float32))
        lambda_2 = jnp.exp(jnp.sum(lambda_q2 * lambda_k2).astype(jnp.float32))
        lambda_full = (lambda_1 - lambda_2 + LAMBDA_INIT).astype(x.dtype)
        aw = attn_weights.reshape(B, H, 2, T, T)
        diff = aw[:, :, 0] - lambda_full * aw[:, :, 1]
        attn = jnp.einsum('bhts,bhsd->bhtd', diff, v)
        a32 = attn.astype(jnp.float32)
        normed = a32 * jax.lax.rsqrt(jnp.mean(a32 * a32, axis=-1, keepdims=True) + 1e-05)
        attn = gamma * normed.astype(attn.dtype)
        attn = attn * (1 - LAMBDA_INIT)
        attn = attn.transpose(0, 2, 1, 3).reshape(B, T, E)
        return attn @ Wo.T

    def _L1_cond2_ref(x, subject_id, weight, bias):
        import jax, jax.numpy as jnp
        import numpy as np
        S, O, H = (8, 256, 256)
        B, N = (32, 128)
        W = weight[subject_id]
        b = bias[subject_id]
        y = jnp.einsum('bnh,boh->bno', x, W) + b[:, None, :]
        return y

    def _L1_ffn_ref(x, wg, w1, b1, w2, b2):
        import jax, jax.numpy as jnp
        import numpy as np
        B, S, M, E, DFF = (4, 512, 256, 8, 1024)
        CAPACITY_FACTOR = 1.25

        def _top1_gate(tokens, wg, capacity):
            gates = jax.nn.softmax(tokens @ wg)
            expert_idx = jnp.argmax(gates, axis=-1)
            mask1 = jax.nn.one_hot(expert_idx, gates.shape[-1], dtype=gates.dtype)
            pos = jnp.sum(jnp.cumsum(mask1, axis=0) * mask1, axis=-1).astype(jnp.int32) - 1
            keep = (pos < capacity).astype(gates.dtype)
            mask1c = mask1 * keep[:, None]
            gates1 = jnp.sum(gates * mask1c, axis=-1)
            loc_oh = jax.nn.one_hot(pos, capacity, dtype=gates.dtype)
            combine = gates1[:, None, None] * mask1c[:, :, None] * loc_oh[:, None, :]
            dispatch = (combine > 0).astype(tokens.dtype)
            return (combine, dispatch)
        d_model = x.shape[-1]
        tokens = x.reshape(-1, d_model)
        T = tokens.shape[0]
        num_experts = wg.shape[1]
        capacity = int(CAPACITY_FACTOR * T / num_experts)
        combine, dispatch = _top1_gate(tokens, wg, capacity)
        dispatched = jnp.einsum('sec,sm->ecm', dispatch, tokens)
        h = jax.nn.relu(jnp.einsum('ecm,emf->ecf', dispatched, w1) + b1[:, None, :])
        expert_out = jnp.einsum('ecf,efm->ecm', h, w2) + b2[:, None, :]
        combined = jnp.einsum('sec,ecm->sm', combine, expert_out)
        return combined.reshape(x.shape)
    x = x + _L0_attn_ref(_L0_cond_ref(x, L0_cond_tau_ctx, condB_tauraws, L0_cond_Wg, L0_cond_bg, L0_cond_Wn1, L0_cond_bn1, cond_256, condB_bn2, cond_1024, L0_cond_Wsoma, L0_cond_bsoma, L0_cond_Wtemp, L0_cond_btemp, L0_cond_Wout, L0_cond_gamma, L0_cond_beta), L0_attn_ln1_w, L0_attn_ln1_b, L0_attn_in_proj_w, L0_attn_conv_w, L0_attn_conv_b, L0_attn_dt_bias, L0_attn_A_log, L0_attn_D, L0_attn_norm_w, L0_attn_out_proj_w, L0_attn_ln2_w, L0_attn_ln2_b, L0_attn_mlp_w1, L0_attn_mlp_b1, L0_attn_mlp_w2, L0_attn_mlp_b2)
    x = x + _L0_ffn_ref(_L0_cond2_ref(x, L0_cond2_W1, L0_cond2_b1, L0_cond2_v, itok_B_0_2), L0_ffn_keys, L0_ffn_w1, L0_ffn_b1, L0_ffn_w2, L0_ffn_b2, L0_ffn_rw, L0_ffn_rb)
    x = x + _L1_attn_ref(_L1_cond_ref(x, condB_zX[:, None], condB_zY[:, None], condB_zR[:, None], 1, 1), L1_attn_Wq, L1_attn_Wk, L1_attn_Wv, L1_attn_Wo, L1_attn_lambda_q1, L1_attn_lambda_k1, L1_attn_lambda_q2, L1_attn_lambda_k2, L1_attn_gamma)
    x = x + _L1_ffn_ref(_L1_cond2_ref(x, itok_B_0_7, L1_cond2_weight, L1_cond2_bias), L1_ffn_wg, L1_ffn_w1, L1_ffn_b1, L1_ffn_w2, L1_ffn_b2)
    return x

_drawn_inputs = setup_inputs


def setup_inputs(seed=0):
    import zlib

    import numpy as np

    out = dict(_drawn_inputs(seed))
    spreads = {'condB_bn2': (0.0, 0.8),
     'L0_cond_bg': (-0.5, 0.6),
     'L0_cond_bn1': (0.0, 0.8),
     'L0_cond_bsoma': (0.0, 0.1),
     'L0_cond_btemp': (0.0, 0.333),
     'L0_cond_gamma': (1.0, 0.2),
     'L0_cond_beta': (0.0, 0.1),
     'L0_attn_ln1_w': (1.0, 0.2),
     'L0_attn_ln1_b': (0.0, 0.1),
     'L0_attn_conv_b': (0.0, 0.1),
     'L0_attn_D': (1.0, 0.539),
     'L0_attn_norm_w': (1.0, 0.2),
     'L0_attn_ln2_w': (1.0, 0.6),
     'L0_attn_ln2_b': (0.0, 0.8),
     'L0_attn_mlp_b1': (0.0, 0.347),
     'L0_attn_mlp_b2': (0.0, 0.1),
     'L0_ffn_b1': (0.0, 0.381),
     'L0_ffn_b2': (0.0, 0.1),
     'L0_ffn_rb': (0.0, 0.8),
     'L1_attn_gamma': (1.0, 0.6),
     'L1_ffn_b1': (0.0, 0.8),
     'L1_ffn_b2': (0.0, 0.66)}
    factors = {'condB_tauraws': 8.0,
     'cond_256': 8.0,
     'cond_1024': 8.0,
     'condB_zX': 4.902,
     'L0_cond_Wn1': 8.0,
     'L0_attn_dt_bias': 8.0,
     'L0_attn_A_log': 8.0,
     'L0_cond2_W1': 8.0,
     'L0_cond2_b1': 8.0,
     'L0_cond2_v': 8.0,
     'L0_ffn_w1': 8.0,
     'L0_ffn_w2': 2.778,
     'L0_ffn_rw': 8.0,
     'L1_attn_lambda_q1': 8.0,
     'L1_attn_lambda_k1': 8.0,
     'L1_attn_lambda_q2': 8.0,
     'L1_attn_lambda_k2': 8.0,
     'L1_cond2_weight': 2.901,
     'L1_cond2_bias': 8.0,
     'L1_ffn_wg': 2.981,
     'L1_ffn_w1': 4.376,
     'L1_ffn_w2': 3.471}
    for name, (base, spread) in spreads.items():
        noise = np.random.default_rng([zlib.crc32(name.encode()), seed]).standard_normal(out[name].shape)
        drawn = base * np.exp(spread * noise) if base else spread * noise
        out[name] = jnp.asarray(drawn.astype(out[name].dtype))
    for name, factor in factors.items():
        out[name] = (out[name] * factor).astype(out[name].dtype)
    return out
```

```python
from contextlib import ExitStack

import numpy as np
import concourse.bass as bass
from concourse import mybir

F32 = mybir.dt.float32
I32 = mybir.dt.int32
U32 = mybir.dt.uint32
BF16 = mybir.dt.bfloat16
F32R = mybir.dt.float32r
ALU = mybir.AluOpType
ACT = mybir.ActivationFunctionType
AX = mybir.AxisListType

B, T, E = 2, 1024, 256
N = B * T
P = 128
NT = N // P
TB = T // P
EB = E // P
W = 512
NW = N // W
HID = 64
DI, NH, DS, HD = 512, 8, 64, 64
CB = 5
FF = 1024
FB = FF // P
E0, TOPK = 16, 4
E1, CAP = 8, 320
NSUB = 8
EPS = 1e-5
NEG = -1e30
LAMBDA_INIT = 0.8 - 0.6 * float(np.exp(-0.3 * 2))

COLS = [("bg", 2), ("bn1", 1), ("bsoma", 2), ("btemp", 2), ("blend", 4), ("wn2", 2), ("ln1w", 2), ("ln1b", 2),
        ("convw", 20), ("convb", 5), ("normw", 4), ("ln2w", 2), ("ln2b", 2), ("mlpb1", 8), ("c2b1", 1), ("c2v", 1),
        ("gam", 2), ("b1a", E0 * FB), ("b1b", E1 * FB)]
ROWS = [("tau", 3), ("bn2", 2), ("gamma", 256), ("beta", 256), ("dtb", 8), ("alog", 8), ("dskip", 8),
        ("mlpb2", 256), ("rb", 16), ("zx", 2), ("zy", 2), ("zr", 2), ("lam", 128)]
CONSTS = [("ident", 128), ("le", 128), ("gt", 128), ("lt", 128), ("ones", 128), ("lap", 512), ("penp", 128),
          ("pens", 128), ("penc", 128), ("delta8", 64), ("penb", 24), ("iota", 16), ("cntp", 8), ("causal", 128)]


def offsets(table):
    at, out = 0, {}
    for name, n in table:
        out[name] = (at, n)
        at += n
    return out, at


COL_AT, NCOL = offsets(COLS)
ROW_AT, NROW = offsets(ROWS)
CONST_AT, NCONST = offsets(CONSTS)


def shape_constants():
    c = np.zeros((P, NCONST), np.float32)
    k = np.arange(P)

    def put(name, a):
        at, n = CONST_AT[name]
        c[:a.shape[0], at:at + n] = a.reshape(a.shape[0], n)

    r, q = k[:, None], k[None, :]
    put("ident", (r == q) * 1.0)
    put("le", (r <= q) * 1.0)
    put("gt", (r > q) * 1.0)
    put("lt", (r < q) * 1.0)
    put("ones", np.ones((P, P)))
    lap = np.zeros((E, E))
    for j in range(E):
        lap[j, j] -= 2.0
        lap[j - 1 if j > 0 else 1, j] += 1.0
        lap[j + 1 if j < E - 1 else E - 2, j] += 1.0
    put("lap", lap.reshape(EB, P, E).transpose(1, 0, 2))
    put("penp", np.where(r <= q, 0.0, NEG))
    put("pens", np.where(r >= q, 0.0, NEG))
    put("penc", np.where(r != q, 0.0, NEG))
    put("delta8", np.broadcast_to(np.eye(8), (P, 8, 8)))
    m = np.arange(8)
    mr, mq = m[:, None], m[None, :]
    put("penb", np.stack([np.where(mr < mq, 0.0, NEG), np.where(mr > mq, 0.0, NEG), np.where(mr != mq, 0.0, NEG)], 1))
    put("iota", np.broadcast_to(np.arange(16), (P, 16)))
    put("cntp", k[:, None] + 1.0 + P * np.arange(8)[None, :])
    put("causal", np.where(q <= r, 0.0, NEG))
    return c


def cond_phase(nc, k):
    ps, c = k.ps, k.col
    with ExitStack() as ctx:
        def sb(name, shape, dt=F32):
            return ctx.enter_context(nc.sbuf_tensor(name, shape, dt))

        k.wsoma, k.wtemp, k.wout = (sb(n, [P, EB, E]) for n in ("wsoma", "wtemp", "wout"))
        k.wn1 = sb("wn1", [P, EB, HID])
        k.wg = sb("wg", [P, 2 * EB, E])
        xT = sb("xT", [P, EB, N])
        ctxT = sb("ctxT", [P, EB, N])
        gatT = sb("gatT", [P, EB, N])
        modT = sb("modT", [P, 2, EB, N])
        somT = sb("somT", [P, EB, N])
        h1T = sb("h1T", [HID, N])
        w2b = sb("w2b", [HID, 2, P])
        alpha = sb("alpha", [P, 3])
        bw = sb("bw", [P, EB, 2])
        tmp = sb("tmp", [P, 8])
        stats = sb("stats", [P, NT, 6])
        mv = sb("mv", [P, NT, 2])
        rstd = sb("rstd", [P, NT])
        SOMA, H1, WG, MOD, GATE, OUT = 0, 8, 12, 20, 28, 36

        block = ctx.enter_context(nc.Block())

        @block.sync
        def _(sp):
            sp.dma_start(k.cols[:, :], k.d["cols"]).then_inc(k.s_small, 16)
            sp.dma_start(k.wsoma[:, :, :], k.d["wsoma"]).then_inc(k.s_small, 16)
            for w in range(NW):
                sp.dma_start(xT[:, :, w * W:(w + 1) * W],
                             k.d["xT"].rearrange("(f p) n -> p f n", p=P)[:, :, w * W:(w + 1) * W]).then_inc(k.s_xT[w], 16)
            sp.dma_start(k.rows[:, :], k.d["rows"].partition_broadcast(P)).then_inc(k.s_rows, 16)
            sp.dma_start(k.wn1[:, :, :], k.d["wn1"]).then_inc(k.s_wA, 16)
            sp.dma_start(k.wg[:, :, :], k.d["wg"]).then_inc(k.s_wA, 16)
            sp.dma_start(k.consts[:, :], k.d["consts"]).then_inc(k.s_wA, 16)
            sp.dma_start(k.wtemp[:, :, :], k.d["wtemp"]).then_inc(k.s_wA, 16)
            sp.dma_start(k.wout[:, :, :], k.d["wout"]).then_inc(k.s_wA, 16)
            sp.dma_start(k.X[:, :, 0:E], k.d["x"].rearrange("(i p) e -> p i e", p=P)).then_inc(k.s_x, 16)
            sp.dma_start(k.win[:, :, :], k.d["win"]).then_inc(k.s_wB, 16)
            sp.dma_start(k.wop[:, :, :], k.d["wop"]).then_inc(k.s_wB, 16)
            sp.dma_start(k.c2w[:, :, :], k.d["c2w"]).then_inc(k.s_wB, 16)
            sp.dma_start(k.keysT[:, :, :], k.d["keysT"]).then_inc(k.s_wB, 16)
            sp.dma_start(k.rwT[:, :, :], k.d["rwT"]).then_inc(k.s_wB, 16)
            sp.dma_start(k.b2a[:, :], k.d["b2a"]).then_inc(k.s_wB, 16)
            sp.wait_ge(k.s_wB, 16 * 6)
            sp.wait_ge(k.s_wA, 16 * 5)
            sp.wait_ge(k.s_x, 16)
            sp.wait_ge(k.s_rows, 16)

        @block.tensor
        def _(pe):
            def product(g, lhs, rhs, m=P, n=W):
                if g >= 8:
                    pe.wait_ge(k.c_evac, g - 7)
                for j, (a, b) in enumerate(zip(lhs, rhs)):
                    last = nc.tensor.matmul(ps[0:m, g % 8, 0:n], a, b, start=(j == 0), stop=(j == len(lhs) - 1))
                last.then_inc(k.c_mm, 1)

            pe.wait_ge(k.s_small, 32)
            for w in range(NW):
                pe.wait_ge(k.s_xT[w], 16)
                tok = slice(w * W, (w + 1) * W)
                for f in range(EB):
                    product(SOMA + w * EB + f, [k.wsoma[:, j, f * P:(f + 1) * P] for j in range(EB)],
                            [xT[:, j, tok] for j in range(EB)])
            pe.wait_ge(k.s_wA, 16 * 5)
            for w in range(NW):
                tok = slice(w * W, (w + 1) * W)
                product(H1 + w, [k.wn1[:, j, :] for j in range(EB)], [xT[:, j, tok] for j in range(EB)], m=HID)
            for w in range(NW):
                tok = slice(w * W, (w + 1) * W)
                pe.wait_ge(k.c_ctx, EB * (w // 2 + 1))
                for f in range(EB):
                    product(WG + w * EB + f, [k.wg[:, j, f * P:(f + 1) * P] for j in range(2 * EB)],
                            [xT[:, 0, tok], xT[:, 1, tok], ctxT[:, 0, tok], ctxT[:, 1, tok]])
            pe.wait_ge(k.c_w2b, 2)
            pe.wait_ge(k.c_evac, H1 + NW)
            for w in range(NW):
                tok = slice(w * W, (w + 1) * W)
                for d in range(2):
                    product(MOD + w * 2 + d, [w2b[:, d, :]], [h1T[:, tok]])
            for w in range(NW):
                tok = slice(w * W, (w + 1) * W)
                pe.wait_ge(k.c_blend, EB * (w // 2 + 1))
                for f in range(EB):
                    product(GATE + w * EB + f, [k.wtemp[:, j, f * P:(f + 1) * P] for j in range(EB)],
                            [gatT[:, j, tok] for j in range(EB)])
            for i in range(NT):
                g, h = OUT + i // 2, i % 2
                if h == 0:
                    pe.wait_ge(k.c_evac, g - 7)
                pe.wait_ge(k.c_sg, i // 4 + 1)
                for j in range(EB):
                    last = nc.tensor.matmul(ps[:, g % 8, h * E:(h + 1) * E], somT[:, j, i * P:(i + 1) * P],
                                            k.wout[:, j, :], start=(h == 0 and j == 0), stop=(j == EB - 1),
                                            skip_group_check=True)
                last.then_inc(k.c_out, 1)

        @block.scalar
        def _(act):
            act.wait_ge(k.s_rows, 16)
            nc.scalar.activation(tmp[:, 0:3], k.rows[:, 0:3], ACT.Exp).then_inc(k.c_tau, 1)
            act.wait_ge(k.c_bdiff, 2)
            nc.scalar.activation(bw[:, :, :], bw[:, :, :], ACT.Exp).then_inc(k.c_bexp, 1)
            act.wait_ge(k.s_small, 32)

            def evac(g, out, func, bias, m=P):
                act.wait_ge(k.c_mm, g + 1)
                nc.scalar.activation(out, ps[0:m, g % 8, :], func, bias=bias).then_inc(k.c_evac, 1)

            for w in range(NW):
                for f in range(EB):
                    evac(SOMA + w * EB + f, somT[:, f, w * W:(w + 1) * W], ACT.Gelu, c("bsoma", f))
            for w in range(NW):
                evac(H1 + w, h1T[:, w * W:(w + 1) * W], ACT.Gelu, c("bn1", 0)[0:HID], m=HID)
            for w in range(NW):
                for f in range(EB):
                    evac(WG + w * EB + f, gatT[:, f, w * W:(w + 1) * W], ACT.Sigmoid, c("bg", f))
            for w in range(NW):
                for d in range(2):
                    evac(MOD + w * 2 + d, modT[:, d, 0, w * W:(w + 1) * W], ACT.Sigmoid, k.row("bn2", d))
            for w in range(NW):
                for f in range(EB):
                    evac(GATE + w * EB + f, ctxT[:, f, w * W:(w + 1) * W], ACT.Sigmoid, c("btemp", f))
            for r in range(2):
                act.wait_ge(k.c_var, r + 1)
                nc.scalar.activation(rstd[:, :], mv[:, :, 1], ACT.Sqrt, bias=k.eps[:, 0:1]).then_inc(k.c_sd, 1)

        @block.vector
        def _(dve):
            then = chain(k, dve, "dve")
            nc.vector.memset(k.eps[:, :], EPS).then_inc(k.c_init, 1)
            nc.vector.memset(k.X[:, :, E:E + 1], 1.0).then_inc(k.c_init, 1)
            dve.wait_ge(k.c_init, 2)
            dve.wait_ge(k.c_tau, 1)
            then(nc.vector.tensor_scalar(tmp[:, 3:6], tmp[:, 0:3], 1.0, None, ALU.add))
            then(nc.vector.reciprocal(alpha[:, :], tmp[:, 3:6]))
            dve.wait_ge(k.s_small, 32)
            bl = c("blend", 0, 4).rearrange("p (f d) -> p f d", d=2)
            then(nc.vector.tensor_tensor(tmp[:, 6:8], bl[:, :, 0], bl[:, :, 1], ALU.max))
            for d in range(2):
                nc.vector.tensor_tensor(bw[:, :, d], bl[:, :, d], tmp[:, 6:8], ALU.subtract).then_inc(k.c_bdiff, 1)
            dve.wait_ge(k.s_wA, 16 * 5)
            for d in range(2):
                nc.vector.tensor_scalar(w2b[:, d, :], k.const("ones")[0:HID], c("wn2", d)[0:HID], None,
                                        ALU.mult).then_inc(k.c_w2b, 1)
            for w in range(NW):
                dve.wait_ge(k.s_xT[w], 16)
            for b in range(B):
                tok = slice(b * T, (b + 1) * T)
                for f in range(EB):
                    nc.vector.tensor_tensor_scan(ctxT[:, f, tok], alpha[:, 2:3].to_broadcast([P, T]), xT[:, f, tok],
                                                 0.0, ALU.mult, ALU.add).then_inc(k.c_ctx, 1)
            dve.wait_ge(k.c_bexp, 1)
            then(nc.vector.tensor_tensor(tmp[:, 0:2], bw[:, :, 0], bw[:, :, 1], ALU.add))
            then(nc.vector.reciprocal(tmp[:, 2:4], tmp[:, 0:2]))
            for d in range(2):
                then(nc.vector.tensor_tensor(bw[:, :, d], bw[:, :, d], tmp[:, 2:4], ALU.mult))
            for b in range(B):
                tok = slice(b * T, (b + 1) * T)
                dve.wait_ge(k.c_evac, WG + 2 * EB * (b + 1))
                for f in range(EB):
                    then(nc.vector.tensor_tensor(gatT[:, f, tok], gatT[:, f, tok], xT[:, f, tok], ALU.mult))
                dve.wait_ge(k.c_evac, MOD + 4 * (b + 1))
                for f in (1, 0):
                    for d in range(2):
                        then(nc.vector.scalar_tensor_tensor(modT[:, d, f, tok], modT[:, d, 0, tok], 0.5,
                                                            gatT[:, f, tok], ALU.add, ALU.mult))
                        then(nc.vector.tensor_tensor_scan(modT[:, d, f, tok], alpha[:, d:d + 1].to_broadcast([P, T]),
                                                          modT[:, d, f, tok], 0.0, ALU.mult, ALU.add))
                    then(nc.vector.tensor_scalar(gatT[:, f, tok], modT[:, 0, f, tok], bw[:, f, 0:1], None, ALU.mult))
                    nc.vector.scalar_tensor_tensor(gatT[:, f, tok], modT[:, 1, f, tok], bw[:, f, 1:2],
                                                   gatT[:, f, tok], ALU.mult, ALU.add).then_inc(k.c_blend, 1)
            for w in range(NW):
                tok = slice(w * W, (w + 1) * W)
                dve.wait_ge(k.c_evac, GATE + EB * (w + 1))
                nc.vector.tensor_tensor(somT[:, :, tok], somT[:, :, tok], ctxT[:, :, tok],
                                        ALU.mult).then_inc(k.c_sg, 1)
            for i in range(NT):
                g, h = OUT + i // 2, i % 2
                dve.wait_ge(k.c_out, 2 * (i // 2) + 2)
                then(nc.vector.bn_stats(stats[:, i, :], ps[:, g % 8, h * E:(h + 1) * E]))
                last = nc.vector.bn_aggr(mv[:, i, :], stats[:, i, :])
                if i < NT - 1:
                    then(last)
            last.then_inc(k.c_var, 1)
            dve.wait_ge(k.c_sd, 1)
            then(nc.vector.reciprocal(rstd[:, :], rstd[:, :]))
            for i in range(NT):
                g, h = OUT + i // 2, i % 2
                nc.vector.tensor_scalar(k.res0[:, i, :], ps[:, g % 8, h * E:(h + 1) * E], mv[:, i, 0:1],
                                        rstd[:, i:i + 1], ALU.subtract, ALU.mult).then_inc(k.c_norm, 1)
            for i in range(NT):
                dve.wait_ge(k.c_aff, 2 * (i // 4 + 1))
                then(nc.vector.bn_stats(stats[:, i, :], k.res0[:, i, :]))
                last = nc.vector.bn_aggr(mv[:, i, :], stats[:, i, :])
                if i < NT - 1:
                    then(last)
            last.then_inc(k.c_var, 1)
            dve.wait_ge(k.c_sd, 2)
            then(nc.vector.reciprocal(rstd[:, :], rstd[:, :]))
            for i in range(NT):
                nc.vector.tensor_scalar(k.hn[:, i, :], k.res0[:, i, :], mv[:, i, 0:1], rstd[:, i:i + 1],
                                        ALU.subtract, ALU.mult).then_inc(k.c_hn, 1)

        @block.gpsimd
        def _(pool):
            pool.wait_ge(k.s_rows, 16)
            for q in range(4):
                r = k.res0[:, 4 * q:4 * q + 4, :]
                pool.wait_ge(k.c_norm, 4 * (q + 1))
                nc.gpsimd.tensor_tensor(r, r, k.row("gamma", 0, E).unsqueeze(1).to_broadcast([P, 4, E]),
                                        ALU.mult).then_inc(k.c_aff, 1)
                pool.wait_ge(k.c_aff, 2 * q + 1)
                nc.gpsimd.tensor_tensor(r, r, k.row("beta", 0, E).unsqueeze(1).to_broadcast([P, 4, E]),
                                        ALU.add).then_inc(k.c_aff, 1)


def chain(k, eng, name):
    sem, count = k.chains[name]

    def then(ins):
        count[0] += 1
        ins.then_inc(sem, 1)
        eng.wait_ge(sem, count[0])
    return then


def transpose_phase(nc, k, src, dst, wname, bname, s):
    with nc.Block() as block:
        @block.tensor
        def _(pe):
            for g in range(NW * EB):
                w, f = g // EB, g % EB
                for j in range(4):
                    last = nc.tensor.transpose(k.ps[:, g, j * P:(j + 1) * P], src[:, 4 * w + j, f * P:(f + 1) * P],
                                               k.const("ident"))
                last.then_inc(s["mm"], 1)

        def evacuate(eng, which):
            for g in range(which, NW * EB, 2):
                w, f = g // EB, g % EB
                eng.wait_ge(s["mm"], g + 1)
                out = dst[:, f, w * W:(w + 1) * W]
                if wname is None:
                    (nc.vector.tensor_copy if which else nc.scalar.copy)(out, k.ps[:, g, :])
                elif bname is None:
                    if which:
                        nc.vector.tensor_scalar(out, k.ps[:, g, :], k.col(wname, f), None, ALU.mult)
                    else:
                        nc.scalar.activation(out, k.ps[:, g, :], ACT.Copy, scale=k.col(wname, f))
                elif which:
                    nc.vector.tensor_scalar(out, k.ps[:, g, :], k.col(wname, f), k.col(bname, f), ALU.mult, ALU.add)
                else:
                    nc.scalar.activation(out, k.ps[:, g, :], ACT.Identity, bias=k.col(bname, f),
                                         scale=k.col(wname, f))

        @block.scalar
        def _(act):
            evacuate(act, 0)

        @block.vector
        def _(dve):
            evacuate(dve, 1)


def inproj_phase(nc, k):
    ps = k.ps
    with ExitStack() as ctx:
        def sb(name, shape, dt=F32):
            return ctx.enter_context(nc.sbuf_tensor(name, shape, dt))

        pre = sb("pre", [P, 2, B, T + 3])
        z = sb("dtz", [P, 4, P])
        DT = 7

        block = ctx.enter_context(nc.Block())

        @block.tensor
        def _(pe):
            for i in range(NT):
                for j in range(EB):
                    last = nc.tensor.matmul(ps[:, DT, i * NH:(i + 1) * NH], k.hT[:, j, i * P:(i + 1) * P],
                                            k.win[:, j, 2 * DI + 2 * DS:], start=(i == 0 and j == 0),
                                            stop=(j == EB - 1), skip_group_check=True)
            last.then_inc(k.i_dt, 1)
            for g in range(CB * NW):
                cb, w = g // NW, g % NW
                if g >= 7:
                    pe.wait_ge(k.i_evac, g - 6)
                for j in range(EB):
                    last = nc.tensor.matmul(ps[:, g % 7, :], k.win[:, j, DI + cb * P:DI + (cb + 1) * P],
                                            k.hT[:, j, w * W:(w + 1) * W], start=(j == 0), stop=(j == EB - 1))
                last.then_inc(k.i_mm, 1)
            pe.wait_ge(k.i_dtA, 1)
            pe.wait_ge(k.i_sp, 1)
            nc.tensor.matmul(ps[:, DT, 0:P], k.const("le"), k.dtA[:, :], start=True, stop=True)
            nc.tensor.matmul(ps[0:DS, DT, P:2 * P], k.const("ones", 0, DS), k.dtA[:, :], start=False, stop=True,
                             skip_group_check=True).then_inc(k.i_cs, 1)

        @block.scalar
        def _(act):
            then = chain(k, act, "act")
            nc.scalar.activation(k.expA[:, :], k.row("alog", 0, NH), ACT.Exp).then_inc(k.i_expA, 1)
            act.wait_ge(k.i_abs, 1)
            then(nc.scalar.activation(z[:, 1, :], z[:, 1, :], ACT.Exp))
            nc.scalar.activation(z[:, 2, :], z[:, 1, :], ACT.Ln, bias=1.0).then_inc(k.i_ln, 1)
            for g in range(CB * NW):
                cb, w = g // NW, g % NW
                act.wait_ge(k.i_mm, g + 1)
                if cb >= 2 and w == 0:
                    act.wait_ge(k.i_conv, cb - 1)
                if g == 0:
                    act.wait_ge(k.i_pad, 1)
                at = 3 + (w % 2) * W
                nc.scalar.copy(pre[:, cb % 2, w // 2, at:at + W], ps[:, g % 7, :]).then_inc(k.i_evac, 1)
                if w == NW - 1 and cb >= 1:
                    act.wait_ge(k.i_conv, cb)
                    nc.scalar.activation(k.post[:, cb - 1, :], k.post[:, cb - 1, :], ACT.Silu).then_inc(k.i_silu, 1)
            act.wait_ge(k.i_conv, CB)
            nc.scalar.activation(k.post[:, CB - 1, :], k.post[:, CB - 1, :], ACT.Silu).then_inc(k.i_silu, 1)
            act.wait_ge(k.i_cs, 1)
            nc.scalar.activation(k.ecs[:, :], ps[:, DT, 0:P], ACT.Exp)
            nc.scalar.activation(k.etot[:, :], ps[0:DS, DT, P:2 * P], ACT.Exp)

        @block.vector
        def _(dve):
            then = chain(k, dve, "dve")
            nc.vector.memset(pre[:, :, :, 0:3], 0.0).then_inc(k.i_pad, 1)
            dve.wait_ge(k.i_dt, 1)
            heads = "p (i h) -> p i h"
            then(nc.vector.tensor_tensor(z[:, 0, :].rearrange(heads, h=NH), ps[:, DT, 0:P].rearrange(heads, h=NH),
                                         k.row("dtb", 0, NH).unsqueeze(1).to_broadcast([P, NT, NH]), ALU.add))
            then(nc.vector.tensor_scalar(z[:, 1, :], z[:, 0, :], -1.0, None, ALU.mult))
            nc.vector.tensor_tensor(z[:, 1, :], z[:, 0, :], z[:, 1, :], ALU.min).then_inc(k.i_abs, 1)
            dve.wait_ge(k.i_ln, 1)
            then(nc.vector.tensor_scalar(z[:, 3, :], z[:, 1, :], 1.0, -1.0, ALU.add, ALU.add))
            then(nc.vector.tensor_scalar(k.dt[:, :], z[:, 3, :], 0.0, None, ALU.is_equal))
            then(nc.vector.tensor_tensor(z[:, 3, :], z[:, 3, :], k.dt[:, :], ALU.add))
            then(nc.vector.tensor_tensor(z[:, 2, :], z[:, 2, :], k.dt[:, :], ALU.add))
            then(nc.vector.reciprocal(z[:, 3, :], z[:, 3, :]))
            then(nc.vector.tensor_tensor(z[:, 2, :], z[:, 2, :], z[:, 3, :], ALU.mult))
            then(nc.vector.tensor_tensor(z[:, 2, :], z[:, 2, :], z[:, 1, :], ALU.mult))
            then(nc.vector.scalar_tensor_tensor(k.dt[:, :], z[:, 0, :], 0.0, z[:, 2, :], ALU.max,
                                                ALU.add)) 
            nc.vector.tensor_scalar(z[:, 0, :], k.dt[:, :], -1.0, None, ALU.mult).then_inc(k.i_sp, 1)
            dve.wait_ge(k.i_sp, 1)
            dve.wait_ge(k.i_expA, 1)
            nc.vector.tensor_tensor(k.dtA[:, :].rearrange(heads, h=NH), z[:, 0, :].rearrange(heads, h=NH),
                                    k.expA[:, :].unsqueeze(1).to_broadcast([P, NT, NH]), ALU.mult).then_inc(k.i_dtA, 1)
            for cb in range(CB):
                dve.wait_ge(k.i_evac, NW * (cb + 1))
                out = k.post[:, cb, :].rearrange("p (b t) -> p b t", b=B)
                then(nc.vector.tensor_scalar(out, pre[:, cb % 2, :, 3:], k.col("convw", 4 * cb + 3),
                                             k.col("convb", cb), ALU.mult, ALU.add))
                for q in (2, 1, 0):
                    last = nc.vector.scalar_tensor_tensor(out, pre[:, cb % 2, :, q:q + T],
                                                          k.col("convw", 4 * cb + q), out, ALU.mult, ALU.add)
                    if q:
                        then(last)
                last.then_inc(k.i_conv, 1)

        @block.sync
        def _(sp):
            sp.wait_ge(k.i_silu, CB)
            sp.dma_start(k.CT[:, :], k.post[DS:2 * DS, CB - 1, :]).then_inc(k.s_ct, 16)
            sp.wait_ge(k.s_ct, 16)


def ssd_phase(nc, k):
    ps = k.ps
    Z, XT, BC, SEG, YD, YO, S = 0, 1, 2, 3, 5, 6, 7
    with ExitStack() as ctx:
        def sb(name, shape, dt=F32):
            return ctx.enter_context(nc.sbuf_tensor(name, shape, dt))

        sz = sb("sz", [P, 2, DI])
        xst = sb("xst", [P, 2, DI])
        xD = sb("xD", [P, 2, DI])
        xdt = sb("xdt", [P, 2, DI])
        xdd = sb("xdd", [P, 2, DI])
        Bt = sb("Bt", [P, 2, DS])
        cbm = sb("cbm", [P, P])
        G = sb("G", [P, NH, P])
        Ex = sb("Ex", [P, NH, P])
        M = sb("M", [P, 2, NH, P])
        y = sb("y", [P, 2, DI])
        h = sb("h", [DS, DI])
        hd = sb("hd", [DS, DI])
        sq = sb("sq", [P, DI])
        ss = sb("ss", [P, NT])
        yo = sb("yo", [P, DI])

        def heads(ap):
            return ap.rearrange("p (h w) -> p h w", h=NH)

        def per_head(t, i, p=P, w=HD):
            return t[0:p, i * NH:(i + 1) * NH].unsqueeze(2).to_broadcast([p, NH, w])

        def off(i):
            return i - i // TB

        block = ctx.enter_context(nc.Block())

        @block.tensor
        def _(pe):
            def prepare(i):
                tok = slice(i * P, (i + 1) * P)
                if i:
                    pe.wait_ge(k.m_xst, i)
                for f in range(4):
                    last = nc.tensor.transpose(ps[:, XT, f * P:(f + 1) * P], k.post[:, f, tok], k.const("ident"))
                last.then_inc(k.m_xt, 1)
                if i:
                    pe.wait_ge(k.m_bcu, 2 * i)
                nc.tensor.transpose(ps[:, BC, 0:DS], k.post[0:DS, 4, tok], k.const("ident", 0, DS)[0:DS, :])
                nc.tensor.matmul(ps[:, BC, P:2 * P], k.post[0:DS, 4, tok], k.CT[:, tok], start=True,
                                 stop=True).then_inc(k.m_bc, 1)
                pe.wait_ge(k.m_G, i + 1)
                if i:
                    pe.wait_ge(k.m_E, i)
                for q in range(NH):
                    last = nc.tensor.matmul(ps[:, SEG + q // 4, (q % 4) * P:(q % 4 + 1) * P], G[:, q, :],
                                            k.const("le"), start=(q % 4 == 0), stop=True, skip_group_check=True)
                last.then_inc(k.m_seg, 1)
                if i:
                    pe.wait_ge(k.m_sz, i)
                for j in range(EB):
                    last = nc.tensor.matmul(ps[:, Z, :], k.hT[:, j, tok], k.win[:, j, 0:DI], start=(j == 0),
                                            stop=(j == EB - 1))
                last.then_inc(k.m_z, 1)

            def combine(i):
                c = i % TB
                pe.wait_ge(k.m_M, i + 1)
                pe.wait_ge(k.m_xdt, i + 1)
                if i:
                    pe.wait_ge(k.m_y2, i)
                for q in range(NH):
                    last = nc.tensor.matmul(ps[:, YD, q * HD:(q + 1) * HD], M[:, i % 2, q, :],
                                            xdt[:, i % 2, q * HD:(q + 1) * HD], start=(q == 0), stop=True,
                                            skip_group_check=True)
                last.then_inc(k.m_yd, 1)
                if c:
                    pe.wait_ge(k.m_h, i - i // TB)
                    if off(i) > 1:
                        pe.wait_ge(k.m_y1, off(i) - 1)
                    nc.tensor.matmul(ps[:, YO, :], k.CT[:, i * P:(i + 1) * P], h[:, :], start=True,
                                     stop=True).then_inc(k.m_yo, 1)
                if c < TB - 1:
                    pe.wait_ge(k.m_xdd, i + 1)
                    if i:
                        pe.wait_ge(k.m_h, i - i // TB)
                    nc.tensor.matmul(ps[0:DS, S, :], Bt[:, i % 2, :], xdd[:, i % 2, :], start=True,
                                     stop=True).then_inc(k.m_S, 1)

            prepare(0)
            for i in range(NT):
                if i + 1 < NT:
                    prepare(i + 1)
                combine(i)

        @block.scalar
        def _(act):
            def square(i):
                act.wait_ge(k.m_yg, i + 1)
                nc.scalar.activation(sq[:, :], k.yg(i), ACT.Square, accum_out=ss[:, i:i + 1]).then_inc(k.m_ss, 1)
                act.wait_ge(k.m_ss, i + 1)

            for i in range(NT):
                act.wait_ge(k.m_xt, i + 1)
                if i >= 2:
                    act.wait_ge(k.m_xD, i - 1)
                    act.wait_ge(k.m_xdt, i - 1)
                nc.scalar.copy(xst[:, i % 2, :], ps[:, XT, :]).then_inc(k.m_xst, 1)
                act.wait_ge(k.m_seg, i + 1)
                if i:
                    act.wait_ge(k.m_M, i)
                    act.wait_ge(k.m_xdd, i)
                nc.scalar.activation(Ex[:, :, :], ps[:, SEG:SEG + 2, :].rearrange("p b (q t) -> p (b q) t", q=4),
                                     ACT.Exp).then_inc(k.m_E, 1)
                act.wait_ge(k.m_z, i + 1)
                if i >= 2:
                    act.wait_ge(k.m_yg, i - 1)
                nc.scalar.activation(sz[:, i % 2, :], ps[:, Z, :], ACT.Silu).then_inc(k.m_sz, 1)
                if i >= 2:
                    square(i - 2)
            square(NT - 2)
            square(NT - 1)
            nc.scalar.activation(k.rms[:, :], ss[:, :], ACT.Sqrt, bias=k.eps[:, 0:1], scale=1.0 / DI)

        @block.gpsimd
        def _(pool):
            for i in range(NT):
                if i:
                    pool.wait_ge(k.m_seg, i)
                nc.gpsimd.tensor_tensor(G[:, :, :], k.const("gt").unsqueeze(1).to_broadcast([P, NH, P]),
                                        per_head(k.dtA, i, w=P), ALU.mult).then_inc(k.m_G, 1)
                pool.wait_ge(k.m_xst, i + 1)
                if i >= 2:
                    pool.wait_ge(k.m_xdd, i - 1)
                    pool.wait_ge(k.m_yd, i - 1)
                nc.gpsimd.tensor_tensor(heads(xdt[:, i % 2, :]), heads(xst[:, i % 2, :]), per_head(k.dt, i),
                                        ALU.mult).then_inc(k.m_xdt, 1)
                if i >= 2:
                    pool.wait_ge(k.m_y2, i - 1)
                nc.gpsimd.tensor_tensor(heads(xD[:, i % 2, :]), heads(xst[:, i % 2, :]),
                                        k.row("dskip", 0, NH).unsqueeze(2).to_broadcast([P, NH, HD]),
                                        ALU.mult).then_inc(k.m_xD, 1)

        @block.vector
        def _(dve):
            then = chain(k, dve, "dve")

            def prepare(i):
                dve.wait_ge(k.m_bc, i + 1)
                if i >= 2:
                    dve.wait_ge(k.m_S, i - 1 - (i - 1) // TB)
                nc.vector.tensor_copy(Bt[:, i % 2, :], ps[:, BC, 0:DS]).then_inc(k.m_bcu, 1)
                if i:
                    dve.wait_ge(k.m_M, i)
                nc.vector.tensor_tensor(cbm[:, :], ps[:, BC, P:2 * P], k.const("le"), ALU.mult).then_inc(k.m_bcu, 1)
                dve.wait_ge(k.m_bcu, 2 * i + 2)
                dve.wait_ge(k.m_E, i + 1)
                if i >= 2:
                    dve.wait_ge(k.m_yd, i - 1)
                nc.vector.tensor_tensor(M[:, i % 2, :, :], Ex[:, :, :],
                                        cbm[:, :].unsqueeze(1).to_broadcast([P, NH, P]), ALU.mult).then_inc(k.m_M, 1)
                dve.wait_ge(k.m_xdt, i + 1)
                nc.vector.tensor_tensor(heads(xdd[:, i % 2, :]), heads(xdt[:, i % 2, :]),
                                        Ex[:, :, P - 1:P].to_broadcast([P, NH, HD]), ALU.mult).then_inc(k.m_xdd, 1)

            def combine(i):
                c, yi = i % TB, y[:, i % 2, :]
                dve.wait_ge(k.m_yd, i + 1)
                dve.wait_ge(k.m_xD, i + 1)
                nc.vector.tensor_tensor(yi, ps[:, YD, :], xD[:, i % 2, :], ALU.add).then_inc(k.m_y2, 1)
                dve.wait_ge(k.m_y2, i + 1)
                if c:
                    dve.wait_ge(k.m_yo, off(i))
                    nc.vector.tensor_tensor(heads(yo[:, :]), heads(ps[:, YO, :]), per_head(k.ecs, i),
                                            ALU.mult).then_inc(k.m_y1, 1)
                    dve.wait_ge(k.m_y1, off(i))
                    then(nc.vector.tensor_tensor(yi, yi, yo[:, :], ALU.add))
                if c == 0:
                    dve.wait_ge(k.m_S, i - i // TB + 1)
                    nc.vector.tensor_copy(h[:, :], ps[0:DS, S, :]).then_inc(k.m_h, 1)
                elif c < TB - 1:
                    then(nc.vector.tensor_tensor(heads(hd[:, :]), heads(h[:, :]), per_head(k.etot, i, p=DS),
                                                 ALU.mult))
                    dve.wait_ge(k.m_S, i - i // TB + 1)
                    nc.vector.tensor_tensor(h[:, :], hd[:, :], ps[0:DS, S, :], ALU.add).then_inc(k.m_h, 1)
                dve.wait_ge(k.m_sz, i + 1)
                nc.vector.tensor_tensor(k.yg(i), yi, sz[:, i % 2, :], ALU.mult).then_inc(k.m_yg, 1)

            for f in range(4):
                nc.vector.tensor_scalar(k.wop[:, f, :], k.wop[:, f, :], k.col("normw", f), None, ALU.mult)
            prepare(0)
            for i in range(NT):
                if i + 1 < NT:
                    prepare(i + 1)
                combine(i)



def outproj_phase(nc, k):
    ps = k.ps
    with ExitStack() as ctx:
        def sb(name, shape, dt=F32):
            return ctx.enter_context(nc.sbuf_tensor(name, shape, dt))

        ygT = sb("ygT", [P, 3, 4, P])
        stats = sb("stats2", [P, NT, 6])
        mv = sb("mv2", [P, NT, 2])
        rstd = sb("rstd2", [P, NT])
        TR, OUT = 0, 4
        block = ctx.enter_context(nc.Block())

        @block.sync
        def _(sp):
            sp.dma_start(k.mw1[:, :, :], k.d["mw1"]).then_inc(k.s_mw, 16)
            sp.dma_start(k.mw2[:, :, :], k.d["mw2"]).then_inc(k.s_mw, 16)

        @block.tensor
        def _(pe):
            def turn(i):
                if i >= 4:
                    pe.wait_ge(k.o_evac, i - 3)
                for f in range(4):
                    last = nc.tensor.transpose(ps[:, TR + i % 4, f * P:(f + 1) * P], k.yg(i)[:, f * P:(f + 1) * P],
                                               k.const("ident"))
                last.then_inc(k.o_tr, 1)

            turn(0)
            turn(1)
            for i in range(NT):
                if i + 2 < NT:
                    turn(i + 2)
                pe.wait_ge(k.o_evac, i + 1)
                if i >= 4:
                    pe.wait_ge(k.o_x, i - 3)
                for f in range(4):
                    last = nc.tensor.matmul(ps[:, OUT + i % 4, 0:E], ygT[:, i % 3, f, :], k.wop[:, f, :],
                                            start=(f == 0), stop=(f == 3))
                last.then_inc(k.o_mm, 1)

        @block.scalar
        def _(act):
            for i in range(NT):
                act.wait_ge(k.o_tr, i + 1)
                if i >= 3:
                    act.wait_ge(k.o_mm, i - 2)
                nc.scalar.copy(ygT[:, i % 3, :, :], ps[:, TR + i % 4, :].rearrange("p (f t) -> p f t", f=4)
                               ).then_inc(k.o_evac, 1)
            act.wait_ge(k.o_var, 1)
            nc.scalar.activation(rstd[:, :], mv[:, :, 1], ACT.Sqrt, bias=k.eps[:, 0:1]).then_inc(k.o_sd, 1)

        @block.vector
        def _(dve):
            then = chain(k, dve, "dve")
            then(nc.vector.reciprocal(k.rms[:, :], k.rms[:, :]))
            for i in range(NT):
                dve.wait_ge(k.o_mm, i + 1)
                nc.vector.scalar_tensor_tensor(k.res0[:, i, :], ps[:, OUT + i % 4, 0:E], k.rms[:, i:i + 1],
                                               k.res0[:, i, :], ALU.mult, ALU.add).then_inc(k.o_x, 1)
                dve.wait_ge(k.o_x, i + 1)
                then(nc.vector.bn_stats(stats[:, i, :], k.res0[:, i, :]))
                last = nc.vector.bn_aggr(mv[:, i, :], stats[:, i, :])
            last.then_inc(k.o_var, 1)
            dve.wait_ge(k.o_sd, 1)
            then(nc.vector.reciprocal(rstd[:, :], rstd[:, :]))
            for i in range(NT):
                nc.vector.tensor_scalar(k.hn[:, i, :], k.res0[:, i, :], mv[:, i, 0:1], rstd[:, i:i + 1],
                                        ALU.subtract, ALU.mult)

        @block.gpsimd
        def _(pool):
            for q in range(4):
                pool.wait_ge(k.o_x, 4 * (q + 1))
                r, xs = k.res0[:, 4 * q:4 * q + 4, :], k.X[:, 4 * q:4 * q + 4, 0:E]
                nc.gpsimd.tensor_tensor(xs, xs, r, ALU.add).then_inc(k.o_add, 1)
                pool.wait_ge(k.o_add, q + 1)
                nc.gpsimd.tensor_tensor(xs, xs, k.row("mlpb2", 0, E).unsqueeze(1).to_broadcast([P, 4, E]), ALU.add)


def mlp_phase(nc, k):
    ps = k.ps
    with ExitStack() as ctx:
        hid = ctx.enter_context(nc.sbuf_tensor("hid", [P, 2, FB, W], F32))
        block = ctx.enter_context(nc.Block())

        @block.tensor
        def _(pe):
            def up(w):
                for f in range(FB):
                    g = w * FB + f
                    if g >= 4:
                        pe.wait_ge(k.p_act, g - 3)
                    for j in range(EB):
                        last = nc.tensor.matmul(ps[:, g % 4, :], k.mw1[:, j, f * P:(f + 1) * P],
                                                k.hT[:, j, w * W:(w + 1) * W], start=(j == 0), stop=(j == EB - 1))
                    last.then_inc(k.p_up, 1)

            def down(w):
                pe.wait_ge(k.p_act, (w + 1) * FB)
                for t in range(4):
                    i = 4 * w + t
                    if i >= 4:
                        pe.wait_ge(k.p_x, i - 3)
                    for f in range(FB):
                        last = nc.tensor.matmul(ps[:, 4 + t, 0:E], hid[:, w % 2, f, t * P:(t + 1) * P],
                                                k.mw2[:, f, :], start=(f == 0), stop=(f == FB - 1))
                    last.then_inc(k.p_down, 1)

            pe.wait_ge(k.s_mw, 32)
            up(0)
            for w in range(NW):
                if w + 1 < NW:
                    up(w + 1)
                down(w)

        @block.scalar
        def _(act):
            for w in range(NW):
                for f in range(FB):
                    act.wait_ge(k.p_up, w * FB + f + 1)
                    if w >= 2 and f == 0:
                        act.wait_ge(k.p_down, 4 * (w - 1))
                    nc.scalar.activation(hid[:, w % 2, f, :], ps[:, (w * FB + f) % 4, :], ACT.Gelu,
                                         bias=k.col("mlpb1", f)).then_inc(k.p_act, 1)

        @block.vector
        def _(dve):
            for i in range(NT):
                dve.wait_ge(k.p_down, i + 1)
                nc.vector.tensor_tensor(k.X[:, i, 0:E], k.X[:, i, 0:E], ps[:, 4 + i % 4, 0:E],
                                        ALU.add).then_inc(k.p_x, 1)


def pool_phase(nc, k):
    ps = k.ps
    A, ROW, MISC, UU, PO = 0, 2, 4, 5, 6
    with ExitStack() as ctx:
        def sb(name, shape, dt=F32):
            return ctx.enter_context(nc.sbuf_tensor(name, shape, dt))

        aT = sb("aT", [HID, N])
        vb = sb("vb", [HID, P])
        srow = sb("srow", [P, N])
        srev = sb("srev", [P, T])
        scol = sb("scol", [P, NT])
        pm = sb("pm", [P, T + 1])
        sm = sb("sm", [P, T + 1])
        negm = sb("negm", [P, T])
        D = sb("D", [P, TB, P])
        it = sb("it", [P, B], I32)
        fl = sb("fl", [P, 2, 3, B])
        pen = sb("pen", [P, P])
        pbl = sb("pbl", [8, 8])
        mx = sb("mx", [P, TB])
        mxd = sb("mxd", [8, TB])
        mxc = sb("mxc", [8, 1])
        e8 = sb("e8", [P, TB, 8])
        ex = sb("ex", [P, TB])
        wt = sb("wt", [8, TB, P])
        U = sb("U", [8, E + 1])
        cnt = sb("cnt", [P, NT])
        den = sb("den", [P, NT])
        pool_rows = k.pooled
        block = ctx.enter_context(nc.Block())

        @block.sync
        def _(sp):
            sp.dma_start(it[:, :], k.d["itok0"].partition_broadcast(P)).then_inc(k.s_it, 16)

        @block.tensor
        def _(pe):
            for w in range(NW):
                if w >= 2:
                    pe.wait_ge(k.q_tanh, w - 1)
                for j in range(EB):
                    last = nc.tensor.matmul(ps[0:HID, A + w % 2, :], k.c2w[:, j, :], k.hT[:, j, w * W:(w + 1) * W],
                                            start=(j == 0), stop=(j == EB - 1))
                last.then_inc(k.q_a, 1)
            pe.wait_ge(k.q_vb, 1)
            for w in range(NW):
                pe.wait_ge(k.q_tanh, w + 1)
                if w >= 2:
                    pe.wait_ge(k.q_srow, w - 1)
                nc.tensor.matmul(ps[:, ROW + w % 2, :], vb[:, :], aT[:, w * W:(w + 1) * W], start=True,
                                 stop=True).then_inc(k.q_row, 1)
            for i in range(NT):
                last = nc.tensor.matmul(ps[:, MISC, i:i + 1], aT[:, i * P:(i + 1) * P], k.col("c2v", 0)[0:HID],
                                        start=(i == 0), stop=True, skip_group_check=True)
            last.then_inc(k.q_col, 1)
            for b in range(B):
                pe.wait_ge(k.q_e8, b + 1)
                if b:
                    pe.wait_ge(k.q_U, b)
                for c in range(TB):
                    last = nc.tensor.matmul(ps[0:8, UU, 0:E + 1], e8[:, c, :], k.X[:, b * TB + c, :],
                                            start=(c == 0), stop=(c == TB - 1))
                last.then_inc(k.q_sum, 1)
                pe.wait_ge(k.q_U, b + 1)
                pe.wait_ge(k.q_D, b + 1)
                for c in range(TB):
                    i = b * TB + c
                    if i >= 2:
                        pe.wait_ge(k.q_out, i - 1)
                    nc.tensor.matmul(ps[:, PO + i % 2, 0:E + 1], D[:, c, :], k.X[:, i, :], start=True, stop=False)
                    nc.tensor.matmul(ps[:, PO + i % 2, 0:E + 1], wt[:, c, :], U[:, :], start=False,
                                     stop=True).then_inc(k.q_pool, 1)

        @block.scalar
        def _(act):
            then = chain(k, act, "act")
            for w in range(NW):
                act.wait_ge(k.q_a, w + 1)
                nc.scalar.activation(aT[:, w * W:(w + 1) * W], ps[0:HID, A + w % 2, :], ACT.Tanh,
                                     bias=k.col("c2b1", 0)[0:HID]).then_inc(k.q_tanh, 1)
            for w in range(NW):
                act.wait_ge(k.q_row, w + 1)
                nc.scalar.copy(srow[:, w * W:(w + 1) * W], ps[:, ROW + w % 2, :]).then_inc(k.q_srow, 1)
            for b in range(B):
                act.wait_ge(k.q_ex, b + 1)
                then(nc.scalar.activation(ex[:, :], ex[:, :], ACT.Exp))
                nc.scalar.activation(ex[:, :], ex[:, :], ACT.Copy).then_inc(k.q_exp, 1)
                act.wait_ge(k.q_dex, b + 1)
                for c in range(TB):
                    last = nc.scalar.activation(D[:, c, :], D[:, c, :], ACT.Exp,
                                                bias=scol[:, b * TB + c:b * TB + c + 1])
                nc.scalar.activation(wt[:, :, :], wt[:, :, :], ACT.Exp, bias=mxc[:, 0:1]).then_inc(k.q_D, 1)

        @block.vector
        def _(dve):
            then = chain(k, dve, "dve")
            nc.vector.tensor_scalar(vb[:, :], k.const("ones")[0:HID], k.col("c2v", 0)[0:HID], None,
                                    ALU.mult).then_inc(k.q_vb, 1)
            dve.wait_ge(k.s_it, 16)
            then(nc.vector.tensor_copy(cnt[:, 0:B], it[:, :]))
            then(nc.vector.tensor_scalar(fl[:, 0, 0, :], cnt[:, 0:B], 0.0, None, ALU.is_equal))
            then(nc.vector.tensor_scalar(fl[:, 0, 1, :], cnt[:, 0:B], 1.0, None, ALU.is_equal))
            then(nc.vector.tensor_tensor(fl[:, 0, 2, :], fl[:, 0, 0, :], fl[:, 0, 1, :], ALU.add))
            then(nc.vector.tensor_scalar(fl[:, 0, 2, :], fl[:, 0, 2, :], -1.0, 1.0, ALU.mult, ALU.add))
            then(nc.vector.tensor_scalar(fl[:, 1, :, :], fl[:, 0, :, :], -1.0, None, ALU.mult))

            def blend(out, pieces, b, sign=0, p=P):
                f = lambda q: fl[0:p, sign, q, b:b + 1]
                then(nc.vector.tensor_scalar(out, pieces[0], f(0), None, ALU.mult))
                for q in (1, 2):
                    then(nc.vector.scalar_tensor_tensor(out, pieces[q], f(q), out, ALU.mult, ALU.add))

            then(nc.vector.memset(pm[:, 0:1], NEG))
            then(nc.vector.memset(sm[:, T:T + 1], NEG))
            dve.wait_ge(k.q_col, 1)
            then(nc.vector.tensor_copy(scol[:, :], ps[:, MISC, 0:NT]))
            for b in range(B):
                dve.wait_ge(k.q_srow, 2 * (b + 1))
                s = srow[:, b * T:(b + 1) * T]
                if b:
                    dve.wait_ge(k.q_sum, b)
                    dve.wait_ge(k.q_D, b)
                then(nc.vector.tensor_reduce(mx[:, :], s.rearrange("p (c t) -> p c t", c=TB), AX.X, ALU.max))
                nc.vector.tensor_tensor(ex[:, :], scol[:, b * TB:(b + 1) * TB], mx[:, :],
                                        ALU.subtract).then_inc(k.q_ex, 1)
                dve.wait_ge(k.q_exp, b + 1)
                nc.vector.tensor_tensor(e8[:, :, :], k.const("delta8", 0, 64).rearrange("p (c q) -> p c q", c=8),
                                        ex[:, :].unsqueeze(2).to_broadcast([P, TB, 8]), ALU.mult).then_inc(k.q_e8, 1)
                then(nc.vector.tensor_tensor(mxd[:, :], mx[0:8, :], k.const("ident", 0, 8)[0:8], ALU.mult))
                then(nc.vector.tensor_reduce(mxc[:, :], mxd[:, :], AX.X, ALU.add))
                then(nc.vector.tensor_tensor_scan(pm[:, 1:T + 1], s, s, NEG, ALU.max, ALU.max))
                rev = srow[:, b * T:(b + 1) * T][:, ::-1]
                then(nc.vector.tensor_tensor_scan(sm[:, 0:T][:, ::-1], rev, rev, NEG, ALU.max, ALU.max))
                then(nc.vector.tensor_tensor(srev[:, :], pm[:, 0:T], sm[:, 1:T + 1], ALU.max))
                blend(negm[:, :], (pm[:, 1:T + 1], sm[:, 0:T], srev[:, :]), b, sign=1)
                blend(pen[:, :], (k.const("penp"), k.const("pens"), k.const("penc")), b)
                pb = k.const("penb", 0, 24)[0:8].rearrange("p (q c) -> p q c", q=3)
                blend(pbl[:, :], (pb[:, 0, :], pb[:, 1, :], pb[:, 2, :]), b, p=8)
                if b:
                    dve.wait_ge(k.q_pool, b * TB)
                rows = negm[:, :].rearrange("p (c t) -> p c t", c=TB)
                then(nc.vector.tensor_tensor(D[:, :, :], rows, pen[:, :].unsqueeze(1).to_broadcast([P, TB, P]),
                                             ALU.add))
                nc.vector.tensor_tensor(wt[:, :, :], rows[0:8], pbl[:, :].unsqueeze(2).to_broadcast([8, TB, P]),
                                        ALU.add).then_inc(k.q_dex, 1)
                cb = cnt[:, b * TB:(b + 1) * TB]
                then(nc.vector.tensor_scalar(srev[:, 0:TB], k.const("cntp", 0, TB), -1.0, T + 1.0, ALU.mult, ALU.add))
                then(nc.vector.tensor_scalar(srev[:, TB:2 * TB], k.const("cntp", 0, TB), 0.0, T - 1.0, ALU.mult,
                                             ALU.add))
                blend(cb, (k.const("cntp", 0, TB), srev[:, 0:TB], srev[:, TB:2 * TB]), b)
                dve.wait_ge(k.q_sum, b + 1)
                nc.vector.tensor_copy(U[:, :], ps[0:8, UU, 0:E + 1]).then_inc(k.q_U, 1)
                for c in range(TB):
                    i = b * TB + c
                    dve.wait_ge(k.q_pool, i + 1)
                    then(nc.vector.tensor_tensor(den[:, i:i + 1], ps[:, PO + i % 2, E:E + 1], cnt[:, i:i + 1],
                                                 ALU.mult))
                    then(nc.vector.reciprocal(den[:, i:i + 1], den[:, i:i + 1]))
                    nc.vector.tensor_scalar(pool_rows[:, i, :], ps[:, PO + i % 2, 0:E], den[:, i:i + 1], None,
                                            ALU.mult).then_inc(k.q_out, 1)


JT = dict(sel=0, n=17, base=33, free=49, pairs=66, blk=82)
JOB = 256
NB = N // JOB


def route_phase(nc, k):
    ps = k.ps
    KK, LG, TR, CNT, BO = 0, 1, 2, 6, 7
    with ExitStack() as ctx:
        def sb(name, shape, dt=F32):
            return ctx.enter_context(nc.sbuf_tensor(name, shape, dt))

        k2 = sb("k2", [P, EB, E0])
        G = sb("Gr", [P, EB, E0])
        rb = sb("rbk", [P, E0])
        lg = sb("lg", [P, NT, E0])
        v8 = sb("v8", [P, NT, 8])
        i8 = sb("i8", [P, NT, 8], U32)
        fi = sb("fi", [P, NT, 8])
        w4 = sb("w4", [P, NT, TOPK])
        den = sb("den4", [P, NT])
        oh = sb("oh", [P, NT, E0])
        wd = sb("wd", [P, NT, E0])
        wT = sb("wT", [E0, N])
        a = sb("act", [1, E0, NB])
        rk = sb("rk", [1, E0, NB])
        nj = sb("nj", [1, 6, E0])
        big = sb("big", [1, E0 * NB * NB])
        lst = sb("lst", [1, E0, NB])
        perm = sb("perm", [1, E0, E0])
        jf = sb("jf", [1, JT["blk"] + E0 * NB])
        block = ctx.enter_context(nc.Block())

        @block.tensor
        def _(pe):
            pe.wait_ge(k.r_k2, 1)
            for j in range(EB):
                last = nc.tensor.matmul(ps[:, KK, 0:E0], k.const("ones"), k2[:, j, :], start=(j == 0),
                                        stop=(j == EB - 1))
            last.then_inc(k.r_kk, 1)
            pe.wait_ge(k.r_G, 1)
            for i in range(NT):
                for j in range(EB):
                    last = nc.tensor.matmul(ps[:, LG, i * E0:(i + 1) * E0], k.hT[:, j, i * P:(i + 1) * P], G[:, j, :],
                                            start=(i == 0 and j == 0), stop=(j == EB - 1), skip_group_check=True)
            last.then_inc(k.r_lg, 1)
            pe.wait_ge(k.r_wd, 1)
            nc.tensor.matmul(ps[:, CNT, 0:NT * E0], k.const("ones"), k.wE[:, :, :].rearrange("p e i -> p (e i)"),
                             start=True, stop=True).then_inc(k.r_cnt, 1)
            for g in range(NW):
                for t in range(4):
                    last = nc.tensor.transpose(ps[0:E0, TR + g, t * P:(t + 1) * P], wd[:, 4 * g + t, :],
                                               k.const("ident"))
                last.then_inc(k.r_tr, 1)
            for i in range(NT):
                if i % 4 == 0:
                    pe.wait_ge(k.r_wT, i // 4 + 1)
                bank = BO if i % 2 else LG
                if i >= 2:
                    pe.wait_ge(k.r_b2, i - 1)
                nc.tensor.matmul(ps[:, bank, 0:E], wT[:, i * P:(i + 1) * P], k.b2a[:, :], start=True,
                                 stop=True).then_inc(k.r_bo, 1)

        @block.scalar
        def _(act):
            act.wait_ge(k.r_v, 1)
            nc.scalar.activation(w4[:, :, :], w4[:, :, :], ACT.Exp).then_inc(k.r_exp, 1)
            for g in range(NW):
                act.wait_ge(k.r_tr, g + 1)
                nc.scalar.copy(wT[:, g * W:(g + 1) * W], ps[0:E0, TR + g, :]).then_inc(k.r_wT, 1)

        @block.gpsimd
        def _(pool):
            for j in range(EB):
                nc.gpsimd.tensor_copy(k.hTh[:, j, :], k.hT[:, j, :]).then_inc(k.r_hi, 1)
            pool.wait_ge(k.r_lg, 1)
            for j in range(EB):
                pool.wait_ge(k.r_hi, j + 1)
                nc.gpsimd.tensor_tensor(k.hTl[:, j, :], k.hT[:, j, :], k.hTh[:, j, :], ALU.subtract)

        @block.vector
        def _(dve):
            then = chain(k, dve, "dve")
            nc.vector.tensor_tensor(k2[:, :, :], k.keysT[:, :, :], k.keysT[:, :, :], ALU.mult).then_inc(k.r_k2, 1)
            nc.vector.scalar_tensor_tensor(G[:, :, :], k.keysT[:, :, :], 2.0, k.rwT[:, :, :], ALU.mult,
                                           ALU.add).then_inc(k.r_G, 1)
            dve.wait_ge(k.r_kk, 1)
            then(nc.vector.tensor_tensor(rb[:, :], k.row("rb", 0, E0), ps[:, KK, 0:E0], ALU.subtract))
            dve.wait_ge(k.r_lg, 1)
            then(nc.vector.tensor_tensor(lg[:, :, :], ps[:, LG, 0:NT * E0].rearrange("p (i e) -> p i e", e=E0),
                                         rb[:, :].unsqueeze(1).to_broadcast([P, NT, E0]), ALU.add))
            for i in range(NT):
                last = nc.vector.max(v8[:, i, :], lg[:, i, :])
            then(last)
            for i in range(NT):
                last = nc.vector.max_index(i8[:, i, :], v8[:, i, :], lg[:, i, :])
            nc.vector.tensor_tensor(w4[:, :, :], v8[:, :, 0:TOPK], v8[:, :, 0:1].to_broadcast([P, NT, TOPK]),
                                    ALU.subtract).then_inc(k.r_v, 1)
            then(last)
            then(nc.vector.tensor_copy(fi[:, :, :], i8[:, :, :]))
            dve.wait_ge(k.r_exp, 1)
            then(nc.vector.tensor_reduce(den[:, :], w4[:, :, :], AX.X, ALU.add))
            then(nc.vector.reciprocal(den[:, :], den[:, :]))
            then(nc.vector.tensor_tensor(w4[:, :, :], w4[:, :, :], den[:, :].unsqueeze(2).to_broadcast([P, NT, TOPK]),
                                         ALU.mult))
            then(nc.vector.memset(wd[:, :, :], 0.0))
            for q in range(TOPK):
                wide = lambda ap: ap.to_broadcast([P, NT, E0])
                then(nc.vector.tensor_tensor(oh[:, :, :], k.const("iota", 0, E0).unsqueeze(1).to_broadcast([P, NT, E0]),
                                             wide(fi[:, :, q:q + 1]), ALU.is_equal))
                then(nc.vector.tensor_tensor(oh[:, :, :], oh[:, :, :], wide(w4[:, :, q:q + 1]), ALU.mult))
                then(nc.vector.tensor_tensor(wd[:, :, :], wd[:, :, :], oh[:, :, :], ALU.add))
            nc.vector.tensor_copy(k.wE[:, :, :], wd[:, :, :].rearrange("p i e -> p e i")).then_inc(k.r_wd, 1)
            dve.wait_ge(k.r_cnt, 1)
            sums = ps[0:1, CNT, 0:NT * E0].rearrange("p (e b t) -> p e b t", e=E0, b=NB)
            then(nc.vector.tensor_reduce(a[:, :, :], sums, AX.X, ALU.add))
            then(nc.vector.tensor_scalar(a[:, :, :], a[:, :, :], 0.0, None, ALU.is_gt))
            then(nc.vector.tensor_reduce(nj[:, 0, :], a[:, :, :], AX.X, ALU.add))
            then(nc.vector.memset(rk[:, :, 0:1], 0.0))
            for q in range(1, NB):
                then(nc.vector.tensor_tensor(rk[:, :, q:q + 1], rk[:, :, q - 1:q], a[:, :, q - 1:q], ALU.add))
            iota = k.const("iota", 0, E0)[0:1]
            eq = big[:, 0:E0 * NB * NB].rearrange("p (e r b) -> p e r b", e=E0, r=NB)
            then(nc.vector.tensor_tensor(a[:, :, :], a[:, :, :], iota[:, 0:NB].unsqueeze(1).to_broadcast([1, E0, NB]),
                                         ALU.mult))
            for e in range(E0):
                then(nc.vector.tensor_tensor(eq[:, e], rk[:, e:e + 1, :].to_broadcast([1, NB, NB]),
                                             iota[:, 0:NB].unsqueeze(2).to_broadcast([1, NB, NB]), ALU.is_equal))
                then(nc.vector.tensor_tensor(eq[:, e], eq[:, e], a[:, e:e + 1, :].to_broadcast([1, NB, NB]), ALU.mult))
            then(nc.vector.tensor_reduce(lst[:, :, :], eq, AX.X, ALU.add))
            then(nc.vector.tensor_scalar(nj[:, 1, :], nj[:, 0, :], 0.0, None, ALU.is_gt))
            then(nc.vector.memset(nj[:, 5, :], 0.0))
            then(nc.vector.tensor_tensor_scan(nj[:, 2, :], nj[:, 1, :], nj[:, 5, :], 0.0, ALU.add, ALU.add))
            then(nc.vector.tensor_tensor(nj[:, 3, :], iota, nj[:, 2, :], ALU.subtract))
            then(nc.vector.tensor_scalar(nj[:, 3, :], nj[:, 3, :], nj[:, 2, E0 - 1:E0], None, ALU.add))
            then(nc.vector.scalar_tensor_tensor(nj[:, 2, :], nj[:, 2, :], 1.0, nj[:, 3, :], ALU.subtract, ALU.subtract))
            then(nc.vector.tensor_tensor(nj[:, 2, :], nj[:, 2, :], nj[:, 1, :], ALU.mult))
            then(nc.vector.tensor_tensor(nj[:, 2, :], nj[:, 2, :], nj[:, 3, :], ALU.add))
            pm = perm[:, :, :]
            then(nc.vector.tensor_tensor(pm, nj[:, 2:3, :].to_broadcast([1, E0, E0]),
                                         iota.unsqueeze(2).to_broadcast([1, E0, E0]), ALU.is_equal))
            pick = big[:, 0:E0 * E0].rearrange("p (s e) -> p s e", e=E0)

            def permute(out, values):
                then(nc.vector.tensor_tensor(pick, pm, values.to_broadcast([1, E0, E0]), ALU.mult))
                then(nc.vector.tensor_reduce(out, pick, AX.X, ALU.add))

            permute(jf[:, JT["sel"]:JT["sel"] + E0], iota.unsqueeze(1))
            permute(jf[:, JT["n"]:JT["n"] + E0], nj[:, 0:1, :])
            for q in range(NB):
                permute(jf[:, JT["blk"] + q:JT["blk"] + E0 * NB:NB], lst[:, :, q].unsqueeze(1))
            jn, jb = jf[:, JT["n"]:JT["n"] + E0], jf[:, JT["base"]:JT["base"] + E0]
            then(nc.vector.tensor_scalar(nj[:, 3, 0:E0 // 2], jf[:, JT["n"]:JT["n"] + E0:2], 0.0, None, ALU.is_gt))
            then(nc.vector.memset(jf[:, JT["pairs"]:JT["blk"]], 0.0))
            then(nc.vector.tensor_reduce(jf[:, JT["pairs"]:JT["pairs"] + 1], nj[:, 3, 0:E0 // 2], AX.X, ALU.add))
            then(nc.vector.tensor_scalar(jf[:, JT["pairs"]:JT["pairs"] + 1], jf[:, JT["pairs"]:JT["pairs"] + 1], 1.0, None,
                                         ALU.max))
            then(nc.vector.tensor_scalar(jn, jn, 1.0, None, ALU.max))
            then(nc.vector.tensor_tensor_scan(jb, jn, nj[:, 5, :], 0.0, ALU.add, ALU.add))
            then(nc.vector.tensor_tensor(jb, jb, jn, ALU.subtract))
            then(nc.vector.memset(jf[:, JT["free"]:JT["free"] + 2], 0.0))
            then(nc.vector.tensor_copy(jf[:, JT["free"] + 2:JT["free"] + E0 + 1], jf[:, JT["base"] + 1:JT["base"] + E0]))
            then(nc.vector.memset(jf[:, JT["sel"] + E0:JT["sel"] + E0 + 1], 0.0))
            nc.vector.tensor_copy(k.jobs[:, :], jf[:, :]).then_inc(k.r_jobs, 1)
            for i in range(NT):
                dve.wait_ge(k.r_bo, i + 1)
                nc.vector.tensor_tensor(k.X[:, i, 0:E], k.X[:, i, 0:E], ps[:, BO if i % 2 else LG, 0:E],
                                        ALU.add).then_inc(k.r_b2, 1)


def product3(nc, out, lhs, rhs, start, stop, **kw):
    for n, (a, b) in enumerate(((0, 0), (0, 1), (1, 0))):
        last = nc.tensor.matmul(out, lhs[a], rhs[b], start=(start and n == 0), stop=(stop and n == 2), **kw)
    return last


def experts_phase(nc, k):
    ps = k.ps
    with ExitStack() as ctx:
        def sb(name, shape, dt=F32):
            return ctx.enter_context(nc.sbuf_tensor(name, shape, dt))

        w1s = [sb(f"ew1s_{q}", [P, EB, FF]) for q in range(2)]
        w2s = [sb(f"ew2s_{q}", [P, FB, E]) for q in range(2)]
        b1s = [sb(f"eb1s_{q}", [P, FB]) for q in range(2)]
        w1 = [[sb(f"ew1_{q}{part}", [P, EB, FF], F32R) for part in "hl"] for q in range(2)]
        w2 = [[sb(f"ew2_{q}{part}", [P, FB, E], F32R) for part in "hl"] for q in range(2)]
        b1 = [sb(f"eb1_{q}", [P, FB]) for q in range(2)]
        assert FB * JOB == N
        hid = k.hT[:, 0, :].rearrange("p (f t) -> p f t", f=FB)
        hidp = [sb(f"ehid{part}", [P, FB, JOB], F32R) for part in "hl"]
        DOWN, TILES = 4, JOB // P
        PAIRS = FB // 2
        block = ctx.enter_context(nc.Block())

        def entry(eng, name, at, limit):
            return eng.value_load(k.jobs[0:1, bass.ds(at + JT[name], 1)], min_val=0, max_val=limit)

        def following(p, q):
            return (p * 2 + 1, 1, p + 1) if q == 0 else (p * 2 + 2, 0, p + 2)

        def jobs(eng, each, prepare):
            pairs = entry(eng, "pairs", 0, E0 // 2)
            if prepare:
                prepare(0, 0, 1)
            with eng.Fori(0, pairs) as p:
                for q in range(2):
                    n = entry(eng, "n", p * 2 + q, NB)
                    base = entry(eng, "base", p * 2 + q, E0 * NB)
                    sel = entry(eng, "sel", p * 2 + q, E0 - 1)
                    if prepare:
                        prepare(*following(p, q))
                    with eng.Fori(0, n) as j:
                        blk = entry(eng, "blk", p * (2 * NB) + q * NB + j, NB - 1)
                        each(base + j, q, blk, p, sel)

        def ahead(eng, prepare):
            pairs = entry(eng, "pairs", 0, E0 // 2)
            prepare(0, 0, 1)
            with eng.Fori(0, pairs) as p:
                for q in range(2):
                    prepare(*following(p, q))

        @block.sync
        def _(sp):
            def load(s, q, loads):
                e = entry(sp, "sel", s, E0 - 1)
                sp.wait_ge(k.e_split, s * 3 + 3)
                sp.dma_start(w1s[q][:, :, :], k.d["ew1"][bass.ds(e, 1)].squeeze(0)).then_inc(k.s_e[q], 16)
                sp.dma_start(w2s[q][:, :, :], k.d["ew2"][bass.ds(e, 1)].squeeze(0)).then_inc(k.s_e[q], 16)
                sp.dma_start(b1s[q][:, :], k.d["eb1"][bass.ds(e, 1)].squeeze(0)).then_inc(k.s_e[q], 16)

            ahead(sp, load)

        @block.gpsimd
        def _(pool):
            pool.sem_inc(k.e_split, 6)

            def low_parts(s, q, loads):
                pool.wait_ge(k.e_h1, s + 1)
                nc.gpsimd.tensor_tensor(w1[q][1][:, :, :], w1s[q][:, :, :], w1[q][0][:, :, :],
                                        ALU.subtract).then_inc(k.e_split, 1)
                pool.wait_ge(k.e_h2, s + 1)
                nc.gpsimd.tensor_tensor(w2[q][1][:, :, :], w2s[q][:, :, :], w2[q][0][:, :, :],
                                        ALU.subtract).then_inc(k.e_split, 1)
                nc.gpsimd.tensor_copy(b1[q][:, :], b1s[q][:, :]).then_inc(k.e_split, 1)

            ahead(pool, low_parts)

        @block.tensor
        def _(pe):
            pe.sem_inc(k.e_down, TILES)

            def job(n, q, blk, p, sel):
                pe.wait_ge(k.e_split, p * 6 + (3 * q + 9))
                tok = bass.ds(blk * JOB, JOB)
                for f in range(FB):
                    if f % 2 == 0:
                        pe.wait_ge(k.e_act, n * FB + (f + 2))
                    for j in range(EB):
                        last = product3(nc, ps[:, f // 2, (f % 2) * JOB:(f % 2 + 1) * JOB],
                                        [w[:, j, f * P:(f + 1) * P] for w in w1[q]],
                                        [k.hTh[:, j, tok], k.hTl[:, j, tok]], f % 2 == 0 and j == 0, j == EB - 1,
                                        skip_group_check=True)
                    if f % 2:
                        last.then_inc(k.e_up, 1)
                for t in range(TILES):
                    pe.wait_ge(k.e_y, n * TILES + (t + 1))
                    for f in range(FB):
                        if t == 0 and f % 2 == 0:
                            pe.wait_ge(k.e_lo, n * PAIRS + (PAIRS + f // 2 + 1))
                        last = product3(nc, ps[:, DOWN + t, 0:E], [h[:, f, t * P:(t + 1) * P] for h in hidp],
                                        [w[:, f, :] for w in w2[q]], f == 0, f == FB - 1)
                    last.then_inc(k.e_down, 1)

            jobs(pe, job, None)

        @block.scalar
        def _(act):
            act.sem_inc(k.e_act, FB)

            def high_parts(s, q, loads):
                free = entry(act, "free", s, E0 * NB)
                act.wait_ge(k.e_y, free * TILES + TILES)
                act.wait_ge(k.s_e[q], loads * 48)
                nc.scalar.copy(w1[q][0][:, :, :], w1s[q][:, :, :]).then_inc(k.e_h1, 1)

            def job(n, q, blk, p, sel):
                act.wait_ge(k.e_split, p * 6 + (3 * q + 9))
                for f in range(FB):
                    if f % 2 == 0:
                        act.wait_ge(k.e_up, n * PAIRS + (f // 2 + 1))
                        act.wait_ge(k.e_lo, n * PAIRS + (f // 2 + 1))
                    nc.scalar.activation(hid[:, f, :], ps[:, f // 2, (f % 2) * JOB:(f % 2 + 1) * JOB], ACT.Gelu,
                                         bias=b1[q][:, f:f + 1]).then_inc(k.e_act, 1)

            jobs(act, job, high_parts)

        @block.vector
        def _(dve):
            dve.sem_inc(k.e_y, TILES)
            dve.sem_inc(k.e_lo, PAIRS)
            X2 = k.X[:, :, :].rearrange("p i e -> p (i e)")
            wE2 = k.wE[:, :, :].rearrange("p e i -> p (e i)")
            hi, lo = hidp

            def high_parts(s, q, loads):
                free = entry(dve, "free", s, E0 * NB)
                dve.wait_ge(k.e_y, free * TILES + TILES)
                dve.wait_ge(k.s_e[q], loads * 48)
                nc.vector.tensor_copy(w2[q][0][:, :, :], w2s[q][:, :, :]).then_inc(k.e_h2, 1)

            def job(n, q, blk, p, e):
                dve.wait_ge(k.e_down, n * TILES + TILES)
                for g in range(PAIRS):
                    f = slice(2 * g, 2 * g + 2)
                    dve.wait_ge(k.e_act, n * FB + (FB + 2 * g + 2))
                    nc.vector.tensor_copy(hi[:, f, :], hid[:, f, :]).then_inc(k.e_dhi, 1)
                    dve.wait_ge(k.e_dhi, n * PAIRS + (g + 1))
                    nc.vector.tensor_tensor(lo[:, f, :], hid[:, f, :], hi[:, f, :], ALU.subtract).then_inc(k.e_lo, 1)
                for t in range(TILES):
                    dve.wait_ge(k.e_down, n * TILES + (TILES + t + 1))
                    dve.wait_ge(k.e_y, n * TILES + (TILES + t))
                    x = X2[:, bass.ds(blk * (TILES * (E + 1)) + t * (E + 1), E)]
                    nc.vector.scalar_tensor_tensor(x, ps[:, DOWN + t, 0:E], wE2[:, bass.ds(e * NT + blk * TILES + t, 1)],
                                                   x, ALU.mult, ALU.add).then_inc(k.e_y, 1)

            jobs(dve, job, high_parts)


def laplace_phase(nc, k):
    ps = k.ps
    with ExitStack() as ctx:
        def sb(name, shape, dt=F32):
            return ctx.enter_context(nc.sbuf_tensor(name, shape, dt))

        nb = sb("nb", [P, EB, N])
        du = k.att[:, :, :].rearrange("p i e -> p (i e)").rearrange("p (f n) -> p f n", f=EB)
        z = sb("zc", [P, 2, B])
        block = ctx.enter_context(nc.Block())
        LAP, Q, K, V = 0, 8, 16, 24

        @block.sync
        def _(sp):
            for dst, src in ((k.wq, k.d["wq"]), (k.wk, k.d["wk"]), (k.wv, k.d["wv"]), (k.wo, k.d["wo"])):
                sp.dma_start(dst[:, :, :], src).then_inc(k.s_wC, 16)

        @block.tensor
        def _(pe):
            for w in range(NW):
                for f in range(EB):
                    for j in range(EB):
                        last = nc.tensor.matmul(ps[:, EB * w + f, :],
                                                k.const("lap", j * E + f * P, P), k.hT[:, j, w * W:(w + 1) * W],
                                                start=(j == 0), stop=(j == EB - 1))
                    last.then_inc(k.l_mm, 1)
            pe.wait_ge(k.s_wC, 64)
            for w in range(NW):
                for g, wt in ((Q, k.wq), (K, k.wk)):
                    for f in range(EB):
                        n = g + EB * w + f
                        if g == Q:
                            pe.wait_ge(k.l_du, EB * w + EB)
                        else:
                            pe.wait_ge(k.l_q, EB * w + f + 1)
                        for j in range(EB):
                            last = nc.tensor.matmul(ps[:, n % 8, :], wt[:, j, f * P:(f + 1) * P],
                                                    du[:, j, w * W:(w + 1) * W], start=(j == 0), stop=(j == EB - 1))
                        last.then_inc(k.l_qk, 1)
            for i in range(NT):
                pe.wait_ge(k.l_k, 8) if i == 0 else None
                if i >= 8:
                    pe.wait_ge(k.l_v, i - 7)
                for j in range(EB):
                    last = nc.tensor.matmul(ps[:, i % 8, 0:E], du[:, j, i * P:(i + 1) * P], k.wv[:, j, :],
                                            start=(j == 0), stop=(j == EB - 1))
                last.then_inc(k.l_vm, 1)

        @block.scalar
        def _(act):
            for w in range(NW):
                for f in range(EB):
                    act.wait_ge(k.l_qk, 4 * w + f + 1)
                    if f == 0:
                        act.wait_ge(k.l_zero, w + 1)
                    for s in range(4):
                        r = slice(32 * s, 32 * s + 32)
                        last = nc.scalar.activation(k.qT[r, 4 * f + s, w * W:(w + 1) * W],
                                                    ps[r, (Q + EB * w + f) % 8, :], ACT.Copy, scale=32.0 ** -0.5)
                    last.then_inc(k.l_q, 1)
                for f in range(EB):
                    act.wait_ge(k.l_qk, 4 * w + EB + f + 1)
                    nc.scalar.copy(k.kT[:, f, w * W:(w + 1) * W], ps[:, (K + EB * w + f) % 8, :]).then_inc(k.l_k, 1)

        @block.gpsimd
        def _(pool):
            for b in range(B):
                y = k.hT[:, :, b * T:(b + 1) * T]
                s = nb[:, :, b * T:(b + 1) * T]
                nc.gpsimd.tensor_tensor(s[:, :, 1:T - 1], y[:, :, 0:T - 2], y[:, :, 2:T], ALU.add).then_inc(k.l_nb, 1)
                for at, of in ((0, 1), (T - 1, T - 2)):
                    nc.gpsimd.tensor_tensor(s[:, :, at:at + 1], y[:, :, of:of + 1], y[:, :, of:of + 1],
                                            ALU.add).then_inc(k.l_nb, 1)
                for w in (2 * b, 2 * b + 1):
                    nc.gpsimd.memset(k.qT[:, :, w * W:(w + 1) * W], 0.0).then_inc(k.l_zero, 1)

        @block.vector
        def _(dve):
            then = chain(k, dve, "dve")
            then(nc.vector.tensor_scalar(z[:, 0, :], k.row("zr", 0, B), -1.0, None, ALU.mult))
            then(nc.vector.scalar_tensor_tensor(z[:, 1, :], k.row("zy", 0, B), -2.0, k.row("zr", 0, B), ALU.mult,
                                                ALU.add))
            for w in range(NW):
                b, tok = w // 2, slice(w * W, (w + 1) * W)
                for f in range(EB):
                    y, o = k.hT[:, f, tok], du[:, f, tok]
                    then(nc.vector.tensor_scalar(o, y, z[:, 0, b:b + 1], z[:, 1, b:b + 1], ALU.mult, ALU.add))
                    then(nc.vector.tensor_tensor(o, o, y, ALU.mult))
                    dve.wait_ge(k.l_nb, 3 * (b + 1))
                    then(nc.vector.scalar_tensor_tensor(o, nb[:, f, tok], k.row("zy", b), o, ALU.mult, ALU.add))
                    dve.wait_ge(k.l_mm, EB * w + f + 1)
                    nc.vector.scalar_tensor_tensor(o, ps[:, EB * w + f, :], k.row("zx", b), o, ALU.mult,
                                                   ALU.add).then_inc(k.l_du, 1)
            for i in range(NT):
                dve.wait_ge(k.l_vm, i + 1)
                nc.vector.tensor_copy(k.v[:, i, :], ps[:, i % 8, 0:E]).then_inc(k.l_v, 1)


HEADS = 4
UNITS = NT * HEADS


def attention_phase(nc, k):
    ps = k.ps
    TR, PV = 4, 6
    with ExitStack() as ctx:
        def sb(name, shape, dt=F32):
            return ctx.enter_context(nc.sbuf_tensor(name, shape, dt))

        pr = sb("pr", [P, 3, 2, T])
        dT = k.hT[:, :, 0:T].rearrange("p q (j t) -> p q j t", t=P)
        nmax = sb("nmax", [P, 2, 2])
        sums = sb("sums", [P, 2, NT * HEADS])
        rr = sb("rr", [P, 2])
        rc = sb("rc", [P, HEADS])
        sq = sb("sqa", [P, E])
        identb = sb("identb", [P, P], BF16)
        maskb = sb("maskb", [P, P], BF16)
        lam = sb("lamt", [P, 68])
        block = ctx.enter_context(nc.Block())

        def unit(n):
            i, h = n // HEADS, n % HEADS
            return i, i % TB, h

        def groups(n):
            c = unit(n)[1]
            return [range(g, min(g + 4, c + 1)) for g in range(0, c + 1, 4)]

        at, first = 0, []
        for n in range(UNITS):
            first.append(at)
            at += len(groups(n))
        first.append(at)

        def half(n, u, wide):
            if unit(n)[1] < 4:
                return ps[:, 2 * u + n % 2, 0:wide]
            return ps[:, 2 * u:2 * u + 2, :].rearrange("p b t -> p (b t)")[:, 0:wide]

        @block.tensor
        def _(pe):
            def scores(n, u):
                i, c, h = unit(n)
                keys = (i - c) * P
                before = n - 1 if c >= 4 or (n and unit(n - 1)[1] >= 4) else n - 2
                if before >= 0:
                    pe.wait_ge(k.a_exp, 2 * before + u + 1)
                s = 2 * h + u
                q = k.qT[:, s, i * P:(i + 1) * P]
                out = half(n, u, (c + 1) * P)
                for at in range(0, c * P, W):
                    to = min(at + W, c * P)
                    nc.tensor.matmul(out[:, at:to], q, k.kT[:, s // 4, keys + at:keys + to], start=True, stop=True)
                own = out[:, c * P:(c + 1) * P]
                nc.tensor.matmul(own, q, k.kT[:, s // 4, i * P:(i + 1) * P], start=True, stop=False)
                nc.tensor.matmul(own, identb[:, :], maskb[:, :], start=False, stop=True).then_inc(k.a_qk, 1)

            def turn(n):
                pe.wait_ge(k.a_d, n + 1)
                for g, blks in enumerate(groups(n)):
                    if first[n] + g >= 2:
                        pe.wait_ge(k.a_ev, first[n] + g - 1)
                    for j in blks:
                        last = nc.tensor.transpose(ps[:, TR + (first[n] + g) % 2, (j % 4) * P:(j % 4 + 1) * P],
                                                   pr[:, n % 3, 0, j * P:(j + 1) * P], k.const("ident"))
                    last.then_inc(k.a_tr, 1)

            def product(n):
                i, c, h = unit(n)
                if h == 0 and i >= 2:
                    pe.wait_ge(k.a_att, i - 1)
                for g, blks in enumerate(groups(n)):
                    pe.wait_ge(k.a_ev, first[n] + g + 1)
                    for j in blks:
                        last = nc.tensor.matmul(ps[:, PV + i % 2, h * 64:(h + 1) * 64], dT[:, n % 2, j, :],
                                                k.v[:, i - c + j, h * 64:(h + 1) * 64], start=(h == 0 and j == 0),
                                                stop=(j == c), skip_group_check=True)
                last.then_inc(k.a_pv, 1)

            pe.wait_ge(k.a_mask, 2)
            for n in range(UNITS + 2):
                if n < UNITS:
                    scores(n, 0)
                if n >= 2:
                    turn(n - 2)
                if n < UNITS:
                    scores(n, 1)
                if n >= 2:
                    product(n - 2)

        @block.scalar
        def _(act):
            act.wait_ge(k.a_lam, 1)
            nc.scalar.activation(lam[:, 64:66], lam[:, 64:66], ACT.Exp).then_inc(k.a_lexp, 1)

            def turn(n):
                for g, blks in enumerate(groups(n)):
                    act.wait_ge(k.a_tr, first[n] + g + 1)
                    if n >= 2 and g == 0:
                        act.wait_ge(k.a_pv, n - 1)
                    nc.scalar.copy(dT[:, n % 2, blks[0]:blks[-1] + 1, :],
                                   ps[:, TR + (first[n] + g) % 2, 0:len(blks) * P].rearrange("p (j t) -> p j t", t=P)
                                   ).then_inc(k.a_ev, 1)

            def exponentials(n, u):
                wide = (unit(n)[1] + 1) * P
                act.wait_ge(k.a_max, 2 * n + u + 1)
                if n >= 3 and u == 0:
                    act.wait_ge(k.a_tr, first[n - 2])
                nc.scalar.activation(pr[:, n % 3, u, 0:wide], half(n, u, wide), ACT.Exp, bias=nmax[:, n % 2, u:u + 1],
                                     accum_out=sums[:, u, n:n + 1]).then_inc(k.a_exp, 1)

            for n in range(UNITS + 2):
                if n < UNITS:
                    exponentials(n, 0)
                if n >= 2:
                    turn(n - 2)
                if n < UNITS:
                    exponentials(n, 1)

        @block.vector
        def _(dve):
            then = chain(k, dve, "dve")
            nc.vector.tensor_copy(identb[:, :], k.const("ident")).then_inc(k.a_mask, 1)
            nc.vector.tensor_copy(maskb[:, :], k.const("causal")).then_inc(k.a_mask, 1)
            l = k.row("lam", 0, 128).rearrange("p (a q d) -> p a q d", a=2, q=2)
            then(nc.vector.tensor_tensor(lam[:, 0:64].rearrange("p (a d) -> p a d", a=2), l[:, :, 0, :], l[:, :, 1, :],
                                         ALU.mult))
            nc.vector.tensor_reduce(lam[:, 64:66], lam[:, 0:64].rearrange("p (a d) -> p a d", a=2), AX.X,
                                    ALU.add).then_inc(k.a_lam, 1)
            dve.wait_ge(k.a_lexp, 1)
            then(nc.vector.tensor_tensor(lam[:, 66:67], lam[:, 65:66], lam[:, 64:65], ALU.subtract))
            then(nc.vector.tensor_scalar(lam[:, 67:68], lam[:, 66:67], -LAMBDA_INIT, None, ALU.add))

            def largest(n, u):
                wide = (unit(n)[1] + 1) * P
                dve.wait_ge(k.a_qk, 2 * n + u + 1)
                if n >= 2:
                    dve.wait_ge(k.a_exp, 2 * n - 3 + u)
                nc.vector.tensor_reduce(nmax[:, n % 2, u:u + 1], half(n, u, wide), AX.X, ALU.max,
                                        negate=True).then_inc(k.a_max, 1)

            def difference(n):
                wide = (unit(n)[1] + 1) * P
                dve.wait_ge(k.a_exp, 2 * n + 2)
                then(nc.vector.reciprocal(rr[:, 0:1], sums[:, 1, n:n + 1]))
                then(nc.vector.scalar_tensor_tensor(rr[:, 1:2], sums[:, 0, n:n + 1], rr[:, 0:1], lam[:, 67:68],
                                                    ALU.mult, ALU.mult))
                nc.vector.scalar_tensor_tensor(pr[:, n % 3, 0, 0:wide], pr[:, n % 3, 1, 0:wide], rr[:, 1:2],
                                               pr[:, n % 3, 0, 0:wide], ALU.mult, ALU.add).then_inc(k.a_d, 1)

            def collect(i):
                dve.wait_ge(k.a_pv, HEADS * (i + 1))
                then(nc.vector.reciprocal(rc[:, :], sums[:, 0, HEADS * i:HEADS * (i + 1)]))
                heads = k.att[:, i, :].rearrange("p (h d) -> p h d", h=HEADS)
                nc.vector.tensor_tensor(heads, ps[:, PV + i % 2, 0:E].rearrange("p (h d) -> p h d", h=HEADS),
                                        rc[:, :].unsqueeze(2).to_broadcast([P, HEADS, 64]),
                                        ALU.mult).then_inc(k.a_att, 1)
                dve.wait_ge(k.a_att, i + 1)
                then(nc.vector.tensor_tensor(sq[:, :], k.att[:, i, :], k.att[:, i, :], ALU.mult))
                then(nc.vector.tensor_reduce(k.ms[:, i, :], sq[:, :].rearrange("p (h d) -> p h d", h=HEADS), AX.X,
                                             ALU.add))

            for n in range(UNITS):
                largest(n, 0)
                if n:
                    difference(n - 1)
                largest(n, 1)
                if n % HEADS == 2 and n > 2:
                    collect(n // HEADS - 1)
            difference(UNITS - 1)
            collect(NT - 1)
            dve.wait_ge(k.a_d, UNITS)


def attention_norm_phase(nc, k):
    with nc.Block() as block:
        @block.scalar
        def _(act):
            nc.scalar.activation(k.ms[:, :, :], k.ms[:, :, :], ACT.Sqrt, bias=k.eps[:, 0:1],
                                 scale=1.0 / 64).then_inc(k.n_sd, 1)

        @block.vector
        def _(dve):
            then = chain(k, dve, "dve")
            dve.wait_ge(k.n_sd, 1)
            then(nc.vector.reciprocal(k.ms[:, :, :], k.ms[:, :, :]))
            then(nc.vector.tensor_scalar(k.ms[:, :, :], k.ms[:, :, :], 1.0 - LAMBDA_INIT, None, ALU.mult))
            heads = k.att[:, :, :].rearrange("p i (h d) -> p (i h) d", h=HEADS)
            scale = k.ms[:, :, :].rearrange("p i h -> p (i h)").unsqueeze(2).to_broadcast([P, NT * HEADS, 64])
            half = NT * HEADS // 2
            nc.vector.tensor_tensor(heads[:, 0:half], heads[:, 0:half], scale[:, 0:half], ALU.mult).then_inc(k.n_1, 1)

        @block.gpsimd
        def _(pool):
            pool.wait_ge(k.n_1, 1)
            heads = k.att[:, :, :].rearrange("p i (h d) -> p (i h) d", h=HEADS)
            scale = k.ms[:, :, :].rearrange("p i h -> p (i h)").unsqueeze(2).to_broadcast([P, NT * HEADS, 64])
            half = NT * HEADS // 2
            nc.gpsimd.tensor_tensor(heads[:, half:], heads[:, half:], scale[:, half:], ALU.mult)


def attention_out_phase(nc, k):
    with nc.Block() as block:
        @block.tensor
        def _(pe):
            for i in range(NT):
                if i >= 8:
                    pe.wait_ge(k.n_x, i - 7)
                for j in range(EB):
                    last = nc.tensor.matmul(k.ps[:, i % 8, 0:E], k.hT[:, j, i * P:(i + 1) * P], k.wo[:, j, :],
                                            start=(j == 0), stop=(j == EB - 1))
                last.then_inc(k.n_mm, 1)

        @block.vector
        def _(dve):
            for i in range(NT):
                dve.wait_ge(k.n_mm, i + 1)
                nc.vector.tensor_tensor(k.X[:, i, 0:E], k.X[:, i, 0:E], k.ps[:, i % 8, 0:E],
                                        ALU.add).then_inc(k.n_x, 1)


SLOTS = E1 * CAP
ST = SLOTS // P
OUTSIDE = 1.0e5


def subject_phase(nc, k):
    ps = k.ps
    with ExitStack() as ctx:
        def sb(name, shape, dt=F32):
            return ctx.enter_context(nc.sbuf_tensor(name, shape, dt))

        it = sb("it1", [1, B], I32)
        ws = sb("ws", [P, B, EB, E])
        bs = sb("bs", [P, B, EB])
        wgt = sb("wgt", [P, EB, E1])
        zero = sb("zero", [P, E])
        cT = sb("cT", [P, EB, N])
        lg = sb("lg1", [P, NT, E1])
        v8 = sb("v81", [P, NT, 8])
        i8 = sb("i81", [P, NT, 8], U32)
        ix = sb("ix", [P, NT])
        oh = sb("oh1", [P, NT, E1])
        base = sb("base1", [P, NT, E1])
        tot = sb("tot1", [P, NT, E1])
        keep = sb("keep", [P, NT])
        slot = sb("slot", [P, NT])
        tmp = sb("tmp1", [P, NT])
        LG, CUM = 0, 1
        block = ctx.enter_context(nc.Block())

        @block.sync
        def _(sp):
            sp.dma_start(it[:, :], k.d["itok1"].unsqueeze(0)).then_inc(k.s_it1, 16)
            sp.dma_start(wgt[:, :, :], k.d["wgt"]).then_inc(k.s_wgt, 16)
            sp.wait_ge(k.s_it1, 16)
            for b in range(B):
                s = sp.value_load(it[0:1, b:b + 1], min_val=0, max_val=NSUB - 1)
                sp.dma_start(ws[:, b, :, :], k.d["subw"][bass.ds(s, 1)].squeeze(0)).then_inc(k.s_ws[b], 16)
                sp.dma_start(bs[:, b, :], k.d["subb"][bass.ds(s, 1)].squeeze(0)).then_inc(k.s_ws[b], 16)
            sp.wait_ge(k.u_zero, 1)
            sp.dma_start(k.xs.rearrange("(p q) e -> p q e", p=P),
                         zero[:, :].unsqueeze(1).to_broadcast([P, ST, E])).then_inc(k.s_xz, 16)
            sp.wait_ge(k.s_xz, 16)

        @block.tensor
        def _(pe):
            for b in range(B):
                pe.wait_ge(k.s_ws[b], 32)
                for w in (2 * b, 2 * b + 1):
                    for f in range(EB):
                        for j in range(EB):
                            last = nc.tensor.matmul(ps[:, EB * w + f, :], ws[:, b, j, f * P:(f + 1) * P],
                                                    k.hT[:, j, w * W:(w + 1) * W], start=(j == 0), stop=(j == EB - 1))
                        last.then_inc(k.u_mm, 1)
            pe.wait_ge(k.u_c, 8)
            pe.wait_ge(k.s_wgt, 16)
            for i in range(NT):
                for j in range(EB):
                    last = nc.tensor.matmul(ps[:, LG, i * E1:(i + 1) * E1], cT[:, j, i * P:(i + 1) * P],
                                            wgt[:, j, :], start=(i == 0 and j == 0), stop=(j == EB - 1),
                                            skip_group_check=True)
            last.then_inc(k.u_lg, 1)
            for g in range(NT // 2):
                if g >= 6:
                    pe.wait_ge(k.u_row, g - 5)
                for t in range(2):
                    for f in range(EB):
                        last = nc.tensor.transpose(ps[:, 2 + g % 6, t * E + f * P:t * E + (f + 1) * P],
                                                   cT[:, f, (2 * g + t) * P:(2 * g + t + 1) * P], k.const("ident"))
                last.then_inc(k.u_tr, 1)
            pe.wait_ge(k.u_oh, 1)
            o = oh[:, :, :].rearrange("p i e -> p (i e)")
            nc.tensor.matmul(ps[:, CUM, 0:P], k.const("lt"), o, start=True, stop=True)
            nc.tensor.matmul(ps[:, CUM, P:2 * P], k.const("ones"), o, start=True, stop=True).then_inc(k.u_cum, 1)

        @block.scalar
        def _(act):
            for w in range(NW):
                for f in range(EB):
                    act.wait_ge(k.u_mm, EB * w + f + 1)
                    nc.scalar.activation(cT[:, f, w * W:(w + 1) * W], ps[:, EB * w + f, :], ACT.Identity,
                                         bias=bs[:, w // 2, f:f + 1]).then_inc(k.u_c, 1)
            act.wait_ge(k.u_sub, 1)
            nc.scalar.activation(lg[:, :, :], lg[:, :, :], ACT.Exp).then_inc(k.u_exp, 1)
            for g in range(NT // 2):
                act.wait_ge(k.u_tr, g + 1)
                nc.scalar.copy(k.rows2[:, 2 * g:2 * g + 2, :], ps[:, 2 + g % 6, :].rearrange("p (t e) -> p t e", t=2)
                               ).then_inc(k.u_row, 1)

        @block.vector
        def _(dve):
            then = chain(k, dve, "dve")
            nc.vector.memset(zero[:, :], 0.0).then_inc(k.u_zero, 1)
            wide = [P, NT, E1]
            dve.wait_ge(k.u_lg, 1)
            then(nc.vector.tensor_copy(lg[:, :, :], ps[:, LG, 0:P].rearrange("p (i e) -> p i e", e=E1)))
            for i in range(NT):
                last = nc.vector.max(v8[:, i, :], lg[:, i, :])
            then(last)
            for i in range(NT):
                last = nc.vector.max_index(i8[:, i, :], v8[:, i, :], lg[:, i, :])
            then(last)
            nc.vector.tensor_tensor(lg[:, :, :], lg[:, :, :], v8[:, :, 0:1].to_broadcast(wide),
                                    ALU.subtract).then_inc(k.u_sub, 1)
            then(nc.vector.tensor_copy(ix[:, :], i8[:, :, 0]))
            nc.vector.tensor_tensor(oh[:, :, :], k.const("iota", 0, E1).unsqueeze(1).to_broadcast(wide),
                                    ix[:, :].unsqueeze(2).to_broadcast(wide), ALU.is_equal).then_inc(k.u_oh, 1)
            dve.wait_ge(k.u_cum, 1)
            then(nc.vector.tensor_copy(tot[:, :, :], ps[:, CUM, P:2 * P].rearrange("p (i e) -> p i e", e=E1)))
            then(nc.vector.memset(base[:, 0, :], 0.0))
            for i in range(1, NT):
                then(nc.vector.tensor_tensor(base[:, i, :], base[:, i - 1, :], tot[:, i - 1, :], ALU.add))
            then(nc.vector.tensor_tensor(base[:, :, :], base[:, :, :],
                                         ps[:, CUM, 0:P].rearrange("p (i e) -> p i e", e=E1), ALU.add))
            then(nc.vector.tensor_tensor(base[:, :, :], base[:, :, :], oh[:, :, :], ALU.mult))
            then(nc.vector.tensor_reduce(slot[:, :], base[:, :, :], AX.X, ALU.add))
            then(nc.vector.tensor_scalar(keep[:, :], slot[:, :], float(CAP), None, ALU.is_lt))
            then(nc.vector.scalar_tensor_tensor(slot[:, :], ix[:, :], float(CAP), slot[:, :], ALU.mult, ALU.add))
            then(nc.vector.tensor_tensor(tmp[:, :], slot[:, :], keep[:, :], ALU.mult))
            nc.vector.tensor_copy(k.take[:, :], tmp[:, :])
            then(nc.vector.tensor_scalar(base[:, :, 0], keep[:, :], -OUTSIDE, OUTSIDE, ALU.mult, ALU.add))
            then(nc.vector.tensor_tensor(slot[:, :], slot[:, :], base[:, :, 0], ALU.add))
            nc.vector.tensor_copy(k.put[:, :], slot[:, :])
            dve.wait_ge(k.u_exp, 1)
            then(nc.vector.tensor_reduce(tmp[:, :], lg[:, :, :], AX.X, ALU.add))
            then(nc.vector.reciprocal(tmp[:, :], tmp[:, :]))
            nc.vector.tensor_tensor(k.gate[:, :], tmp[:, :], keep[:, :], ALU.mult)


def dispatch_phase(nc, k):
    ps = k.ps
    with ExitStack() as ctx:
        xr = ctx.enter_context(nc.sbuf_tensor("xr", [P, ST, E], F32))
        block = ctx.enter_context(nc.Block())

        @block.gpsimd
        def _(pool):
            for i in range(NT):
                nc.gpsimd.indirect_dma_start(out=k.xs, out_offset=bass.IndirectOffsetOnAxis(ap=k.put[:, i:i + 1], axis=0),
                                             in_=k.rows2[:, i, :], in_offset=None, bounds_check=SLOTS - 1,
                                             oob_is_err=False).then_inc(k.s_put, 16)

        @block.sync
        def _(sp):
            for e in range(2):
                load_expert(sp, k, e)
            sp.dma_start(k.b2b[:, :, :], k.d["b2b"].partition_broadcast(P)).then_inc(k.s_b2b, 16)
            sp.wait_ge(k.s_put, 16 * NT)
            for q in range(5):
                n = ST // 5
                sp.dma_start(xr[:, q * n:(q + 1) * n, :], k.xs.rearrange("(g p) e -> p g e", p=P)[:, q * n:(q + 1) * n, :]
                             ).then_inc(k.s_xr[q], 16)

        @block.tensor
        def _(pe):
            for g in range(ST // 2):
                if g % 2 == 0:
                    pe.wait_ge(k.s_xr[g // 2], 16)
                if g >= 8:
                    pe.wait_ge(k.v_ev[g % 2], (g - 8) // 2 + 1)
                for f in range(EB):
                    for t in range(2):
                        last = nc.tensor.transpose(ps[:, g % 8, f * 2 * P + t * P:f * 2 * P + (t + 1) * P],
                                                   xr[:, 2 * g + t, f * P:(f + 1) * P], k.const("ident"))
                last.then_inc(k.v_tr, 1)

        def evacuate(eng, which):
            for g in range(which, ST // 2, 2):
                eng.wait_ge(k.v_tr, g + 1)
                copy = nc.vector.tensor_copy if which else nc.scalar.copy
                copy(k.xsT[:, :, g * 2 * P:(g + 1) * 2 * P],
                     ps[:, g % 8, :].rearrange("p (f t) -> p f t", f=EB)).then_inc(k.v_ev[which], 1)

        @block.scalar
        def _(act):
            evacuate(act, 0)

        @block.vector
        def _(dve):
            evacuate(dve, 1)


def load_expert(sp, k, e):
    sp.dma_start(k.fw1[e % 2][:, :, :], k.d["fw1"][e]).then_inc(k.s_f[e % 2], 16)
    sp.dma_start(k.fw2[e % 2][:, :, :], k.d["fw2"][e]).then_inc(k.s_f[e % 2], 16)


def capacity_phase(nc, k):
    ps = k.ps
    chunks = [(0, P), (P, P), (2 * P, CAP - 2 * P)]
    NC = len(chunks)
    with ExitStack() as ctx:
        hid = ctx.enter_context(nc.sbuf_tensor("fhid", [P, 2, FB, CAP], F32))
        yr = ctx.enter_context(nc.sbuf_tensor("yr", [P, 2, NC, E], F32))
        block = ctx.enter_context(nc.Block())
        DOWN = 4

        @block.sync
        def _(sp):
            for e in range(E1):
                for c, (at, m) in enumerate(chunks):
                    sp.wait_ge(k.f_y, e * NC + c + 1)
                    sp.dma_start(k.ys[e * CAP + at:e * CAP + at + m, :], yr[0:m, e % 2, c, :]
                                 ).then_inc(k.s_ys[e % 2], 16)
                if e + 2 < E1:
                    load_expert(sp, k, e + 2)
            for q in range(2):
                sp.wait_ge(k.s_ys[q], 16 * NC * E1 // 2)

        @block.tensor
        def _(pe):
            def up(e):
                pe.wait_ge(k.s_f[e % 2], 32 * (e // 2 + 1))
                for f in range(FB):
                    g = e * FB + f
                    if g >= 4:
                        pe.wait_ge(k.f_act, g - 3)
                    for j in range(EB):
                        last = nc.tensor.matmul(ps[:, g % 4, 0:CAP], k.fw1[e % 2][:, j, f * P:(f + 1) * P],
                                                k.xsT[:, j, e * CAP:(e + 1) * CAP], start=(j == 0), stop=(j == EB - 1))
                    last.then_inc(k.f_up, 1)

            def down(e):
                for c, (at, m) in enumerate(chunks):
                    if e:
                        pe.wait_ge(k.f_y, (e - 1) * NC + c + 1)
                    for f in range(FB):
                        if c == 0:
                            pe.wait_ge(k.f_act, e * FB + f + 1)
                        last = nc.tensor.matmul(ps[0:m, DOWN + c, 0:E], hid[:, e % 2, f, at:at + m],
                                                k.fw2[e % 2][:, f, :], start=(f == 0), stop=(f == FB - 1))
                    last.then_inc(k.f_down, 1)

            up(0)
            for e in range(E1):
                if e + 1 < E1:
                    up(e + 1)
                down(e)

        @block.scalar
        def _(act):
            for e in range(E1):
                for f in range(FB):
                    act.wait_ge(k.f_up, e * FB + f + 1)
                    if e >= 2 and f == 0:
                        act.wait_ge(k.f_down, NC * (e - 1))
                    nc.scalar.activation(hid[:, e % 2, f, :], ps[:, (e * FB + f) % 4, 0:CAP], ACT.Relu,
                                         bias=k.col("b1b", e * FB + f)).then_inc(k.f_act, 1)

        @block.vector
        def _(dve):
            for e in range(E1):
                for c, (at, m) in enumerate(chunks):
                    dve.wait_ge(k.f_down, e * NC + c + 1)
                    if e >= 2 and c == 0:
                        dve.wait_ge(k.s_ys[e % 2], 16 * NC * (e // 2))
                    nc.vector.tensor_tensor(yr[0:m, e % 2, c, :], ps[0:m, DOWN + c, 0:E], k.b2b[0:m, e, :],
                                            ALU.add).then_inc(k.f_y, 1)


def combine_phase(nc, k):
    with ExitStack() as ctx:
        g = ctx.enter_context(nc.sbuf_tensor("g", [P, NT, E], F32))
        block = ctx.enter_context(nc.Block())

        @block.gpsimd
        def _(pool):
            for i in range(NT):
                nc.gpsimd.indirect_dma_start(out=g[:, i, :], out_offset=None, in_=k.ys,
                                             in_offset=bass.IndirectOffsetOnAxis(ap=k.take[:, i:i + 1], axis=0)
                                             ).then_inc(k.s_take[i % 4], 16)
                if i % 4 == 3 and i < NT - 1:
                    for q in range(4):
                        pool.wait_ge(k.s_take[q], 16 * (i // 4 + 1))

        @block.vector
        def _(dve):
            for i in range(NT):
                dve.wait_ge(k.s_take[i % 4], 16 * (i // 4 + 1))
                nc.vector.scalar_tensor_tensor(g[:, i, :], g[:, i, :], k.gate[:, i:i + 1], k.X[:, i, 0:E], ALU.mult,
                                               ALU.add).then_inc(k.g_x, 1)

        @block.sync
        def _(sp):
            out = k.d["out"].rearrange("(i p) e -> p i e", p=P)
            for q in range(4):
                sp.wait_ge(k.g_x, 4 * (q + 1))
                sp.dma_start(out[:, 4 * q:4 * q + 4, :], g[:, 4 * q:4 * q + 4, :]).then_inc(k.s_out, 16)
            sp.wait_ge(k.s_out, 64)


def taken(nc):
    def take(names):
        handles = [nc.alloc_semaphore(name) for name in names.split()]
        take.handles += handles
        return handles
    take.handles = []
    return take


def network(nc, d):
    class Shared:
        pass

    k = Shared()
    k.d = d
    with ExitStack() as ctx:
        def sb(name, shape, dt=F32):
            return ctx.enter_context(nc.sbuf_tensor(name, shape, dt))

        k.cols = sb("cols", [P, NCOL])
        k.rows = sb("rows", [P, NROW])
        k.consts = sb("consts", [P, NCONST])
        k.win = sb("win", [P, EB, 1160])
        k.wop = sb("wop", [P, 4, E])
        k.c2w = sb("c2w", [P, EB, HID])
        k.keysT, k.rwT = (sb(n, [P, EB, E0]) for n in ("keysT", "rwT"))
        k.b2a = sb("b2a", [E0, E])
        k.eps = sb("eps", [P, 1])
        k.X = sb("X", [P, NT, E + 1])
        k.ps = ctx.enter_context(nc.psum_tensor("ps", [P, 8, W], F32))

        def piece(tensor, table, name, at, n):
            return tensor[:, table[name][0] + at:table[name][0] + at + n]

        k.col = lambda name, at, n=1: piece(k.cols, COL_AT, name, at, n)
        k.row = lambda name, at, n=1: piece(k.rows, ROW_AT, name, at, n)
        k.const = lambda name, at=0, n=P: piece(k.consts, CONST_AT, name, at, n)

        k.s_out, k.s_it1, k.s_wC = taken(nc)("s_out s_it1 s_wC")
        k.chains = {n: (ctx.enter_context(nc.semaphore(f"own_{n}")), [0]) for n in ("dve", "act", "pool")}
        first = taken(nc)
        k.s_small, k.s_rows, k.s_wA, k.s_wB, k.s_x, k.s_xT_0, k.s_xT_1 = first("s_small s_rows s_wA s_wB s_x s_xT_0 s_xT_1")
        k.s_xT_2, k.s_xT_3, k.c_mm, k.c_evac, k.c_ctx, k.c_w2b, k.c_blend = first("s_xT_2 s_xT_3 c_mm c_evac c_ctx c_w2b c_blend")
        k.c_sg, k.c_out, k.c_tau, k.c_bdiff, k.c_bexp, k.c_var, k.c_sd = first("c_sg c_out c_tau c_bdiff c_bexp c_var c_sd")
        k.c_dve, k.c_init, k.c_norm, k.c_aff, k.c_hn = first("c_dve c_init c_norm c_aff c_hn")
        k.i_dt, k.i_evac, k.i_mm, k.i_dtA, k.i_sp, k.i_cs, k.i_expA = first("i_dt i_evac i_mm i_dtA i_sp i_cs i_expA")
        k.i_abs, k.i_ln, k.i_conv, k.i_pad, k.i_silu, k.s_ct, k.s_mw = first("i_abs i_ln i_conv i_pad i_silu s_ct s_mw")
        k.m_xst, k.m_xt, k.m_bcu, k.m_bc, k.m_G, k.m_E, k.m_seg = first("m_xst m_xt m_bcu m_bc m_G m_E m_seg")
        k.m_sz, k.m_z, k.m_M, k.m_xdt, k.m_y2, k.m_yd, k.m_h = first("m_sz m_z m_M m_xdt m_y2 m_yd m_h")
        k.m_y1, k.m_yo, k.m_xdd, k.m_S, k.m_yg, k.m_ss, k.m_xD = first("m_y1 m_yo m_xdd m_S m_yg m_ss m_xD")
        k.o_evac, k.o_tr, k.o_x, k.o_mm, k.o_var, k.o_sd, k.o_add = first("o_evac o_tr o_x o_mm o_var o_sd o_add")
        k.p_act, k.p_up, k.p_x, k.p_down = first("p_act p_up p_x p_down")
        k.r_k2, k.r_kk, k.r_G, k.r_lg, k.r_wd, k.r_cnt, k.r_tr = first("r_k2 r_kk r_G r_lg r_wd r_cnt r_tr")
        k.r_wT, k.r_b2, k.r_bo, k.r_v, k.r_exp, k.r_jobs, k.e_y = first("r_wT r_b2 r_bo r_v r_exp r_jobs e_y")
        k.e_act, k.e_up, k.e_down, k.s_e_0, k.s_e_1, k.r_hi = first("e_act e_up e_down s_e_0 s_e_1 r_hi")
        k.e_split, k.e_h1, k.e_h2, k.e_lo, k.e_dhi = first("e_split e_h1 e_h2 e_lo e_dhi")
        k.t_1, k.t_2, k.t_3, k.t_4, k.s_it = first("t_1 t_2 t_3 t_4 s_it")
        k.q_tanh, k.q_a, k.q_vb, k.q_srow, k.q_row, k.q_col, k.q_e8 = first("q_tanh q_a q_vb q_srow q_row q_col q_e8")
        k.q_U, k.q_sum, k.q_D, k.q_out, k.q_pool, k.q_ex, k.q_exp = first("q_U q_sum q_D q_out q_pool q_ex q_exp")
        [k.q_dex] = first("q_dex")
        k.s_xT = [k.s_xT_0, k.s_xT_1, k.s_xT_2, k.s_xT_3]
        k.s_e = [k.s_e_0, k.s_e_1]
        with ExitStack() as layer0:
            def arena(name, shape, dt=F32):
                return layer0.enter_context(nc.sbuf_tensor(name, shape, dt))

            k.hT = arena("hT", [P, EB, N])
            stream = layer0.enter_context(ExitStack())
            k.res0, k.hn = (stream.enter_context(nc.sbuf_tensor(n, [P, NT, E], F32)) for n in ("res0", "hn"))
            cond_phase(nc, k)
            with ExitStack() as mamba:
                def inner(name, shape, dt=F32):
                    return mamba.enter_context(nc.sbuf_tensor(name, shape, dt))

                k.post = inner("post", [P, CB, N])
                k.CT = inner("CT", [DS, N])
                k.rms = inner("rms", [P, NT])
                k.dt, k.dtA, k.ecs = (inner(n, [P, P]) for n in ("dt", "dtA", "ecs"))
                k.etot = inner("etot", [DS, P])
                k.expA = inner("expA", [P, NH])
                transpose_phase(nc, k, k.hn, k.hT, "ln1w", "ln1b", {"mm": k.t_1})
                inproj_phase(nc, k)
                ygB = inner("ygB", [P, NT // 2, DI])
                ygA = k.hn[:, :, :].rearrange("p i e -> p (i e)").rearrange("p (i e) -> p i e", e=DI)
                k.yg = lambda i: ygA[:, i, :] if i < NT // 2 else ygB[:, i - NT // 2, :]
                ssd_phase(nc, k)
                k.mw1 = k.post[:, 0, :].rearrange("p (j n) -> p j n", j=EB)
                k.mw2 = k.post[:, 1, :].rearrange("p (j n) -> p j n", j=FB)
                outproj_phase(nc, k)
                transpose_phase(nc, k, k.hn, k.hT, "ln2w", "ln2b", {"mm": k.t_2})
                mlp_phase(nc, k)
            transpose_phase(nc, k, k.X, k.hT, None, None, {"mm": k.t_3})
            stream.close()
            k.hTh, k.hTl = (arena(n, [P, EB, N], F32R) for n in ("hTh", "hTl"))
            pooled = layer0.enter_context(ExitStack())
            k.pooled = pooled.enter_context(nc.sbuf_tensor("pooled", [P, NT, E], F32))
            pool_phase(nc, k)
            transpose_phase(nc, k, k.pooled, k.hT, None, None, {"mm": k.t_4})
            pooled.close()
            k.wE = arena("wE", [P, E0, NT])
            k.jobs = arena("jobs", [1, JT["blk"] + E0 * NB], I32)
            route_phase(nc, k)
            experts_phase(nc, k)
        nc.clear_and_free_semaphores(first.handles)
        nc.all_engine_barrier()
        second = taken(nc)
        k.t_5, k.t_6, k.t_7, k.l_mm, k.l_qk, k.l_vm, k.l_du = second("t_5 t_6 t_7 l_mm l_qk l_vm l_du")
        k.l_q, k.l_k, k.l_v, k.l_nb, k.l_zero = second("l_q l_k l_v l_nb l_zero")
        k.a_exp, k.a_qk, k.a_d, k.a_ev, k.a_tr, k.a_att, k.a_pv = second("a_exp a_qk a_d a_ev a_tr a_att a_pv")
        k.a_mask, k.a_lam, k.a_lexp, k.a_max, k.n_sd, k.n_1, k.n_mm = second("a_mask a_lam a_lexp a_max n_sd n_1 n_mm")
        [k.n_x] = second("n_x")
        k.s_wgt, k.s_xz, k.s_put, k.s_b2b, k.u_zero, k.u_mm, k.u_c = second("s_wgt s_xz s_put s_b2b u_zero u_mm u_c")
        k.u_lg, k.u_row, k.u_tr, k.u_oh, k.u_cum, k.u_sub, k.u_exp = second("u_lg u_row u_tr u_oh u_cum u_sub u_exp")
        k.v_tr, k.f_y, k.f_act, k.f_up, k.f_down, k.g_x = second("v_tr f_y f_act f_up f_down g_x")
        k.s_ws, k.v_ev, k.s_f, k.s_ys = ([nc.alloc_semaphore(f"{n}{q}") for q in range(2)]
                                         for n in ("s_ws", "v_ev", "s_f", "s_ys"))
        k.s_xr = [nc.alloc_semaphore(f"s_xr{q}") for q in range(5)]
        k.s_take = [nc.alloc_semaphore(f"s_take{q}") for q in range(4)]
        with ExitStack() as layer1:
            def arena(name, shape, dt=F32):
                return layer1.enter_context(nc.sbuf_tensor(name, shape, dt))

            k.hT = arena("hT1", [P, EB, N])
            with ExitStack() as attn:
                def inner(name, shape, dt=F32):
                    return attn.enter_context(nc.sbuf_tensor(name, shape, dt))

                k.wq, k.wk, k.wv, k.wo = (inner(n, [P, EB, E]) for n in ("wq", "wk", "wv", "wo"))
                k.qT, k.kT = inner("qT", [P, 8, N]), inner("kT", [P, EB, N])
                k.v, k.att = inner("v", [P, NT, E]), inner("att", [P, NT, E])
                k.ms = inner("ms", [P, NT, HEADS])
                transpose_phase(nc, k, k.X, k.hT, None, None, {"mm": k.t_5})
                laplace_phase(nc, k)
                attention_phase(nc, k)
                attention_norm_phase(nc, k)
                transpose_phase(nc, k, k.att, k.hT, "gam", None, {"mm": k.t_6})
                attention_out_phase(nc, k)
            k.xs = nc.dram_tensor("slot_rows", (SLOTS, E), F32, kind="Internal").ap()
            k.ys = nc.dram_tensor("slot_results", (SLOTS, E), F32, kind="Internal").ap()
            k.put, k.take = arena("put", [P, NT], U32), arena("take", [P, NT], U32)
            k.gate = arena("gate", [P, NT])
            k.fw1 = [arena(f"fw1_{q}", [P, EB, FF]) for q in range(2)]
            k.fw2 = [arena(f"fw2_{q}", [P, FB, E]) for q in range(2)]
            k.b2b = arena("b2b", [P, E1, E])
            k.xsT = arena("xsT", [P, EB, SLOTS])
            with nc.sbuf_tensor("rows2", [P, NT, E], F32) as k.rows2:
                transpose_phase(nc, k, k.X, k.hT, None, None, {"mm": k.t_7})
                subject_phase(nc, k)
                dispatch_phase(nc, k)
            capacity_phase(nc, k)
            combine_phase(nc, k)


def blocks(w):
    return w.reshape(w.shape[0] // P, P, w.shape[1]).transpose(1, 0, 2)


def layout(v):
    a = {}
    x = v["x"].reshape(N, E)
    a["x"], a["xT"] = x, x.T
    for n, w in (("wsoma", "L0_cond_Wsoma"), ("wtemp", "L0_cond_Wtemp"), ("wout", "L0_cond_Wout"),
                 ("wn1", "L0_cond_Wn1"), ("wg", "L0_cond_Wg"), ("win", "L0_attn_in_proj_w"),
                 ("wop", "L0_attn_out_proj_w"), ("mw1", "L0_attn_mlp_w1"), ("mw2", "L0_attn_mlp_w2"),
                 ("keysT", "L0_ffn_keys"), ("rwT", "L0_ffn_rw"), ("wq", "L1_attn_Wq"), ("wk", "L1_attn_Wk"),
                 ("wv", "L1_attn_Wv"), ("wo", "L1_attn_Wo")):
        a[n] = blocks(v[w].T)
    a["c2w"] = blocks(v["L0_cond2_W1"])
    a["b2a"] = v["L0_ffn_b2"]
    a["itok0"] = v["itok_B_0_2"]
    a["itok1"] = v["itok_B_0_7"]
    a["subw"] = v["L1_cond2_weight"].transpose(0, 2, 1).reshape(NSUB, EB, P, E).transpose(0, 2, 1, 3)
    a["subb"] = v["L1_cond2_bias"].reshape(NSUB, EB, P).transpose(0, 2, 1)
    a["wgt"] = blocks(v["L1_ffn_wg"])
    a["fw1"] = v["L1_ffn_w1"].reshape(E1, EB, P, FF).transpose(0, 2, 1, 3)
    a["fw2"] = v["L1_ffn_w2"].reshape(E1, FB, P, E).transpose(0, 2, 1, 3)
    a["b2b"] = v["L1_ffn_b2"]
    a["ew1"] = v["L0_ffn_w1"].transpose(0, 2, 1).reshape(E0, EB, P, FF).transpose(0, 2, 1, 3)
    a["ew2"] = v["L0_ffn_w2"].transpose(0, 2, 1).reshape(E0, FB, P, E).transpose(0, 2, 1, 3)
    a["eb1"] = v["L0_ffn_b1"].reshape(E0, FB, P).transpose(0, 2, 1)

    def column(x):
        x = x.reshape(-1)
        if x.size < P:
            return np.concatenate([x, np.zeros(P - x.size, x.dtype)])[:, None]
        return x.reshape(x.size // P, P).T

    cols = {"bg": v["L0_cond_bg"], "bn1": v["L0_cond_bn1"], "bsoma": v["L0_cond_bsoma"], "btemp": v["L0_cond_btemp"],
            "ln1w": v["L0_attn_ln1_w"], "ln1b": v["L0_attn_ln1_b"], "convb": v["L0_attn_conv_b"],
            "normw": v["L0_attn_norm_w"], "ln2w": v["L0_attn_ln2_w"], "ln2b": v["L0_attn_ln2_b"],
            "mlpb1": v["L0_attn_mlp_b1"], "c2b1": v["L0_cond2_b1"], "c2v": v["L0_cond2_v"]}
    cols = {n: column(x) for n, x in cols.items()}
    cols["blend"] = v["cond_1024"].reshape(2, EB, P).transpose(2, 1, 0).reshape(P, 4)
    cols["wn2"] = np.concatenate([column(v["cond_256"][0]), column(v["cond_256"][1])], 1)
    cols["convw"] = v["L0_attn_conv_w"].reshape(CB, P, 4).transpose(1, 0, 2).reshape(P, 20)
    cols["gam"] = column(np.concatenate([v["L1_attn_gamma"]] * 4))
    cols["b1a"] = v["L0_ffn_b1"].reshape(E0, FB, P).transpose(2, 0, 1).reshape(P, E0 * FB)
    cols["b1b"] = v["L1_ffn_b1"].reshape(E1, FB, P).transpose(2, 0, 1).reshape(P, E1 * FB)
    a["cols"] = np.concatenate([cols[n] for n, _ in COLS], 1)
    rows = {"tau": [v["condB_tauraws"], v["L0_cond_tau_ctx"]], "bn2": [v["condB_bn2"]], "gamma": [v["L0_cond_gamma"]],
            "beta": [v["L0_cond_beta"]], "dtb": [v["L0_attn_dt_bias"]], "alog": [v["L0_attn_A_log"]],
            "dskip": [v["L0_attn_D"]], "mlpb2": [v["L0_attn_mlp_b2"]], "rb": [v["L0_ffn_rb"]],
            "zx": [v["condB_zX"]], "zy": [v["condB_zY"]], "zr": [v["condB_zR"]],
            "lam": [v["L1_attn_lambda_q1"], v["L1_attn_lambda_k1"], v["L1_attn_lambda_q2"], v["L1_attn_lambda_k2"]]}
    a["rows"] = np.concatenate([x.reshape(-1) for n, _ in ROWS for x in rows[n]])
    a["consts"] = shape_constants()
    return a


def kernel(**inputs):
    import concourse.bacc as _bacc
    from concourse import mybir as _mybir
    from concourse.bass_utils import run_bass_kernel_spmd as _run

    nc = _bacc.Bacc("TRN2", target_bir_lowering=False, num_devices=1)
    arrays, d = {}, {}
    for name, a in layout({n: np.asarray(x) for n, x in inputs.items()}).items():
        a = np.ascontiguousarray(a)
        arrays[f"in_{name}_dram"] = a
        d[name] = nc.dram_tensor(f"in_{name}_dram", a.shape, _mybir.dt.from_np(a.dtype), kind="ExternalInput").ap()
    d["out"] = nc.dram_tensor("out_0_dram", (N, E), F32, kind="ExternalOutput").ap()
    network(nc, d)
    r = _run(nc, [arrays], core_ids=[0])
    return r.results[0]["out_0_dram"].reshape(B, T, E)
```

```python
from contextlib import ExitStack

import numpy as np
import concourse.bass as bass
from concourse import mybir

F32 = mybir.dt.float32
I32 = mybir.dt.int32
U32 = mybir.dt.uint32
BF16 = mybir.dt.bfloat16
F32R = mybir.dt.float32r
ALU = mybir.AluOpType
ACT = mybir.ActivationFunctionType
AX = mybir.AxisListType

B, T, E = 2, 1024, 256
N = B * T
P = 128
NT = N // P
TB = T // P
EB = E // P
W = 512
NW = N // W
HID = 64
DI, NH, DS, HD = 512, 8, 64, 64
CB = 5
FF = 1024
FB = FF // P
E0, TOPK = 16, 4
E1, CAP = 8, 320
NSUB = 8
EPS = 1e-5
NEG = -1e30
LAMBDA_INIT = 0.8 - 0.6 * float(np.exp(-0.3 * 2))

COLS = [("bg", 2), ("bn1", 1), ("bsoma", 2), ("btemp", 2), ("blend", 4), ("wn2", 2), ("ln1w", 2), ("ln1b", 2),
        ("convw", 20), ("convb", 5), ("normw", 4), ("ln2w", 2), ("ln2b", 2), ("mlpb1", 8), ("c2b1", 1), ("c2v", 1),
        ("gam", 2), ("b1a", E0 * FB), ("b1b", E1 * FB)]
ROWS = [("tau", 3), ("bn2", 2), ("gamma", 256), ("beta", 256), ("dtb", 8), ("alog", 8), ("dskip", 8),
        ("mlpb2", 256), ("rb", 16), ("zx", 2), ("zy", 2), ("zr", 2), ("lam", 128)]
CONSTS = [("ident", 128), ("le", 128), ("gt", 128), ("lt", 128), ("ones", 128), ("lap", 512), ("penp", 128),
          ("pens", 128), ("penc", 128), ("delta8", 64), ("penb", 24), ("iota", 16), ("cntp", 8), ("causal", 128)]


def offsets(table):
    at, out = 0, {}
    for name, n in table:
        out[name] = (at, n)
        at += n
    return out, at


COL_AT, NCOL = offsets(COLS)
ROW_AT, NROW = offsets(ROWS)
CONST_AT, NCONST = offsets(CONSTS)


def shape_constants():
    c = np.zeros((P, NCONST), np.float32)
    k = np.arange(P)

    def put(name, a):
        at, n = CONST_AT[name]
        c[:a.shape[0], at:at + n] = a.reshape(a.shape[0], n)

    r, q = k[:, None], k[None, :]
    put("ident", (r == q) * 1.0)
    put("le", (r <= q) * 1.0)
    put("gt", (r > q) * 1.0)
    put("lt", (r < q) * 1.0)
    put("ones", np.ones((P, P)))
    lap = np.zeros((E, E))
    for j in range(E):
        lap[j, j] -= 2.0
        lap[j - 1 if j > 0 else 1, j] += 1.0
        lap[j + 1 if j < E - 1 else E - 2, j] += 1.0
    put("lap", lap.reshape(EB, P, E).transpose(1, 0, 2))
    put("penp", np.where(r <= q, 0.0, NEG))
    put("pens", np.where(r >= q, 0.0, NEG))
    put("penc", np.where(r != q, 0.0, NEG))
    put("delta8", np.broadcast_to(np.eye(8), (P, 8, 8)))
    m = np.arange(8)
    mr, mq = m[:, None], m[None, :]
    put("penb", np.stack([np.where(mr < mq, 0.0, NEG), np.where(mr > mq, 0.0, NEG), np.where(mr != mq, 0.0, NEG)], 1))
    put("iota", np.broadcast_to(np.arange(16), (P, 16)))
    put("cntp", k[:, None] + 1.0 + P * np.arange(8)[None, :])
    put("causal", np.where(q <= r, 0.0, NEG))
    return c


def cond_phase(nc, k):
    ps, c = k.ps, k.col
    with ExitStack() as ctx:
        def sb(name, shape, dt=F32):
            return ctx.enter_context(nc.sbuf_tensor(name, shape, dt))

        k.wsoma, k.wtemp, k.wout = (sb(n, [P, EB, E]) for n in ("wsoma", "wtemp", "wout"))
        k.wn1 = sb("wn1", [P, EB, HID])
        k.wg = sb("wg", [P, 2 * EB, E])
        xT = sb("xT", [P, EB, N])
        ctxT = sb("ctxT", [P, EB, N])
        gatT = sb("gatT", [P, EB, N])
        modT = sb("modT", [P, 2, EB, N])
        somT = sb("somT", [P, EB, N])
        h1T = sb("h1T", [HID, N])
        w2b = sb("w2b", [HID, 2, P])
        alpha = sb("alpha", [P, 3])
        bw = sb("bw", [P, EB, 2])
        tmp = sb("tmp", [P, 8])
        stats = sb("stats", [P, NT, 6])
        mv = sb("mv", [P, NT, 2])
        rstd = sb("rstd", [P, NT])
        SOMA, H1, WG, MOD, GATE, OUT = 0, 8, 12, 20, 28, 36

        block = ctx.enter_context(nc.Block())

        @block.sync
        def _(sp):
            sp.dma_start(k.cols[:, :], k.d["cols"]).then_inc(k.s_small, 16)
            sp.dma_start(k.wsoma[:, :, :], k.d["wsoma"]).then_inc(k.s_small, 16)
            for w in range(NW):
                sp.dma_start(xT[:, :, w * W:(w + 1) * W],
                             k.d["xT"].rearrange("(f p) n -> p f n", p=P)[:, :, w * W:(w + 1) * W]).then_inc(k.s_xT[w], 16)
            sp.dma_start(k.rows[:, :], k.d["rows"].partition_broadcast(P)).then_inc(k.s_rows, 16)
            sp.dma_start(k.wn1[:, :, :], k.d["wn1"]).then_inc(k.s_wA, 16)
            sp.dma_start(k.wg[:, :, :], k.d["wg"]).then_inc(k.s_wA, 16)
            sp.dma_start(k.consts[:, :], k.d["consts"]).then_inc(k.s_wA, 16)
            sp.dma_start(k.wtemp[:, :, :], k.d["wtemp"]).then_inc(k.s_wA, 16)
            sp.dma_start(k.wout[:, :, :], k.d["wout"]).then_inc(k.s_wA, 16)
            sp.dma_start(k.X[:, :, 0:E], k.d["x"].rearrange("(i p) e -> p i e", p=P)).then_inc(k.s_x, 16)
            sp.dma_start(k.win[:, :, :], k.d["win"]).then_inc(k.s_wB, 16)
            sp.dma_start(k.wop[:, :, :], k.d["wop"]).then_inc(k.s_wB, 16)
            sp.dma_start(k.c2w[:, :, :], k.d["c2w"]).then_inc(k.s_wB, 16)
            sp.dma_start(k.keysT[:, :, :], k.d["keysT"]).then_inc(k.s_wB, 16)
            sp.dma_start(k.rwT[:, :, :], k.d["rwT"]).then_inc(k.s_wB, 16)
            sp.dma_start(k.b2a[:, :], k.d["b2a"]).then_inc(k.s_wB, 16)
            sp.wait_ge(k.s_wB, 16 * 6)
            sp.wait_ge(k.s_wA, 16 * 5)
            sp.wait_ge(k.s_x, 16)
            sp.wait_ge(k.s_rows, 16)

        @block.tensor
        def _(pe):
            def product(g, lhs, rhs, m=P, n=W):
                if g >= 8:
                    pe.wait_ge(k.c_evac, g - 7)
                for j, (a, b) in enumerate(zip(lhs, rhs)):
                    last = nc.tensor.matmul(ps[0:m, g % 8, 0:n], a, b, start=(j == 0), stop=(j == len(lhs) - 1))
                last.then_inc(k.c_mm, 1)

            pe.wait_ge(k.s_small, 32)
            for w in range(NW):
                pe.wait_ge(k.s_xT[w], 16)
                tok = slice(w * W, (w + 1) * W)
                for f in range(EB):
                    product(SOMA + w * EB + f, [k.wsoma[:, j, f * P:(f + 1) * P] for j in range(EB)],
                            [xT[:, j, tok] for j in range(EB)])
            pe.wait_ge(k.s_wA, 16 * 5)
            for w in range(NW):
                tok = slice(w * W, (w + 1) * W)
                product(H1 + w, [k.wn1[:, j, :] for j in range(EB)], [xT[:, j, tok] for j in range(EB)], m=HID)
            for w in range(NW):
                tok = slice(w * W, (w + 1) * W)
                pe.wait_ge(k.c_ctx, EB * (w // 2 + 1))
                for f in range(EB):
                    product(WG + w * EB + f, [k.wg[:, j, f * P:(f + 1) * P] for j in range(2 * EB)],
                            [xT[:, 0, tok], xT[:, 1, tok], ctxT[:, 0, tok], ctxT[:, 1, tok]])
            pe.wait_ge(k.c_w2b, 2)
            pe.wait_ge(k.c_evac, H1 + NW)
            for w in range(NW):
                tok = slice(w * W, (w + 1) * W)
                for d in range(2):
                    product(MOD + w * 2 + d, [w2b[:, d, :]], [h1T[:, tok]])
            for w in range(NW):
                tok = slice(w * W, (w + 1) * W)
                pe.wait_ge(k.c_blend, EB * (w // 2 + 1))
                for f in range(EB):
                    product(GATE + w * EB + f, [k.wtemp[:, j, f * P:(f + 1) * P] for j in range(EB)],
                            [gatT[:, j, tok] for j in range(EB)])
            for i in range(NT):
                g, h = OUT + i // 2, i % 2
                if h == 0:
                    pe.wait_ge(k.c_evac, g - 7)
                pe.wait_ge(k.c_sg, i // 4 + 1)
                for j in range(EB):
                    last = nc.tensor.matmul(ps[:, g % 8, h * E:(h + 1) * E], somT[:, j, i * P:(i + 1) * P],
                                            k.wout[:, j, :], start=(h == 0 and j == 0), stop=(j == EB - 1),
                                            skip_group_check=True)
                last.then_inc(k.c_out, 1)

        @block.scalar
        def _(act):
            act.wait_ge(k.s_rows, 16)
            nc.scalar.activation(tmp[:, 0:3], k.rows[:, 0:3], ACT.Exp).then_inc(k.c_tau, 1)
            act.wait_ge(k.c_bdiff, 2)
            nc.scalar.activation(bw[:, :, :], bw[:, :, :], ACT.Exp).then_inc(k.c_bexp, 1)
            act.wait_ge(k.s_small, 32)

            def evac(g, out, func, bias, m=P):
                act.wait_ge(k.c_mm, g + 1)
                nc.scalar.activation(out, ps[0:m, g % 8, :], func, bias=bias).then_inc(k.c_evac, 1)

            for w in range(NW):
                for f in range(EB):
                    evac(SOMA + w * EB + f, somT[:, f, w * W:(w + 1) * W], ACT.Gelu, c("bsoma", f))
            for w in range(NW):
                evac(H1 + w, h1T[:, w * W:(w + 1) * W], ACT.Gelu, c("bn1", 0)[0:HID], m=HID)
            for w in range(NW):
                for f in range(EB):
                    evac(WG + w * EB + f, gatT[:, f, w * W:(w + 1) * W], ACT.Sigmoid, c("bg", f))
            for w in range(NW):
                for d in range(2):
                    evac(MOD + w * 2 + d, modT[:, d, 0, w * W:(w + 1) * W], ACT.Sigmoid, k.row("bn2", d))
            for w in range(NW):
                for f in range(EB):
                    evac(GATE + w * EB + f, ctxT[:, f, w * W:(w + 1) * W], ACT.Sigmoid, c("btemp", f))
            for r in range(2):
                act.wait_ge(k.c_var, r + 1)
                nc.scalar.activation(rstd[:, :], mv[:, :, 1], ACT.Sqrt, bias=k.eps[:, 0:1]).then_inc(k.c_sd, 1)

        @block.vector
        def _(dve):
            then = chain(k, dve, "dve")
            nc.vector.memset(k.eps[:, :], EPS).then_inc(k.c_init, 1)
            nc.vector.memset(k.X[:, :, E:E + 1], 1.0).then_inc(k.c_init, 1)
            dve.wait_ge(k.c_init, 2)
            dve.wait_ge(k.c_tau, 1)
            then(nc.vector.tensor_scalar(tmp[:, 3:6], tmp[:, 0:3], 1.0, None, ALU.add))
            then(nc.vector.reciprocal(alpha[:, :], tmp[:, 3:6]))
            dve.wait_ge(k.s_small, 32)
            bl = c("blend", 0, 4).rearrange("p (f d) -> p f d", d=2)
            then(nc.vector.tensor_tensor(tmp[:, 6:8], bl[:, :, 0], bl[:, :, 1], ALU.max))
            for d in range(2):
                nc.vector.tensor_tensor(bw[:, :, d], bl[:, :, d], tmp[:, 6:8], ALU.subtract).then_inc(k.c_bdiff, 1)
            dve.wait_ge(k.s_wA, 16 * 5)
            for d in range(2):
                nc.vector.tensor_scalar(w2b[:, d, :], k.const("ones")[0:HID], c("wn2", d)[0:HID], None,
                                        ALU.mult).then_inc(k.c_w2b, 1)
            for w in range(NW):
                dve.wait_ge(k.s_xT[w], 16)
            for b in range(B):
                tok = slice(b * T, (b + 1) * T)
                for f in range(EB):
                    nc.vector.tensor_tensor_scan(ctxT[:, f, tok], alpha[:, 2:3].to_broadcast([P, T]), xT[:, f, tok],
                                                 0.0, ALU.mult, ALU.add).then_inc(k.c_ctx, 1)
            dve.wait_ge(k.c_bexp, 1)
            then(nc.vector.tensor_tensor(tmp[:, 0:2], bw[:, :, 0], bw[:, :, 1], ALU.add))
            then(nc.vector.reciprocal(tmp[:, 2:4], tmp[:, 0:2]))
            for d in range(2):
                then(nc.vector.tensor_tensor(bw[:, :, d], bw[:, :, d], tmp[:, 2:4], ALU.mult))
            for b in range(B):
                tok = slice(b * T, (b + 1) * T)
                dve.wait_ge(k.c_evac, WG + 2 * EB * (b + 1))
                for f in range(EB):
                    then(nc.vector.tensor_tensor(gatT[:, f, tok], gatT[:, f, tok], xT[:, f, tok], ALU.mult))
                dve.wait_ge(k.c_evac, MOD + 4 * (b + 1))
                for f in (1, 0):
                    for d in range(2):
                        then(nc.vector.scalar_tensor_tensor(modT[:, d, f, tok], modT[:, d, 0, tok], 0.5,
                                                            gatT[:, f, tok], ALU.add, ALU.mult))
                        then(nc.vector.tensor_tensor_scan(modT[:, d, f, tok], alpha[:, d:d + 1].to_broadcast([P, T]),
                                                          modT[:, d, f, tok], 0.0, ALU.mult, ALU.add))
                    then(nc.vector.tensor_scalar(gatT[:, f, tok], modT[:, 0, f, tok], bw[:, f, 0:1], None, ALU.mult))
                    nc.vector.scalar_tensor_tensor(gatT[:, f, tok], modT[:, 1, f, tok], bw[:, f, 1:2],
                                                   gatT[:, f, tok], ALU.mult, ALU.add).then_inc(k.c_blend, 1)
            for w in range(NW):
                tok = slice(w * W, (w + 1) * W)
                dve.wait_ge(k.c_evac, GATE + EB * (w + 1))
                nc.vector.tensor_tensor(somT[:, :, tok], somT[:, :, tok], ctxT[:, :, tok],
                                        ALU.mult).then_inc(k.c_sg, 1)
            for i in range(NT):
                g, h = OUT + i // 2, i % 2
                dve.wait_ge(k.c_out, 2 * (i // 2) + 2)
                last = nc.vector.bn_stats(stats[:, i, :], ps[:, g % 8, h * E:(h + 1) * E])
            then(last)
            for i in range(NT):
                last = nc.vector.bn_aggr(mv[:, i, :], stats[:, i, :])
            last.then_inc(k.c_var, 1)
            dve.wait_ge(k.c_var, 1)
            dve.wait_ge(k.c_sd, 1)
            then(nc.vector.reciprocal(rstd[:, :], rstd[:, :]))
            for i in range(NT):
                g, h = OUT + i // 2, i % 2
                nc.vector.tensor_scalar(k.res0[:, i, :], ps[:, g % 8, h * E:(h + 1) * E], mv[:, i, 0:1],
                                        rstd[:, i:i + 1], ALU.subtract, ALU.mult).then_inc(k.c_norm, 1)
            for q in (2, 3):
                r = k.res0[:, 4 * q:4 * q + 4, :]
                dve.wait_ge(k.c_norm, 4 * (q + 1))
                then(nc.vector.tensor_tensor(r, r, k.row("gamma", 0, E).unsqueeze(1).to_broadcast([P, 4, E]), ALU.mult))
                then(nc.vector.tensor_tensor(r, r, k.row("beta", 0, E).unsqueeze(1).to_broadcast([P, 4, E]), ALU.add))
            for i in (*range(NT // 2, NT), *range(NT // 2)):
                if i < NT // 2:
                    dve.wait_ge(k.c_aff, 2 * (i // 4 + 1))
                last = nc.vector.bn_stats(stats[:, i, :], k.res0[:, i, :])
            then(last)
            for i in range(NT):
                last = nc.vector.bn_aggr(mv[:, i, :], stats[:, i, :])
            last.then_inc(k.c_var, 1)
            dve.wait_ge(k.c_sd, 2)
            then(nc.vector.reciprocal(rstd[:, :], rstd[:, :]))
            for i in range(NT):
                nc.vector.tensor_scalar(k.hn[:, i, :], k.res0[:, i, :], mv[:, i, 0:1], rstd[:, i:i + 1],
                                        ALU.subtract, ALU.mult).then_inc(k.c_hn, 1)

        @block.gpsimd
        def _(pool):
            pool.wait_ge(k.s_rows, 16)
            for q in range(2):
                r = k.res0[:, 4 * q:4 * q + 4, :]
                pool.wait_ge(k.c_norm, 4 * (q + 1))
                nc.gpsimd.tensor_tensor(r, r, k.row("gamma", 0, E).unsqueeze(1).to_broadcast([P, 4, E]),
                                        ALU.mult).then_inc(k.c_aff, 1)
                pool.wait_ge(k.c_aff, 2 * q + 1)
                nc.gpsimd.tensor_tensor(r, r, k.row("beta", 0, E).unsqueeze(1).to_broadcast([P, 4, E]),
                                        ALU.add).then_inc(k.c_aff, 1)


def chain(k, eng, name):
    sem, count = k.chains[name]

    def then(ins):
        count[0] += 1
        ins.then_inc(sem, 1)
        eng.wait_ge(sem, count[0])
    return then


def transpose_phase(nc, k, src, dst, wname, bname, s, loads=None):
    with nc.Block() as block:
        if loads:
            block.sync(loads)

        @block.tensor
        def _(pe):
            for g in range(NW * EB):
                w, f = g // EB, g % EB
                for j in range(4):
                    last = nc.tensor.transpose(k.ps[:, g, j * P:(j + 1) * P], src[:, 4 * w + j, f * P:(f + 1) * P],
                                               k.const("ident"))
                last.then_inc(s["mm"], 1)

        def evacuate(eng, which):
            for g in range(which, NW * EB, 2):
                w, f = g // EB, g % EB
                eng.wait_ge(s["mm"], g + 1)
                out = dst[:, f, w * W:(w + 1) * W]
                if wname is None:
                    (nc.vector.tensor_copy if which else nc.scalar.copy)(out, k.ps[:, g, :])
                elif bname is None:
                    if which:
                        nc.vector.tensor_scalar(out, k.ps[:, g, :], k.col(wname, f), None, ALU.mult)
                    else:
                        nc.scalar.activation(out, k.ps[:, g, :], ACT.Copy, scale=k.col(wname, f))
                elif which:
                    nc.vector.tensor_scalar(out, k.ps[:, g, :], k.col(wname, f), k.col(bname, f), ALU.mult, ALU.add)
                else:
                    nc.scalar.activation(out, k.ps[:, g, :], ACT.Identity, bias=k.col(bname, f),
                                         scale=k.col(wname, f))

        @block.scalar
        def _(act):
            evacuate(act, 0)

        @block.vector
        def _(dve):
            evacuate(dve, 1)


def inproj_phase(nc, k):
    ps = k.ps
    with ExitStack() as ctx:
        def sb(name, shape, dt=F32):
            return ctx.enter_context(nc.sbuf_tensor(name, shape, dt))

        pre = sb("pre", [P, CB, B, T + 3])
        z = sb("dtz", [P, 4, P])
        DT = 7
        ORDER = (4, 0, 1, 2, 3)

        block = ctx.enter_context(nc.Block())

        @block.tensor
        def _(pe):
            for g in range(CB * NW):
                cb, w = ORDER[g // NW], g % NW
                if g == NW:
                    for i in range(NT):
                        for j in range(EB):
                            last = nc.tensor.matmul(ps[:, DT, i * NH:(i + 1) * NH], k.hT[:, j, i * P:(i + 1) * P],
                                                    k.win[:, j, 2 * DI + 2 * DS:], start=(i == 0 and j == 0),
                                                    stop=(j == EB - 1), skip_group_check=True)
                    last.then_inc(k.i_dt, 1)
                if g >= 7:
                    pe.wait_ge(k.i_evac, g - 6)
                for j in range(EB):
                    last = nc.tensor.matmul(ps[:, g % 7, :], k.win[:, j, DI + cb * P:DI + (cb + 1) * P],
                                            k.hT[:, j, w * W:(w + 1) * W], start=(j == 0), stop=(j == EB - 1))
                last.then_inc(k.i_mm, 1)
            pe.wait_ge(k.i_dtA, 1)
            pe.wait_ge(k.i_sp, 1)
            nc.tensor.matmul(ps[:, DT, 0:P], k.const("le"), k.dtA[:, :], start=True, stop=True)
            nc.tensor.matmul(ps[0:DS, DT, P:2 * P], k.const("ones", 0, DS), k.dtA[:, :], start=False, stop=True,
                             skip_group_check=True).then_inc(k.i_cs, 1)

        @block.scalar
        def _(act):
            then = chain(k, act, "act")
            nc.scalar.activation(k.expA[:, :], k.row("alog", 0, NH), ACT.Exp).then_inc(k.i_expA, 1)
            for g in range(CB * NW):
                cb, w = ORDER[g // NW], g % NW
                if g == NW:
                    act.wait_ge(k.i_abs, 1)
                    then(nc.scalar.activation(z[:, 1, :], z[:, 1, :], ACT.Exp))
                    nc.scalar.activation(z[:, 2, :], z[:, 1, :], ACT.Ln, bias=1.0).then_inc(k.i_ln, 1)
                act.wait_ge(k.i_mm, g + 1)
                if g == 0:
                    act.wait_ge(k.i_pad, 1)
                at = 3 + (w % 2) * W
                nc.scalar.copy(pre[:, cb, w // 2, at:at + W], ps[:, g % 7, :])
                nc.scalar.activation(k.post[:, cb, w * W:(w + 1) * W], ps[:, g % 7, :], ACT.Identity,
                                     bias=k.col("convb", cb), scale=k.col("convw", 4 * cb + 3)).then_inc(k.i_evac, 1)
            for n, cb in enumerate(ORDER):
                act.wait_ge(k.i_conv, n + 1)
                nc.scalar.activation(k.post[:, cb, :], k.post[:, cb, :], ACT.Silu).then_inc(k.i_silu, 1)
            act.wait_ge(k.i_cs, 1)
            nc.scalar.activation(k.ecs[:, :], ps[:, DT, 0:P], ACT.Exp)
            nc.scalar.activation(k.etot[:, :], ps[0:DS, DT, P:2 * P], ACT.Exp)

        @block.vector
        def _(dve):
            then = chain(k, dve, "dve")
            nc.vector.memset(pre[:, :, :, 0:3], 0.0).then_inc(k.i_pad, 1)

            def convolve(n):
                cb = ORDER[n]
                dve.wait_ge(k.i_evac, NW * (n + 1))
                out = k.post[:, cb, :].rearrange("p (b t) -> p b t", b=B)
                for q in (2, 1, 0):
                    last = nc.vector.scalar_tensor_tensor(out, pre[:, cb, :, q:q + T], k.col("convw", 4 * cb + q), out,
                                                          ALU.mult, ALU.add)
                    if q:
                        then(last)
                last.then_inc(k.i_conv, 1)

            convolve(0)
            dve.wait_ge(k.i_dt, 1)
            heads = "p (i h) -> p i h"
            then(nc.vector.tensor_tensor(z[:, 0, :].rearrange(heads, h=NH), ps[:, DT, 0:P].rearrange(heads, h=NH),
                                         k.row("dtb", 0, NH).unsqueeze(1).to_broadcast([P, NT, NH]), ALU.add))
            then(nc.vector.tensor_scalar(z[:, 1, :], z[:, 0, :], -1.0, None, ALU.mult))
            nc.vector.tensor_tensor(z[:, 1, :], z[:, 0, :], z[:, 1, :], ALU.min).then_inc(k.i_abs, 1)
            dve.wait_ge(k.i_ln, 1)
            then(nc.vector.tensor_scalar(z[:, 3, :], z[:, 1, :], 1.0, -1.0, ALU.add, ALU.add))
            then(nc.vector.tensor_scalar(k.dt[:, :], z[:, 3, :], 0.0, None, ALU.is_equal))
            then(nc.vector.tensor_tensor(z[:, 3, :], z[:, 3, :], k.dt[:, :], ALU.add))
            then(nc.vector.tensor_tensor(z[:, 2, :], z[:, 2, :], k.dt[:, :], ALU.add))
            then(nc.vector.reciprocal(z[:, 3, :], z[:, 3, :]))
            then(nc.vector.tensor_tensor(z[:, 2, :], z[:, 2, :], z[:, 3, :], ALU.mult))
            then(nc.vector.tensor_tensor(z[:, 2, :], z[:, 2, :], z[:, 1, :], ALU.mult))
            then(nc.vector.scalar_tensor_tensor(k.dt[:, :], z[:, 0, :], 0.0, z[:, 2, :], ALU.max,
                                                ALU.add)) 
            nc.vector.tensor_scalar(z[:, 0, :], k.dt[:, :], -1.0, None, ALU.mult).then_inc(k.i_sp, 1)
            dve.wait_ge(k.i_sp, 1)
            dve.wait_ge(k.i_expA, 1)
            nc.vector.tensor_tensor(k.dtA[:, :].rearrange(heads, h=NH), z[:, 0, :].rearrange(heads, h=NH),
                                    k.expA[:, :].unsqueeze(1).to_broadcast([P, NT, NH]), ALU.mult).then_inc(k.i_dtA, 1)
            for n in range(1, CB):
                convolve(n)

        @block.sync
        def _(sp):
            sp.wait_ge(k.i_silu, 1)
            sp.dma_start(k.CT[:, :], k.post[DS:2 * DS, CB - 1, :]).then_inc(k.s_ct, 16)
            sp.wait_ge(k.s_ct, 16)


def ssd_phase(nc, k):
    ps = k.ps
    Z, XT, BC, SEG, YD, YO, S = 0, 1, 2, 3, 5, 6, 7
    with ExitStack() as ctx:
        def sb(name, shape, dt=F32):
            return ctx.enter_context(nc.sbuf_tensor(name, shape, dt))

        sz = sb("sz", [P, 2, DI])
        xst = sb("xst", [P, 2, DI])
        xD = sb("xD", [P, 2, DI])
        xdt = sb("xdt", [P, 2, DI])
        xdd = sb("xdd", [P, 2, DI])
        Bt = sb("Bt", [P, 2, DS])
        cbm = sb("cbm", [P, P])
        G = sb("G", [P, 2, NH, P])
        Ex = sb("Ex", [P, NH, P])
        M = sb("M", [P, 2, NH, P])
        y = sb("y", [P, DI])
        h = sb("h", [DS, DI])
        hd = sb("hd", [DS, DI])
        sq = sb("sq", [P, DI], BF16)
        ss = sb("ss", [P, NT])
        yo = sb("yo", [P, DI])

        def heads(ap):
            return ap.rearrange("p (h w) -> p h w", h=NH)

        def per_head(t, i, p=P, w=HD):
            return t[0:p, i * NH:(i + 1) * NH].unsqueeze(2).to_broadcast([p, NH, w])

        def off(i):
            return i - i // TB

        block = ctx.enter_context(nc.Block())

        @block.tensor
        def _(pe):
            def prepare(i):
                tok = slice(i * P, (i + 1) * P)
                if i:
                    pe.wait_ge(k.m_xst, i)
                for f in range(4):
                    last = nc.tensor.transpose(ps[:, XT, f * P:(f + 1) * P], k.post[:, f, tok], k.const("ident"))
                last.then_inc(k.m_xt, 1)
                if i:
                    pe.wait_ge(k.m_bcu, 2 * i)
                nc.tensor.transpose(ps[:, BC, 0:DS], k.post[0:DS, 4, tok], k.const("ident", 0, DS)[0:DS, :])
                nc.tensor.matmul(ps[:, BC, P:2 * P], k.post[0:DS, 4, tok], k.CT[:, tok], start=True,
                                 stop=True).then_inc(k.m_bc, 1)
                pe.wait_ge(k.m_G, i + 1)
                if i:
                    pe.wait_ge(k.m_E, i)
                for q in range(NH):
                    last = nc.tensor.matmul(ps[:, SEG + q // 4, (q % 4) * P:(q % 4 + 1) * P], G[:, i % 2, q, :],
                                            k.const("le"), start=(q % 4 == 0), stop=True, skip_group_check=True)
                last.then_inc(k.m_seg, 1)
                if i:
                    pe.wait_ge(k.m_sz, i)
                for j in range(EB):
                    last = nc.tensor.matmul(ps[:, Z, :], k.hT[:, j, tok], k.win[:, j, 0:DI], start=(j == 0),
                                            stop=(j == EB - 1))
                last.then_inc(k.m_z, 1)

            def combine(i):
                c = i % TB
                pe.wait_ge(k.m_M, i + 1)
                pe.wait_ge(k.m_xdt, i + 1)
                if i:
                    pe.wait_ge(k.m_y2, i)
                for q in range(NH):
                    last = nc.tensor.matmul(ps[:, YD, q * HD:(q + 1) * HD], M[:, i % 2, q, :],
                                            xdt[:, i % 2, q * HD:(q + 1) * HD], start=(q == 0), stop=True,
                                            skip_group_check=True)
                last.then_inc(k.m_yd, 1)
                if c:
                    pe.wait_ge(k.m_h, i - i // TB)
                    if off(i) > 1:
                        pe.wait_ge(k.m_y1, off(i) - 1)
                    nc.tensor.matmul(ps[:, YO, :], k.CT[:, i * P:(i + 1) * P], h[:, :], start=True,
                                     stop=True).then_inc(k.m_yo, 1)
                if c < TB - 1:
                    pe.wait_ge(k.m_xdd, i + 1)
                    if i:
                        pe.wait_ge(k.m_h, i - i // TB)
                    nc.tensor.matmul(ps[0:DS, S, :], Bt[:, i % 2, :], xdd[:, i % 2, :], start=True,
                                     stop=True).then_inc(k.m_S, 1)

            prepare(0)
            for i in range(NT):
                if i + 1 < NT:
                    prepare(i + 1)
                combine(i)

        @block.scalar
        def _(act):
            def square(i):
                act.wait_ge(k.m_yg, i + 1)
                nc.scalar.activation(sq[:, :], k.yg(i), ACT.Square, accum_out=ss[:, i:i + 1]).then_inc(k.m_ss, 1)
                act.wait_ge(k.m_ss, i + 1)

            for i in range(NT):
                act.wait_ge(k.m_xt, i + 1)
                if i >= 2:
                    act.wait_ge(k.m_xD, i - 1)
                    act.wait_ge(k.m_xdt, i - 1)
                nc.scalar.copy(xst[:, i % 2, :], ps[:, XT, :]).then_inc(k.m_xst, 1)
                act.wait_ge(k.m_seg, i + 1)
                if i:
                    act.wait_ge(k.m_M, i)
                    act.wait_ge(k.m_xdd, i)
                nc.scalar.activation(Ex[:, :, :], ps[:, SEG:SEG + 2, :].rearrange("p b (q t) -> p (b q) t", q=4),
                                     ACT.Exp).then_inc(k.m_E, 1)
                act.wait_ge(k.m_z, i + 1)
                if i >= 2:
                    act.wait_ge(k.m_yg, i - 1)
                nc.scalar.activation(sz[:, i % 2, :], ps[:, Z, :], ACT.Tanh, scale=0.5).then_inc(k.m_tz, 1)
                if i >= 2:
                    square(i - 2)
            square(NT - 2)
            square(NT - 1)
            nc.scalar.activation(k.rms[:, :], ss[:, :], ACT.Sqrt, bias=k.eps[:, 0:1], scale=0.25 / DI)

        @block.gpsimd
        def _(pool):
            def masked_steps(i):
                if i >= 2:
                    pool.wait_ge(k.m_seg, i - 1)
                nc.gpsimd.tensor_tensor(G[:, i % 2, :, :], k.const("gt").unsqueeze(1).to_broadcast([P, NH, P]),
                                        per_head(k.dtA, i, w=P), ALU.mult).then_inc(k.m_G, 1)

            masked_steps(0)
            for i in range(NT):
                if i + 1 < NT:
                    masked_steps(i + 1)
                pool.wait_ge(k.m_xst, i + 1)
                if i >= 2:
                    pool.wait_ge(k.m_xdd, i - 1)
                    pool.wait_ge(k.m_yd, i - 1)
                nc.gpsimd.tensor_tensor(heads(xdt[:, i % 2, :]), heads(xst[:, i % 2, :]), per_head(k.dt, i),
                                        ALU.mult).then_inc(k.m_xdt, 1)
                if i >= 2:
                    pool.wait_ge(k.m_y2, i - 1)
                nc.gpsimd.tensor_tensor(heads(xD[:, i % 2, :]), heads(xst[:, i % 2, :]),
                                        k.row("dskip", 0, NH).unsqueeze(2).to_broadcast([P, NH, HD]),
                                        ALU.mult).then_inc(k.m_xD, 1)
                pool.wait_ge(k.m_xdt, i + 1)
                pool.wait_ge(k.m_E, i + 1)
                if i >= 2:
                    pool.wait_ge(k.m_S, i - 1 - (i - 1) // TB)
                nc.gpsimd.tensor_tensor(heads(xdd[:, i % 2, :]), heads(xdt[:, i % 2, :]),
                                        Ex[:, :, P - 1:P].to_broadcast([P, NH, HD]), ALU.mult).then_inc(k.m_xdd, 1)

        @block.vector
        def _(dve):
            then = chain(k, dve, "dve")

            def prepare(i):
                dve.wait_ge(k.m_bc, i + 1)
                if i >= 2:
                    dve.wait_ge(k.m_S, i - 1 - (i - 1) // TB)
                nc.vector.tensor_copy(Bt[:, i % 2, :], ps[:, BC, 0:DS]).then_inc(k.m_bcu, 1)
                if i:
                    dve.wait_ge(k.m_M, i)
                nc.vector.tensor_tensor(cbm[:, :], ps[:, BC, P:2 * P], k.const("le"), ALU.mult).then_inc(k.m_bcu, 1)
                dve.wait_ge(k.m_bcu, 2 * i + 2)
                dve.wait_ge(k.m_E, i + 1)
                if i >= 2:
                    dve.wait_ge(k.m_yd, i - 1)
                nc.vector.tensor_tensor(M[:, i % 2, :, :], Ex[:, :, :],
                                        cbm[:, :].unsqueeze(1).to_broadcast([P, NH, P]), ALU.mult).then_inc(k.m_M, 1)

                dve.wait_ge(k.m_tz, i + 1)
                nc.vector.scalar_tensor_tensor(sz[:, i % 2, :], sz[:, i % 2, :], 1.0, ps[:, Z, :], ALU.add,
                                               ALU.mult).then_inc(k.m_sz, 1)

            def combine(i):
                c, yi = i % TB, y[:, :]
                dve.wait_ge(k.m_yd, i + 1)
                dve.wait_ge(k.m_xD, i + 1)
                if i:
                    dve.wait_ge(k.m_yg, i)
                nc.vector.tensor_tensor(yi, ps[:, YD, :], xD[:, i % 2, :], ALU.add).then_inc(k.m_y2, 1)
                dve.wait_ge(k.m_y2, i + 1)
                if c:
                    dve.wait_ge(k.m_yo, off(i))
                    nc.vector.tensor_tensor(heads(yo[:, :]), heads(ps[:, YO, :]), per_head(k.ecs, i),
                                            ALU.mult).then_inc(k.m_y1, 1)
                    dve.wait_ge(k.m_y1, off(i))
                    then(nc.vector.tensor_tensor(yi, yi, yo[:, :], ALU.add))
                if c == 0:
                    dve.wait_ge(k.m_S, i - i // TB + 1)
                    nc.vector.tensor_copy(h[:, :], ps[0:DS, S, :]).then_inc(k.m_h, 1)
                elif c < TB - 1:
                    then(nc.vector.tensor_tensor(heads(hd[:, :]), heads(h[:, :]), per_head(k.etot, i, p=DS),
                                                 ALU.mult))
                    dve.wait_ge(k.m_S, i - i // TB + 1)
                    nc.vector.tensor_tensor(h[:, :], hd[:, :], ps[0:DS, S, :], ALU.add).then_inc(k.m_h, 1)
                dve.wait_ge(k.m_sz, i + 1)
                nc.vector.tensor_tensor(k.yg(i), yi, sz[:, i % 2, :], ALU.mult).then_inc(k.m_yg, 1)

            for f in range(4):
                nc.vector.tensor_scalar(k.wop[:, f, :], k.wop[:, f, :], k.col("normw", f), 0.5, ALU.mult, ALU.mult)
            prepare(0)
            for i in range(NT):
                if i + 1 < NT:
                    prepare(i + 1)
                combine(i)



def outproj_phase(nc, k):
    ps = k.ps
    with ExitStack() as ctx:
        def sb(name, shape, dt=F32):
            return ctx.enter_context(nc.sbuf_tensor(name, shape, dt))

        ygT = sb("ygT", [P, 3, 4, P])
        stats = sb("stats2", [P, NT, 6])
        mv = sb("mv2", [P, NT, 2])
        rstd = sb("rstd2", [P, NT])
        TR, OUT = 0, 4
        block = ctx.enter_context(nc.Block())

        @block.tensor
        def _(pe):
            def turn(i):
                if i >= 4:
                    pe.wait_ge(k.o_evac, i - 3)
                for f in range(4):
                    last = nc.tensor.transpose(ps[:, TR + i % 4, f * P:(f + 1) * P], k.yg(i)[:, f * P:(f + 1) * P],
                                               k.const("ident"))
                last.then_inc(k.o_tr, 1)

            turn(0)
            turn(1)
            for i in range(NT):
                if i + 2 < NT:
                    turn(i + 2)
                pe.wait_ge(k.o_evac, i + 1)
                if i >= 4:
                    pe.wait_ge(k.o_x, i - 3)
                for f in range(4):
                    last = nc.tensor.matmul(ps[:, OUT + i % 4, 0:E], ygT[:, i % 3, f, :], k.wop[:, f, :],
                                            start=(f == 0), stop=(f == 3))
                last.then_inc(k.o_mm, 1)

        @block.scalar
        def _(act):
            for i in range(NT):
                act.wait_ge(k.o_tr, i + 1)
                if i >= 3:
                    act.wait_ge(k.o_mm, i - 2)
                nc.scalar.copy(ygT[:, i % 3, :, :], ps[:, TR + i % 4, :].rearrange("p (f t) -> p f t", f=4)
                               ).then_inc(k.o_evac, 1)
            act.wait_ge(k.o_var, 1)
            nc.scalar.activation(rstd[:, :], mv[:, :, 1], ACT.Sqrt, bias=k.eps[:, 0:1]).then_inc(k.o_sd, 1)

        @block.vector
        def _(dve):
            then = chain(k, dve, "dve")
            then(nc.vector.reciprocal(k.rms[:, :], k.rms[:, :]))
            for i in range(NT):
                dve.wait_ge(k.o_mm, i + 1)
                nc.vector.scalar_tensor_tensor(k.res0[:, i, :], ps[:, OUT + i % 4, 0:E], k.rms[:, i:i + 1],
                                               k.res0[:, i, :], ALU.mult, ALU.add).then_inc(k.o_x, 1)
                dve.wait_ge(k.o_x, i + 1)
                last = nc.vector.bn_stats(stats[:, i, :], k.res0[:, i, :])
            then(last)
            for i in range(NT):
                last = nc.vector.bn_aggr(mv[:, i, :], stats[:, i, :])
            last.then_inc(k.o_var, 1)
            dve.wait_ge(k.o_sd, 1)
            then(nc.vector.reciprocal(rstd[:, :], rstd[:, :]))
            for i in range(NT):
                nc.vector.tensor_scalar(k.hn[:, i, :], k.res0[:, i, :], mv[:, i, 0:1], rstd[:, i:i + 1],
                                        ALU.subtract, ALU.mult)

        @block.gpsimd
        def _(pool):
            for q in range(4):
                pool.wait_ge(k.o_x, 4 * (q + 1))
                r, xs = k.res0[:, 4 * q:4 * q + 4, :], k.X[:, 4 * q:4 * q + 4, 0:E]
                nc.gpsimd.tensor_tensor(xs, xs, r, ALU.add).then_inc(k.o_add, 1)
                pool.wait_ge(k.o_add, q + 1)
                nc.gpsimd.tensor_tensor(xs, xs, k.row("mlpb2", 0, E).unsqueeze(1).to_broadcast([P, 4, E]), ALU.add)


def load_mlp(k):
    def loads(sp):
        sp.dma_start(k.mw1[:, :, :], k.d["mw1"]).then_inc(k.s_mw, 16)
        sp.dma_start(k.mw2[:, :, :], k.d["mw2"]).then_inc(k.s_mw2, 16)
    return loads


def mlp_phase(nc, k):
    ps = k.ps
    with ExitStack() as ctx:
        def parts(name, shape):
            return [ctx.enter_context(nc.sbuf_tensor(name + part, shape, F32R)) for part in "hl"]

        w1, w2 = parts("mw1_", [P, EB, FF]), parts("mw2_", [P, FB, E])
        hTp = parts("mhT_", [P, EB, N])
        hidp = parts("mhid_", [P, FB, W])
        hid = k.hn[:, :, :].rearrange("p i e -> p (i e)").rearrange("p (f t) -> p f t", f=FB)
        block = ctx.enter_context(nc.Block())

        @block.tensor
        def _(pe):
            for w in range(NW):
                tok = slice(w * W, (w + 1) * W)
                pe.wait_ge(k.p_in, w + 1)
                if w == 0:
                    pe.wait_ge(k.p_w, 1)
                for f in range(FB):
                    g = w * FB + f
                    if g >= 4:
                        pe.wait_ge(k.p_act, g - 3)
                    for j in range(EB):
                        last = product3(nc, ps[:, g % 4, :], [x[:, j, f * P:(f + 1) * P] for x in w1],
                                        [x[:, j, tok] for x in hTp], j == 0, j == EB - 1)
                    last.then_inc(k.p_up, 1)
                if w == 0:
                    pe.wait_ge(k.p_w, 2)
                for t in range(4):
                    i = 4 * w + t
                    if i >= 4:
                        pe.wait_ge(k.p_x, i - 3)
                    for f in range(FB):
                        if t == 0:
                            pe.wait_ge(k.p_lo, w * FB + f + 1)
                        last = product3(nc, ps[:, 4 + t, 0:E], [h[:, f, t * P:(t + 1) * P] for h in hidp],
                                        [x[:, f, :] for x in w2], f == 0, f == FB - 1)
                    last.then_inc(k.p_down, 1)

        @block.scalar
        def _(act):
            act.wait_ge(k.s_mw, 16)
            nc.scalar.copy(w1[0][:, :, :], k.mw1[:, :, :]).then_inc(k.p_wh, 1)
            act.wait_ge(k.s_mw2, 16)
            nc.scalar.copy(w2[0][:, :, :], k.mw2[:, :, :]).then_inc(k.p_wh, 1)
            for g in range(NW * FB):
                act.wait_ge(k.p_up, g + 1)
                if g >= FB:
                    act.wait_ge(k.p_lo, g - FB + 1)
                nc.scalar.activation(hid[:, g % FB, :], ps[:, g % 4, :], ACT.Gelu,
                                     bias=k.col("mlpb1", g % FB)).then_inc(k.p_act, 1)

        @block.gpsimd
        def _(pool):
            for n, (parts_, whole) in enumerate(((w1, k.mw1), (w2, k.mw2))):
                pool.wait_ge(k.p_wh, n + 1)
                nc.gpsimd.tensor_tensor(parts_[1][:, :, :], whole[:, :, :], parts_[0][:, :, :],
                                        ALU.subtract).then_inc(k.p_w, 1)

        @block.vector
        def _(dve):
            for w in range(NW):
                x = k.hT[:, :, w * W:(w + 1) * W]
                hi, lo = (p[:, :, w * W:(w + 1) * W] for p in hTp)
                nc.vector.tensor_copy(hi, x).then_inc(k.p_inh, 1)
                dve.wait_ge(k.p_inh, w + 1)
                nc.vector.tensor_tensor(lo, x, hi, ALU.subtract).then_inc(k.p_in, 1)
            for w in range(NW):
                if w:
                    dve.wait_ge(k.p_down, 4 * w)
                for f in range(FB):
                    g = w * FB + f
                    dve.wait_ge(k.p_act, g + 1)
                    nc.vector.tensor_copy(hidp[0][:, f, :], hid[:, f, :]).then_inc(k.p_hi, 1)
                    dve.wait_ge(k.p_hi, g + 1)
                    nc.vector.tensor_tensor(hidp[1][:, f, :], hid[:, f, :], hidp[0][:, f, :],
                                            ALU.subtract).then_inc(k.p_lo, 1)
                for t in range(4):
                    i = 4 * w + t
                    dve.wait_ge(k.p_down, i + 1)
                    nc.vector.tensor_tensor(k.X[:, i, 0:E], k.X[:, i, 0:E], ps[:, 4 + t, 0:E],
                                            ALU.add).then_inc(k.p_x, 1)


def pool_phase(nc, k):
    ps = k.ps
    A, ROW, MISC, UU = 0, 2, 4, 5
    PO = (6, 7, 0, 1)
    with ExitStack() as ctx:
        def sb(name, shape, dt=F32):
            return ctx.enter_context(nc.sbuf_tensor(name, shape, dt))

        aT = sb("aT", [HID, N])
        vb = sb("vb", [HID, P])
        srow = sb("srow", [P, N])
        srev = sb("srev", [P, T])
        scol = sb("scol", [P, NT])
        pm = sb("pm", [P, T + 1])
        sm = sb("sm", [P, T + 1])
        negm = sb("negm", [P, T])
        D = sb("D", [P, B, TB, P])
        it = sb("it", [P, B], I32)
        fl = sb("fl", [P, 2, 3, B])
        pen = sb("pen", [P, P])
        pbl = sb("pbl", [8, 8])
        mx = sb("mx", [P, TB])
        mxd = sb("mxd", [8, TB])
        mxc = sb("mxc", [8, B])
        e8 = sb("e8", [P, B, TB, 8])
        ex = sb("ex", [P, B, TB])
        wt = sb("wt", [8, B, TB, P])
        U = sb("U", [8, B, E + 1])
        cnt = sb("cnt", [P, NT])
        den = sb("den", [P, NT])
        pool_rows = k.pooled
        block = ctx.enter_context(nc.Block())

        @block.sync
        def _(sp):
            sp.dma_start(it[:, :], k.d["itok0"].partition_broadcast(P)).then_inc(k.s_it, 16)

        @block.tensor
        def _(pe):
            for w in range(NW):
                if w >= 2:
                    pe.wait_ge(k.q_tanh, w - 1)
                for j in range(EB):
                    last = nc.tensor.matmul(ps[0:HID, A + w % 2, :], k.c2w[:, j, :], k.hT[:, j, w * W:(w + 1) * W],
                                            start=(j == 0), stop=(j == EB - 1))
                last.then_inc(k.q_a, 1)
            pe.wait_ge(k.q_vb, 1)
            for w in range(NW):
                pe.wait_ge(k.q_tanh, w + 1)
                if w >= 2:
                    pe.wait_ge(k.q_srow, w - 1)
                nc.tensor.matmul(ps[:, ROW + w % 2, :], vb[:, :], aT[:, w * W:(w + 1) * W], start=True,
                                 stop=True).then_inc(k.q_row, 1)
            for i in range(NT):
                last = nc.tensor.matmul(ps[:, MISC, i:i + 1], aT[:, i * P:(i + 1) * P], k.col("c2v", 0)[0:HID],
                                        start=(i == 0), stop=True, skip_group_check=True)
            last.then_inc(k.q_col, 1)
            for b in range(B):
                pe.wait_ge(k.q_e8, b + 1)
                if b:
                    pe.wait_ge(k.q_U, b)
                for c in range(TB):
                    last = nc.tensor.matmul(ps[0:8, UU, 0:E + 1], e8[:, b, c, :], k.X[:, b * TB + c, :],
                                            start=(c == 0), stop=(c == TB - 1))
                last.then_inc(k.q_sum, 1)
            for b in range(B):
                pe.wait_ge(k.q_U, b + 1)
                pe.wait_ge(k.q_D, b + 1)
                for c in range(TB):
                    i = b * TB + c
                    if i >= 4:
                        pe.wait_ge(k.q_out, i - 3)
                    nc.tensor.matmul(ps[:, PO[i % 4], 0:E + 1], D[:, b, c, :], k.X[:, i, :], start=True, stop=False)
                    nc.tensor.matmul(ps[:, PO[i % 4], 0:E + 1], wt[:, b, c, :], U[:, b, :], start=False,
                                     stop=True).then_inc(k.q_pool, 1)

        @block.scalar
        def _(act):
            then = chain(k, act, "act")
            for w in range(NW):
                act.wait_ge(k.q_a, w + 1)
                nc.scalar.activation(aT[:, w * W:(w + 1) * W], ps[0:HID, A + w % 2, :], ACT.Tanh,
                                     bias=k.col("c2b1", 0)[0:HID]).then_inc(k.q_tanh, 1)
            for w in range(NW):
                act.wait_ge(k.q_row, w + 1)
                nc.scalar.copy(srow[:, w * W:(w + 1) * W], ps[:, ROW + w % 2, :]).then_inc(k.q_srow, 1)
            for b in range(B):
                act.wait_ge(k.q_ex, b + 1)
                nc.scalar.activation(ex[:, b, :], ex[:, b, :], ACT.Exp).then_inc(k.q_exp, 1)
                act.wait_ge(k.q_dex, b + 1)
                for c in range(TB):
                    last = nc.scalar.activation(D[:, b, c, :], D[:, b, c, :], ACT.Exp,
                                                bias=scol[:, b * TB + c:b * TB + c + 1])
                nc.scalar.activation(wt[:, b, :, :], wt[:, b, :, :], ACT.Exp, bias=mxc[:, b:b + 1]).then_inc(k.q_D, 1)

        @block.vector
        def _(dve):
            then = chain(k, dve, "dve")
            nc.vector.tensor_scalar(vb[:, :], k.const("ones")[0:HID], k.col("c2v", 0)[0:HID], None,
                                    ALU.mult).then_inc(k.q_vb, 1)
            dve.wait_ge(k.s_it, 16)
            then(nc.vector.tensor_copy(cnt[:, 0:B], it[:, :]))
            then(nc.vector.tensor_scalar(fl[:, 0, 0, :], cnt[:, 0:B], 0.0, None, ALU.is_equal))
            then(nc.vector.tensor_scalar(fl[:, 0, 1, :], cnt[:, 0:B], 1.0, None, ALU.is_equal))
            then(nc.vector.tensor_tensor(fl[:, 0, 2, :], fl[:, 0, 0, :], fl[:, 0, 1, :], ALU.add))
            then(nc.vector.tensor_scalar(fl[:, 0, 2, :], fl[:, 0, 2, :], -1.0, 1.0, ALU.mult, ALU.add))
            then(nc.vector.tensor_scalar(fl[:, 1, :, :], fl[:, 0, :, :], -1.0, None, ALU.mult))

            def blend(out, pieces, b, sign=0, p=P):
                f = lambda q: fl[0:p, sign, q, b:b + 1]
                then(nc.vector.tensor_scalar(out, pieces[0], f(0), None, ALU.mult))
                for q in (1, 2):
                    then(nc.vector.scalar_tensor_tensor(out, pieces[q], f(q), out, ALU.mult, ALU.add))

            then(nc.vector.memset(pm[:, 0:1], NEG))
            then(nc.vector.memset(sm[:, T:T + 1], NEG))
            dve.wait_ge(k.q_col, 1)
            then(nc.vector.tensor_copy(scol[:, :], ps[:, MISC, 0:NT]))
            for b in range(B):
                dve.wait_ge(k.q_srow, 2 * (b + 1))
                s = srow[:, b * T:(b + 1) * T]
                then(nc.vector.tensor_reduce(mx[:, :], s.rearrange("p (c t) -> p c t", c=TB), AX.X, ALU.max))
                nc.vector.tensor_tensor(ex[:, b, :], scol[:, b * TB:(b + 1) * TB], mx[:, :],
                                        ALU.subtract).then_inc(k.q_ex, 1)
                then(nc.vector.tensor_tensor(mxd[:, :], mx[0:8, :], k.const("ident", 0, 8)[0:8], ALU.mult))
                then(nc.vector.tensor_reduce(mxc[:, b:b + 1], mxd[:, :], AX.X, ALU.add))
                dve.wait_ge(k.q_exp, b + 1)
                nc.vector.tensor_tensor(e8[:, b, :, :], k.const("delta8", 0, 64).rearrange("p (c q) -> p c q", c=8),
                                        ex[:, b, :].unsqueeze(2).to_broadcast([P, TB, 8]), ALU.mult).then_inc(k.q_e8, 1)
                then(nc.vector.tensor_tensor_scan(pm[:, 1:T + 1], s, s, NEG, ALU.max, ALU.max))
                rev = srow[:, b * T:(b + 1) * T][:, ::-1]
                then(nc.vector.tensor_tensor_scan(sm[:, 0:T][:, ::-1], rev, rev, NEG, ALU.max, ALU.max))
                then(nc.vector.tensor_tensor(srev[:, :], pm[:, 0:T], sm[:, 1:T + 1], ALU.max))
                blend(negm[:, :], (pm[:, 1:T + 1], sm[:, 0:T], srev[:, :]), b, sign=1)
                blend(pen[:, :], (k.const("penp"), k.const("pens"), k.const("penc")), b)
                pb = k.const("penb", 0, 24)[0:8].rearrange("p (q c) -> p q c", q=3)
                blend(pbl[:, :], (pb[:, 0, :], pb[:, 1, :], pb[:, 2, :]), b, p=8)
                rows = negm[:, :].rearrange("p (c t) -> p c t", c=TB)
                then(nc.vector.tensor_tensor(D[:, b, :, :], rows, pen[:, :].unsqueeze(1).to_broadcast([P, TB, P]),
                                             ALU.add))
                nc.vector.tensor_tensor(wt[:, b, :, :], rows[0:8], pbl[:, :].unsqueeze(2).to_broadcast([8, TB, P]),
                                        ALU.add).then_inc(k.q_dex, 1)
                cb = cnt[:, b * TB:(b + 1) * TB]
                then(nc.vector.tensor_scalar(srev[:, 0:TB], k.const("cntp", 0, TB), -1.0, T + 1.0, ALU.mult, ALU.add))
                then(nc.vector.tensor_scalar(srev[:, TB:2 * TB], k.const("cntp", 0, TB), 0.0, T - 1.0, ALU.mult,
                                             ALU.add))
                blend(cb, (k.const("cntp", 0, TB), srev[:, 0:TB], srev[:, TB:2 * TB]), b)
                dve.wait_ge(k.q_sum, b + 1)
                nc.vector.tensor_copy(U[:, b, :], ps[0:8, UU, 0:E + 1]).then_inc(k.q_U, 1)
            for i in range(NT):
                dve.wait_ge(k.q_pool, i + 1)
                then(nc.vector.tensor_tensor(den[:, i:i + 1], ps[:, PO[i % 4], E:E + 1], cnt[:, i:i + 1], ALU.mult))
                then(nc.vector.reciprocal(den[:, i:i + 1], den[:, i:i + 1]))
                nc.vector.tensor_scalar(pool_rows[:, i, :], ps[:, PO[i % 4], 0:E], den[:, i:i + 1], None,
                                        ALU.mult).then_inc(k.q_out, 1)


JT = dict(sel=0, n=17, base=33, free=49, pairs=66, blk=82)
JOB = 256
NB = N // JOB


def route_phase(nc, k):
    ps = k.ps
    KK, LG, TR, CNT, BO = 0, 1, 2, 6, 7
    with ExitStack() as ctx:
        def sb(name, shape, dt=F32):
            return ctx.enter_context(nc.sbuf_tensor(name, shape, dt))

        k2 = sb("k2", [P, EB, E0])
        G = sb("Gr", [P, EB, E0])
        rb = sb("rbk", [P, E0])
        lg = sb("lg", [P, NT, E0])
        v8 = sb("v8", [P, NT, 8])
        i8 = sb("i8", [P, NT, 8], U32)
        fi = sb("fi", [P, NT, 8])
        w4 = sb("w4", [P, NT, TOPK])
        den = sb("den4", [P, NT])
        oh = sb("oh", [P, NT, E0])
        wd = sb("wd", [P, NT, E0])
        a = sb("act", [1, E0, NB])
        rk = sb("rk", [1, E0, NB])
        nj = sb("nj", [1, 6, E0])
        big = sb("big", [1, E0 * NB * NB])
        lst = sb("lst", [1, E0, NB])
        perm = sb("perm", [1, E0, E0])
        jf = sb("jf", [1, JT["blk"] + E0 * NB])
        block = ctx.enter_context(nc.Block())

        @block.tensor
        def _(pe):
            pe.wait_ge(k.r_k2, 1)
            for j in range(EB):
                last = nc.tensor.matmul(ps[:, KK, 0:E0], k.const("ones"), k2[:, j, :], start=(j == 0),
                                        stop=(j == EB - 1))
            last.then_inc(k.r_kk, 1)
            pe.wait_ge(k.r_G, 1)
            for i in range(NT):
                for j in range(EB):
                    last = nc.tensor.matmul(ps[:, LG, i * E0:(i + 1) * E0], k.hT[:, j, i * P:(i + 1) * P], G[:, j, :],
                                            start=(i == 0 and j == 0), stop=(j == EB - 1), skip_group_check=True)
            last.then_inc(k.r_lg, 1)
            pe.wait_ge(k.r_wd, 1)
            nc.tensor.matmul(ps[:, CNT, 0:NT * E0], k.const("ones"), k.wE[:, :, :].rearrange("p e i -> p (e i)"),
                             start=True, stop=True).then_inc(k.r_cnt, 1)
            for g in range(NW):
                for t in range(4):
                    last = nc.tensor.transpose(ps[0:E0, TR + g, t * P:(t + 1) * P], wd[:, 4 * g + t, :],
                                               k.const("ident"))
                last.then_inc(k.r_tr, 1)

        @block.scalar
        def _(act):
            act.wait_ge(k.r_v, 1)
            nc.scalar.activation(w4[:, :, :], w4[:, :, :], ACT.Exp).then_inc(k.r_exp, 1)
            for g in range(NW):
                act.wait_ge(k.r_tr, g + 1)
                nc.scalar.copy(k.wT[:, g * W:(g + 1) * W], ps[0:E0, TR + g, :]).then_inc(k.r_wT, 1)

        @block.sync
        def _(sp):
            sp.wait_ge(k.r_sel, 1)
            load_first_mixture(sp, k, 0, 0)

        @block.gpsimd
        def _(pool):
            for j in range(EB):
                nc.gpsimd.tensor_copy(k.hTh[:, j, :], k.hT[:, j, :]).then_inc(k.r_hi, 1)
            pool.wait_ge(k.r_lg, 1)
            for j in range(EB):
                pool.wait_ge(k.r_hi, j + 1)
                nc.gpsimd.tensor_tensor(k.hTl[:, j, :], k.hT[:, j, :], k.hTh[:, j, :], ALU.subtract)

        @block.vector
        def _(dve):
            then = chain(k, dve, "dve")
            nc.vector.tensor_tensor(k2[:, :, :], k.keysT[:, :, :], k.keysT[:, :, :], ALU.mult).then_inc(k.r_k2, 1)
            nc.vector.scalar_tensor_tensor(G[:, :, :], k.keysT[:, :, :], 2.0, k.rwT[:, :, :], ALU.mult,
                                           ALU.add).then_inc(k.r_G, 1)
            dve.wait_ge(k.r_kk, 1)
            then(nc.vector.tensor_tensor(rb[:, :], k.row("rb", 0, E0), ps[:, KK, 0:E0], ALU.subtract))
            dve.wait_ge(k.r_lg, 1)
            then(nc.vector.tensor_tensor(lg[:, :, :], ps[:, LG, 0:NT * E0].rearrange("p (i e) -> p i e", e=E0),
                                         rb[:, :].unsqueeze(1).to_broadcast([P, NT, E0]), ALU.add))
            for i in range(NT):
                last = nc.vector.max(v8[:, i, :], lg[:, i, :])
            then(last)
            for i in range(NT):
                last = nc.vector.max_index(i8[:, i, :], v8[:, i, :], lg[:, i, :])
            nc.vector.tensor_tensor(w4[:, :, :], v8[:, :, 0:TOPK], v8[:, :, 0:1].to_broadcast([P, NT, TOPK]),
                                    ALU.subtract).then_inc(k.r_v, 1)
            then(last)
            then(nc.vector.tensor_copy(fi[:, :, :], i8[:, :, :]))
            dve.wait_ge(k.r_exp, 1)
            then(nc.vector.tensor_reduce(den[:, :], w4[:, :, :], AX.X, ALU.add))
            then(nc.vector.reciprocal(den[:, :], den[:, :]))
            then(nc.vector.tensor_tensor(w4[:, :, :], w4[:, :, :], den[:, :].unsqueeze(2).to_broadcast([P, NT, TOPK]),
                                         ALU.mult))
            then(nc.vector.memset(wd[:, :, :], 0.0))
            for q in range(TOPK):
                wide = lambda ap: ap.to_broadcast([P, NT, E0])
                then(nc.vector.tensor_tensor(oh[:, :, :], k.const("iota", 0, E0).unsqueeze(1).to_broadcast([P, NT, E0]),
                                             wide(fi[:, :, q:q + 1]), ALU.is_equal))
                then(nc.vector.tensor_tensor(oh[:, :, :], oh[:, :, :], wide(w4[:, :, q:q + 1]), ALU.mult))
                then(nc.vector.tensor_tensor(wd[:, :, :], wd[:, :, :], oh[:, :, :], ALU.add))
            nc.vector.tensor_copy(k.wE[:, :, :], wd[:, :, :].rearrange("p i e -> p e i")).then_inc(k.r_wd, 1)
            dve.wait_ge(k.r_cnt, 1)
            sums = ps[0:1, CNT, 0:NT * E0].rearrange("p (e b t) -> p e b t", e=E0, b=NB)
            then(nc.vector.tensor_reduce(a[:, :, :], sums, AX.X, ALU.add))
            then(nc.vector.tensor_scalar(a[:, :, :], a[:, :, :], 0.0, None, ALU.is_gt))
            then(nc.vector.tensor_reduce(nj[:, 0, :], a[:, :, :], AX.X, ALU.add))
            iota = k.const("iota", 0, E0)[0:1]
            then(nc.vector.tensor_scalar(nj[:, 1, :], nj[:, 0, :], 0.0, None, ALU.is_gt))
            then(nc.vector.memset(nj[:, 5, :], 0.0))
            then(nc.vector.tensor_tensor_scan(nj[:, 2, :], nj[:, 1, :], nj[:, 5, :], 0.0, ALU.add, ALU.add))
            then(nc.vector.tensor_tensor(nj[:, 3, :], iota, nj[:, 2, :], ALU.subtract))
            then(nc.vector.tensor_scalar(nj[:, 3, :], nj[:, 3, :], nj[:, 2, E0 - 1:E0], None, ALU.add))
            then(nc.vector.scalar_tensor_tensor(nj[:, 2, :], nj[:, 2, :], 1.0, nj[:, 3, :], ALU.subtract, ALU.subtract))
            then(nc.vector.tensor_tensor(nj[:, 2, :], nj[:, 2, :], nj[:, 1, :], ALU.mult))
            then(nc.vector.tensor_tensor(nj[:, 2, :], nj[:, 2, :], nj[:, 3, :], ALU.add))
            pm = perm[:, :, :]
            then(nc.vector.tensor_tensor(pm, nj[:, 2:3, :].to_broadcast([1, E0, E0]),
                                         iota.unsqueeze(2).to_broadcast([1, E0, E0]), ALU.is_equal))
            pick = big[:, 0:E0 * E0].rearrange("p (s e) -> p s e", e=E0)

            def permute(out, values):
                then(nc.vector.tensor_tensor(pick, pm, values.to_broadcast([1, E0, E0]), ALU.mult))
                then(nc.vector.tensor_reduce(out, pick, AX.X, ALU.add))

            permute(jf[:, JT["sel"]:JT["sel"] + E0], iota.unsqueeze(1))
            then(nc.vector.memset(jf[:, JT["sel"] + E0:JT["n"]], 0.0))
            nc.vector.tensor_copy(k.jobs[:, 0:JT["n"]], jf[:, 0:JT["n"]]).then_inc(k.r_sel, 1)
            permute(jf[:, JT["n"]:JT["n"] + E0], nj[:, 0:1, :])
            then(nc.vector.memset(rk[:, :, 0:1], 0.0))
            for q in range(1, NB):
                then(nc.vector.tensor_tensor(rk[:, :, q:q + 1], rk[:, :, q - 1:q], a[:, :, q - 1:q], ALU.add))
            eq = big[:, 0:E0 * NB * NB].rearrange("p (e r b) -> p e r b", e=E0, r=NB)
            then(nc.vector.tensor_tensor(a[:, :, :], a[:, :, :], iota[:, 0:NB].unsqueeze(1).to_broadcast([1, E0, NB]),
                                         ALU.mult))
            for e in range(E0):
                then(nc.vector.tensor_tensor(eq[:, e], rk[:, e:e + 1, :].to_broadcast([1, NB, NB]),
                                             iota[:, 0:NB].unsqueeze(2).to_broadcast([1, NB, NB]), ALU.is_equal))
                then(nc.vector.tensor_tensor(eq[:, e], eq[:, e], a[:, e:e + 1, :].to_broadcast([1, NB, NB]), ALU.mult))
            then(nc.vector.tensor_reduce(lst[:, :, :], eq, AX.X, ALU.add))
            for q in range(NB):
                permute(jf[:, JT["blk"] + q:JT["blk"] + E0 * NB:NB], lst[:, :, q].unsqueeze(1))
            jn, jb = jf[:, JT["n"]:JT["n"] + E0], jf[:, JT["base"]:JT["base"] + E0]
            then(nc.vector.tensor_scalar(nj[:, 3, 0:E0 // 2], jf[:, JT["n"]:JT["n"] + E0:2], 0.0, None, ALU.is_gt))
            then(nc.vector.memset(jf[:, JT["pairs"]:JT["blk"]], 0.0))
            then(nc.vector.tensor_reduce(jf[:, JT["pairs"]:JT["pairs"] + 1], nj[:, 3, 0:E0 // 2], AX.X, ALU.add))
            then(nc.vector.tensor_scalar(jf[:, JT["pairs"]:JT["pairs"] + 1], jf[:, JT["pairs"]:JT["pairs"] + 1], 1.0, None,
                                         ALU.max))
            then(nc.vector.tensor_scalar(jn, jn, 1.0, None, ALU.max))
            then(nc.vector.tensor_tensor_scan(jb, jn, nj[:, 5, :], 0.0, ALU.add, ALU.add))
            then(nc.vector.tensor_tensor(jb, jb, jn, ALU.subtract))
            then(nc.vector.memset(jf[:, JT["free"]:JT["free"] + 2], 0.0))
            then(nc.vector.tensor_copy(jf[:, JT["free"] + 2:JT["free"] + E0 + 1], jf[:, JT["base"] + 1:JT["base"] + E0]))
            nc.vector.tensor_copy(k.jobs[:, JT["n"]:], jf[:, JT["n"]:])

def product3(nc, out, lhs, rhs, start, stop, **kw):
    for n, (a, b) in enumerate(((0, 0), (0, 1), (1, 0))):
        last = nc.tensor.matmul(out, lhs[a], rhs[b], start=(start and n == 0), stop=(stop and n == 2), **kw)
    return last


def job_entry(eng, k, name, at, limit):
    return eng.value_load(k.jobs[0:1, bass.ds(at + JT[name], 1)], min_val=0, max_val=limit)


def load_first_mixture(sp, k, s, q):
    e = job_entry(sp, k, "sel", s, E0 - 1)
    sp.dma_start(k.w1s[q][:, :, :], k.d["ew1"][bass.ds(e, 1)].squeeze(0)).then_inc(k.s_e[q], 16)
    sp.dma_start(k.w2s[q][:, :, :], k.d["ew2"][bass.ds(e, 1)].squeeze(0)).then_inc(k.s_e[q], 16)
    sp.dma_start(k.b1s[q][:, :], k.d["eb1"][bass.ds(e, 1)].squeeze(0)).then_inc(k.s_e[q], 16)


def experts_phase(nc, k):
    ps = k.ps
    with ExitStack() as ctx:
        def sb(name, shape, dt=F32):
            return ctx.enter_context(nc.sbuf_tensor(name, shape, dt))

        w1s, w2s, b1s = k.w1s, k.w2s, k.b1s
        w1 = [[sb(f"ew1_{q}{part}", [P, EB, FF], F32R) for part in "hl"] for q in range(2)]
        w2 = [[sb(f"ew2_{q}{part}", [P, FB, E], F32R) for part in "hl"] for q in range(2)]
        b1 = [sb(f"eb1_{q}", [P, FB]) for q in range(2)]
        assert FB * JOB == N
        hid = k.hT[:, 0, :].rearrange("p (f t) -> p f t", f=FB)
        hidp = [sb(f"ehid{part}", [P, FB, JOB], F32R) for part in "hl"]
        DOWN, BO, TILES = 4, 6, JOB // P
        PAIRS = FB // 2
        block = ctx.enter_context(nc.Block())

        def entry(eng, name, at, limit):
            return job_entry(eng, k, name, at, limit)

        def following(p, q):
            return (p * 2 + 1, 1, p + 1) if q == 0 else (p * 2 + 2, 0, p + 2)

        def jobs(eng, each, prepare, begin=None):
            pairs = entry(eng, "pairs", 0, E0 // 2)
            if prepare:
                prepare(0, 0, 1)
            if begin:
                begin()
            with eng.Fori(0, pairs) as p:
                for q in range(2):
                    n = entry(eng, "n", p * 2 + q, NB)
                    base = entry(eng, "base", p * 2 + q, E0 * NB)
                    sel = entry(eng, "sel", p * 2 + q, E0 - 1)
                    if prepare:
                        prepare(*following(p, q))
                    with eng.Fori(0, n) as j:
                        blk = entry(eng, "blk", p * (2 * NB) + q * NB + j, NB - 1)
                        each(base + j, q, blk, p, sel)

        @block.sync
        def _(sp):
            pairs = entry(sp, "pairs", 0, E0 // 2)
            with sp.Fori(0, pairs) as p:
                for q in range(2):
                    s, parity, loads = following(p, q)
                    sp.wait_ge(k.e_split, s * 3 + 3)
                    load_first_mixture(sp, k, s, parity)

        @block.gpsimd
        def _(pool):
            pool.sem_inc(k.e_split, 6)

            def low_parts(s, q, loads):
                pool.wait_ge(k.e_h1, s + 1)
                nc.gpsimd.tensor_tensor(w1[q][1][:, :, :], w1s[q][:, :, :], w1[q][0][:, :, :],
                                        ALU.subtract).then_inc(k.e_split, 1)
                pool.wait_ge(k.e_h2, s + 1)
                nc.gpsimd.tensor_tensor(w2[q][1][:, :, :], w2s[q][:, :, :], w2[q][0][:, :, :],
                                        ALU.subtract).then_inc(k.e_split, 1)
                nc.gpsimd.tensor_copy(b1[q][:, :], b1s[q][:, :]).then_inc(k.e_split, 1)

            pairs = entry(pool, "pairs", 0, E0 // 2)
            low_parts(0, 0, 1)
            with pool.Fori(0, pairs) as p:
                for q in range(2):
                    low_parts(*following(p, q))

        @block.tensor
        def _(pe):
            pe.sem_inc(k.e_down, TILES)

            def job(n, q, blk, p, sel):
                pe.wait_ge(k.e_split, p * 6 + (3 * q + 9))
                tok = bass.ds(blk * JOB, JOB)
                for f in range(FB):
                    if f % 2 == 0:
                        pe.wait_ge(k.e_act, n * FB + (f + 2))
                    for j in range(EB):
                        last = product3(nc, ps[:, f // 2, (f % 2) * JOB:(f % 2 + 1) * JOB],
                                        [w[:, j, f * P:(f + 1) * P] for w in w1[q]],
                                        [k.hTh[:, j, tok], k.hTl[:, j, tok]], f % 2 == 0 and j == 0, j == EB - 1,
                                        skip_group_check=True)
                    if f % 2:
                        last.then_inc(k.e_up, 1)
                for t in range(TILES):
                    pe.wait_ge(k.e_y, n * TILES + (t + 1))
                    for f in range(FB):
                        if t == 0 and f % 2 == 0:
                            pe.wait_ge(k.e_lo, n * PAIRS + (PAIRS + f // 2 + 1))
                        last = product3(nc, ps[:, DOWN + t, 0:E], [h[:, f, t * P:(t + 1) * P] for h in hidp],
                                        [w[:, f, :] for w in w2[q]], f == 0, f == FB - 1)
                    last.then_inc(k.e_down, 1)

            for i in range(NT):
                if i >= 2:
                    pe.wait_ge(k.r_b2, i - 1)
                nc.tensor.matmul(ps[:, BO + i % 2, 0:E], k.wT[:, i * P:(i + 1) * P], k.b2a[:, :], start=True,
                                 stop=True).then_inc(k.r_bo, 1)
            jobs(pe, job, None)

        @block.scalar
        def _(act):
            act.sem_inc(k.e_act, FB)

            def high_parts(s, q, loads):
                free = entry(act, "free", s, E0 * NB)
                act.wait_ge(k.e_y, free * TILES + TILES)
                act.wait_ge(k.s_e[q], loads * 48)
                nc.scalar.copy(w1[q][0][:, :, :], w1s[q][:, :, :]).then_inc(k.e_h1, 1)

            def job(n, q, blk, p, sel):
                act.wait_ge(k.e_split, p * 6 + (3 * q + 9))
                for f in range(FB):
                    if f % 2 == 0:
                        act.wait_ge(k.e_up, n * PAIRS + (f // 2 + 1))
                        act.wait_ge(k.e_lo, n * PAIRS + (f // 2 + 1))
                    nc.scalar.activation(hid[:, f, :], ps[:, f // 2, (f % 2) * JOB:(f % 2 + 1) * JOB], ACT.Gelu,
                                         bias=b1[q][:, f:f + 1]).then_inc(k.e_act, 1)

            jobs(act, job, high_parts)

        @block.vector
        def _(dve):
            dve.sem_inc(k.e_y, TILES)
            dve.sem_inc(k.e_lo, PAIRS)
            X2 = k.X[:, :, :].rearrange("p i e -> p (i e)")
            wE2 = k.wE[:, :, :].rearrange("p e i -> p (e i)")
            hi, lo = hidp

            def high_parts(s, q, loads):
                free = entry(dve, "free", s, E0 * NB)
                dve.wait_ge(k.e_y, free * TILES + TILES)
                dve.wait_ge(k.s_e[q], loads * 48)
                nc.vector.tensor_copy(w2[q][0][:, :, :], w2s[q][:, :, :]).then_inc(k.e_h2, 1)

            def job(n, q, blk, p, e):
                dve.wait_ge(k.e_down, n * TILES + TILES)
                for g in range(PAIRS):
                    f = slice(2 * g, 2 * g + 2)
                    dve.wait_ge(k.e_act, n * FB + (FB + 2 * g + 2))
                    nc.vector.tensor_copy(hi[:, f, :], hid[:, f, :]).then_inc(k.e_dhi, 1)
                    dve.wait_ge(k.e_dhi, n * PAIRS + (g + 1))
                    nc.vector.tensor_tensor(lo[:, f, :], hid[:, f, :], hi[:, f, :], ALU.subtract).then_inc(k.e_lo, 1)
                for t in range(TILES):
                    dve.wait_ge(k.e_down, n * TILES + (TILES + t + 1))
                    dve.wait_ge(k.e_y, n * TILES + (TILES + t))
                    x = X2[:, bass.ds(blk * (TILES * (E + 1)) + t * (E + 1), E)]
                    nc.vector.scalar_tensor_tensor(x, ps[:, DOWN + t, 0:E], wE2[:, bass.ds(e * NT + blk * TILES + t, 1)],
                                                   x, ALU.mult, ALU.add).then_inc(k.e_y, 1)

            def second_biases():
                for i in range(NT):
                    dve.wait_ge(k.r_bo, i + 1)
                    nc.vector.tensor_tensor(k.X[:, i, 0:E], k.X[:, i, 0:E], ps[:, BO + i % 2, 0:E],
                                            ALU.add).then_inc(k.r_b2, 1)
                dve.wait_ge(k.r_b2, NT)

            jobs(dve, job, high_parts, second_biases)


def laplace_phase(nc, k):
    ps = k.ps
    with ExitStack() as ctx:
        def sb(name, shape, dt=F32):
            return ctx.enter_context(nc.sbuf_tensor(name, shape, dt))

        nb = sb("nb", [P, EB, N])
        du = k.att[:, :, :].rearrange("p i e -> p (i e)").rearrange("p (f n) -> p f n", f=EB)
        z = sb("zc", [P, 2, B])
        block = ctx.enter_context(nc.Block())
        LAP, Q, K, V = 0, 8, 16, 24

        @block.sync
        def _(sp):
            for dst, src in ((k.wq, k.d["wq"]), (k.wk, k.d["wk"]), (k.wv, k.d["wv"]), (k.wo, k.d["wo"])):
                sp.dma_start(dst[:, :, :], src).then_inc(k.s_wC, 16)

        @block.tensor
        def _(pe):
            for w in range(NW):
                for f in range(EB):
                    for j in range(EB):
                        last = nc.tensor.matmul(ps[:, EB * w + f, :],
                                                k.const("lap", j * E + f * P, P), k.hT[:, j, w * W:(w + 1) * W],
                                                start=(j == 0), stop=(j == EB - 1))
                    last.then_inc(k.l_mm, 1)
            pe.wait_ge(k.s_wC, 64)
            for w in range(NW):
                for g, wt in ((Q, k.wq), (K, k.wk)):
                    for f in range(EB):
                        n = g + EB * w + f
                        if g == Q:
                            pe.wait_ge(k.l_du, EB * w + EB)
                        else:
                            pe.wait_ge(k.l_q, EB * w + f + 1)
                        for j in range(EB):
                            last = nc.tensor.matmul(ps[:, n % 8, :], wt[:, j, f * P:(f + 1) * P],
                                                    du[:, j, w * W:(w + 1) * W], start=(j == 0), stop=(j == EB - 1))
                        last.then_inc(k.l_qk, 1)
            for i in range(NT):
                pe.wait_ge(k.l_k, 8) if i == 0 else None
                if i >= 8:
                    pe.wait_ge(k.l_v, i - 7)
                for j in range(EB):
                    last = nc.tensor.matmul(ps[:, i % 8, 0:E], du[:, j, i * P:(i + 1) * P], k.wv[:, j, :],
                                            start=(j == 0), stop=(j == EB - 1))
                last.then_inc(k.l_vm, 1)

        @block.scalar
        def _(act):
            for w in range(NW):
                for f in range(EB):
                    act.wait_ge(k.l_qk, 4 * w + f + 1)
                    if f == 0:
                        act.wait_ge(k.l_zero, w + 1)
                    for s in range(4):
                        r = slice(32 * s, 32 * s + 32)
                        last = nc.scalar.activation(k.qT[r, 4 * f + s, w * W:(w + 1) * W],
                                                    ps[r, (Q + EB * w + f) % 8, :], ACT.Copy, scale=32.0 ** -0.5)
                    last.then_inc(k.l_q, 1)
                for f in range(EB):
                    act.wait_ge(k.l_qk, 4 * w + EB + f + 1)
                    nc.scalar.copy(k.kT[:, f, w * W:(w + 1) * W], ps[:, (K + EB * w + f) % 8, :]).then_inc(k.l_k, 1)

        @block.gpsimd
        def _(pool):
            for b in range(B):
                y = k.hT[:, :, b * T:(b + 1) * T]
                s = nb[:, :, b * T:(b + 1) * T]
                nc.gpsimd.tensor_tensor(s[:, :, 1:T - 1], y[:, :, 0:T - 2], y[:, :, 2:T], ALU.add).then_inc(k.l_nb, 1)
                for at, of in ((0, 1), (T - 1, T - 2)):
                    nc.gpsimd.tensor_tensor(s[:, :, at:at + 1], y[:, :, of:of + 1], y[:, :, of:of + 1],
                                            ALU.add).then_inc(k.l_nb, 1)
                for w in (2 * b, 2 * b + 1):
                    nc.gpsimd.memset(k.qT[:, :, w * W:(w + 1) * W], 0.0).then_inc(k.l_zero, 1)

        @block.vector
        def _(dve):
            then = chain(k, dve, "dve")
            then(nc.vector.tensor_scalar(z[:, 0, :], k.row("zr", 0, B), -1.0, None, ALU.mult))
            then(nc.vector.scalar_tensor_tensor(z[:, 1, :], k.row("zy", 0, B), -2.0, k.row("zr", 0, B), ALU.mult,
                                                ALU.add))
            for w in range(NW):
                b, tok = w // 2, slice(w * W, (w + 1) * W)
                for f in range(EB):
                    y, o = k.hT[:, f, tok], du[:, f, tok]
                    then(nc.vector.tensor_scalar(o, y, z[:, 0, b:b + 1], z[:, 1, b:b + 1], ALU.mult, ALU.add))
                    then(nc.vector.tensor_tensor(o, o, y, ALU.mult))
                    dve.wait_ge(k.l_nb, 3 * (b + 1))
                    then(nc.vector.scalar_tensor_tensor(o, nb[:, f, tok], k.row("zy", b), o, ALU.mult, ALU.add))
                    dve.wait_ge(k.l_mm, EB * w + f + 1)
                    nc.vector.scalar_tensor_tensor(o, ps[:, EB * w + f, :], k.row("zx", b), o, ALU.mult,
                                                   ALU.add).then_inc(k.l_du, 1)
            for i in range(NT):
                dve.wait_ge(k.l_vm, i + 1)
                nc.vector.tensor_copy(k.v[:, i, :], ps[:, i % 8, 0:E]).then_inc(k.l_v, 1)


HEADS = 4
UNITS = NT * HEADS


def attention_phase(nc, k):
    ps = k.ps
    TR, PV = 4, 6
    with ExitStack() as ctx:
        def sb(name, shape, dt=F32):
            return ctx.enter_context(nc.sbuf_tensor(name, shape, dt))

        pr = sb("pr", [P, 3, 2, T])
        dT = k.hT[:, :, 0:T].rearrange("p q (j t) -> p q j t", t=P)
        nmax = sb("nmax", [P, 2, 2])
        sums = sb("sums", [P, 2, NT * HEADS])
        rr = sb("rr", [P, 2])
        rc = sb("rc", [P, HEADS])
        sq = sb("sqa", [P, E])
        identb = sb("identb", [P, P], BF16)
        maskb = sb("maskb", [P, P], BF16)
        lam = sb("lamt", [P, 68])
        block = ctx.enter_context(nc.Block())

        def unit(n):
            i, h = n // HEADS, n % HEADS
            return i, i % TB, h

        def groups(n):
            c = unit(n)[1]
            return [range(g, min(g + 4, c + 1)) for g in range(0, c + 1, 4)]

        at, first = 0, []
        for n in range(UNITS):
            first.append(at)
            at += len(groups(n))
        first.append(at)

        def half(n, u, wide):
            if unit(n)[1] < 4:
                return ps[:, 2 * u + n % 2, 0:wide]
            return ps[:, 2 * u:2 * u + 2, :].rearrange("p b t -> p (b t)")[:, 0:wide]

        @block.tensor
        def _(pe):
            def scores(n, u):
                i, c, h = unit(n)
                keys = (i - c) * P
                before = n - 1 if c >= 4 or (n and unit(n - 1)[1] >= 4) else n - 2
                if before >= 0:
                    pe.wait_ge(k.a_exp, 2 * before + u + 1)
                s = 2 * h + u
                q = k.qT[:, s, i * P:(i + 1) * P]
                out = half(n, u, (c + 1) * P)
                for at in range(0, c * P, W):
                    to = min(at + W, c * P)
                    nc.tensor.matmul(out[:, at:to], q, k.kT[:, s // 4, keys + at:keys + to], start=True, stop=True)
                own = out[:, c * P:(c + 1) * P]
                nc.tensor.matmul(own, q, k.kT[:, s // 4, i * P:(i + 1) * P], start=True, stop=False)
                nc.tensor.matmul(own, identb[:, :], maskb[:, :], start=False, stop=True).then_inc(k.a_qk, 1)

            def turn(n):
                pe.wait_ge(k.a_d, n + 1)
                for g, blks in enumerate(groups(n)):
                    if first[n] + g >= 2:
                        pe.wait_ge(k.a_ev, first[n] + g - 1)
                    for j in blks:
                        last = nc.tensor.transpose(ps[:, TR + (first[n] + g) % 2, (j % 4) * P:(j % 4 + 1) * P],
                                                   pr[:, n % 3, 0, j * P:(j + 1) * P], k.const("ident"))
                    last.then_inc(k.a_tr, 1)

            def product(n):
                i, c, h = unit(n)
                if h == 0 and i >= 2:
                    pe.wait_ge(k.a_att, i - 1)
                for g, blks in enumerate(groups(n)):
                    pe.wait_ge(k.a_ev, first[n] + g + 1)
                    for j in blks:
                        last = nc.tensor.matmul(ps[:, PV + i % 2, h * 64:(h + 1) * 64], dT[:, n % 2, j, :],
                                                k.v[:, i - c + j, h * 64:(h + 1) * 64], start=(h == 0 and j == 0),
                                                stop=(j == c), skip_group_check=True)
                last.then_inc(k.a_pv, 1)

            pe.wait_ge(k.a_mask, 2)
            for n in range(UNITS + 2):
                if n >= 2:
                    turn(n - 2)
                if n < UNITS:
                    scores(n, 0)
                    scores(n, 1)
                if n >= 2:
                    product(n - 2)

        @block.scalar
        def _(act):
            act.wait_ge(k.a_lam, 1)
            nc.scalar.activation(lam[:, 64:66], lam[:, 64:66], ACT.Exp).then_inc(k.a_lexp, 1)

            def turn(n):
                for g, blks in enumerate(groups(n)):
                    act.wait_ge(k.a_tr, first[n] + g + 1)
                    if n >= 2 and g == 0:
                        act.wait_ge(k.a_pv, n - 1)
                    nc.scalar.copy(dT[:, n % 2, blks[0]:blks[-1] + 1, :],
                                   ps[:, TR + (first[n] + g) % 2, 0:len(blks) * P].rearrange("p (j t) -> p j t", t=P)
                                   ).then_inc(k.a_ev, 1)

            def exponentials(n, u):
                wide = (unit(n)[1] + 1) * P
                act.wait_ge(k.a_max, 2 * n + u + 1)
                if n >= 3 and u == 0:
                    act.wait_ge(k.a_tr, first[n - 2])
                nc.scalar.activation(pr[:, n % 3, u, 0:wide], half(n, u, wide), ACT.Exp, bias=nmax[:, n % 2, u:u + 1],
                                     accum_out=sums[:, u, n:n + 1]).then_inc(k.a_exp, 1)

            for n in range(UNITS + 2):
                if n >= 2:
                    turn(n - 2)
                if n < UNITS:
                    exponentials(n, 0)
                    exponentials(n, 1)

        @block.vector
        def _(dve):
            then = chain(k, dve, "dve")
            nc.vector.tensor_copy(identb[:, :], k.const("ident")).then_inc(k.a_mask, 1)
            nc.vector.tensor_copy(maskb[:, :], k.const("causal")).then_inc(k.a_mask, 1)
            l = k.row("lam", 0, 128).rearrange("p (a q d) -> p a q d", a=2, q=2)
            then(nc.vector.tensor_tensor(lam[:, 0:64].rearrange("p (a d) -> p a d", a=2), l[:, :, 0, :], l[:, :, 1, :],
                                         ALU.mult))
            nc.vector.tensor_reduce(lam[:, 64:66], lam[:, 0:64].rearrange("p (a d) -> p a d", a=2), AX.X,
                                    ALU.add).then_inc(k.a_lam, 1)
            dve.wait_ge(k.a_lexp, 1)
            then(nc.vector.tensor_tensor(lam[:, 66:67], lam[:, 65:66], lam[:, 64:65], ALU.subtract))
            then(nc.vector.tensor_scalar(lam[:, 67:68], lam[:, 66:67], -LAMBDA_INIT, None, ALU.add))

            def largest(n, u):
                wide = (unit(n)[1] + 1) * P
                dve.wait_ge(k.a_qk, 2 * n + u + 1)
                if n >= 2:
                    dve.wait_ge(k.a_exp, 2 * n - 3 + u)
                nc.vector.tensor_reduce(nmax[:, n % 2, u:u + 1], half(n, u, wide), AX.X, ALU.max,
                                        negate=True).then_inc(k.a_max, 1)

            def difference(n):
                wide = (unit(n)[1] + 1) * P
                dve.wait_ge(k.a_exp, 2 * n + 2)
                then(nc.vector.reciprocal(rr[:, 0:1], sums[:, 1, n:n + 1]))
                then(nc.vector.scalar_tensor_tensor(rr[:, 1:2], sums[:, 0, n:n + 1], rr[:, 0:1], lam[:, 67:68],
                                                    ALU.mult, ALU.mult))
                nc.vector.scalar_tensor_tensor(pr[:, n % 3, 0, 0:wide], pr[:, n % 3, 1, 0:wide], rr[:, 1:2],
                                               pr[:, n % 3, 0, 0:wide], ALU.mult, ALU.add).then_inc(k.a_d, 1)

            def collect(i):
                dve.wait_ge(k.a_pv, HEADS * (i + 1))
                then(nc.vector.reciprocal(rc[:, :], sums[:, 0, HEADS * i:HEADS * (i + 1)]))
                heads = k.att[:, i, :].rearrange("p (h d) -> p h d", h=HEADS)
                nc.vector.tensor_tensor(heads, ps[:, PV + i % 2, 0:E].rearrange("p (h d) -> p h d", h=HEADS),
                                        rc[:, :].unsqueeze(2).to_broadcast([P, HEADS, 64]),
                                        ALU.mult).then_inc(k.a_att, 1)
                dve.wait_ge(k.a_att, i + 1)
                then(nc.vector.tensor_tensor(sq[:, :], k.att[:, i, :], k.att[:, i, :], ALU.mult))
                then(nc.vector.tensor_reduce(k.ms[:, i, :], sq[:, :].rearrange("p (h d) -> p h d", h=HEADS), AX.X,
                                             ALU.add))

            for n in range(UNITS):
                if n:
                    difference(n - 1)
                largest(n, 0)
                largest(n, 1)
                if n % HEADS == 2 and n > 2:
                    collect(n // HEADS - 1)
            difference(UNITS - 1)
            collect(NT - 1)
            dve.wait_ge(k.a_d, UNITS)


def attention_norm_phase(nc, k):
    with nc.Block() as block:
        @block.scalar
        def _(act):
            nc.scalar.activation(k.ms[:, :, :], k.ms[:, :, :], ACT.Sqrt, bias=k.eps[:, 0:1],
                                 scale=1.0 / 64).then_inc(k.n_sd, 1)

        @block.vector
        def _(dve):
            then = chain(k, dve, "dve")
            dve.wait_ge(k.n_sd, 1)
            then(nc.vector.reciprocal(k.ms[:, :, :], k.ms[:, :, :]))
            then(nc.vector.tensor_scalar(k.ms[:, :, :], k.ms[:, :, :], 1.0 - LAMBDA_INIT, None, ALU.mult))
            heads = k.att[:, :, :].rearrange("p i (h d) -> p (i h) d", h=HEADS)
            scale = k.ms[:, :, :].rearrange("p i h -> p (i h)").unsqueeze(2).to_broadcast([P, NT * HEADS, 64])
            half = NT * HEADS // 2
            nc.vector.tensor_tensor(heads[:, 0:half], heads[:, 0:half], scale[:, 0:half], ALU.mult).then_inc(k.n_1, 1)

        @block.gpsimd
        def _(pool):
            pool.wait_ge(k.n_1, 1)
            heads = k.att[:, :, :].rearrange("p i (h d) -> p (i h) d", h=HEADS)
            scale = k.ms[:, :, :].rearrange("p i h -> p (i h)").unsqueeze(2).to_broadcast([P, NT * HEADS, 64])
            half = NT * HEADS // 2
            nc.gpsimd.tensor_tensor(heads[:, half:], heads[:, half:], scale[:, half:], ALU.mult)


def attention_out_phase(nc, k):
    with nc.Block() as block:
        @block.tensor
        def _(pe):
            for i in range(NT):
                if i >= 8:
                    pe.wait_ge(k.n_x, i - 7)
                for j in range(EB):
                    last = nc.tensor.matmul(k.ps[:, i % 8, 0:E], k.hT[:, j, i * P:(i + 1) * P], k.wo[:, j, :],
                                            start=(j == 0), stop=(j == EB - 1))
                last.then_inc(k.n_mm, 1)

        @block.vector
        def _(dve):
            for i in range(NT):
                dve.wait_ge(k.n_mm, i + 1)
                nc.vector.tensor_tensor(k.X[:, i, 0:E], k.X[:, i, 0:E], k.ps[:, i % 8, 0:E],
                                        ALU.add).then_inc(k.n_x, 1)


SLOTS = E1 * CAP
ST = SLOTS // P
OUTSIDE = 1.0e5


def subject_phase(nc, k):
    ps = k.ps
    with ExitStack() as ctx:
        def sb(name, shape, dt=F32):
            return ctx.enter_context(nc.sbuf_tensor(name, shape, dt))

        it = sb("it1", [1, B], I32)
        ws = sb("ws", [P, B, EB, E])
        bs = sb("bs", [P, B, EB])
        wgt = sb("wgt", [P, EB, E1])
        zero = sb("zero", [P, E])
        cT = sb("cT", [P, EB, N])
        lg = sb("lg1", [P, NT, E1])
        v8 = sb("v81", [P, NT, 8])
        i8 = sb("i81", [P, NT, 8], U32)
        ix = sb("ix", [P, NT])
        oh = sb("oh1", [P, NT, E1])
        base = sb("base1", [P, NT, E1])
        tot = sb("tot1", [P, NT, E1])
        keep = sb("keep", [P, NT])
        slot = sb("slot", [P, NT])
        tmp = sb("tmp1", [P, NT])
        LG, CUM = 0, 1
        block = ctx.enter_context(nc.Block())

        @block.sync
        def _(sp):
            sp.dma_start(it[:, :], k.d["itok1"].unsqueeze(0)).then_inc(k.s_it1, 16)
            sp.dma_start(wgt[:, :, :], k.d["wgt"]).then_inc(k.s_wgt, 16)
            sp.wait_ge(k.s_it1, 16)
            for b in range(B):
                s = sp.value_load(it[0:1, b:b + 1], min_val=0, max_val=NSUB - 1)
                sp.dma_start(ws[:, b, :, :], k.d["subw"][bass.ds(s, 1)].squeeze(0)).then_inc(k.s_ws[b], 16)
                sp.dma_start(bs[:, b, :], k.d["subb"][bass.ds(s, 1)].squeeze(0)).then_inc(k.s_ws[b], 16)
            sp.wait_ge(k.u_zero, 1)
            sp.dma_start(k.xs.rearrange("(p q) e -> p q e", p=P),
                         zero[:, :].unsqueeze(1).to_broadcast([P, ST, E])).then_inc(k.s_xz, 16)
            sp.wait_ge(k.s_xz, 16)

        @block.tensor
        def _(pe):
            for b in range(B):
                pe.wait_ge(k.s_ws[b], 32)
                for w in (2 * b, 2 * b + 1):
                    for f in range(EB):
                        for j in range(EB):
                            last = nc.tensor.matmul(ps[:, EB * w + f, :], ws[:, b, j, f * P:(f + 1) * P],
                                                    k.hT[:, j, w * W:(w + 1) * W], start=(j == 0), stop=(j == EB - 1))
                        last.then_inc(k.u_mm, 1)
            pe.wait_ge(k.u_c, 8)
            pe.wait_ge(k.s_wgt, 16)
            for i in range(NT):
                for j in range(EB):
                    last = nc.tensor.matmul(ps[:, LG, i * E1:(i + 1) * E1], cT[:, j, i * P:(i + 1) * P],
                                            wgt[:, j, :], start=(i == 0 and j == 0), stop=(j == EB - 1),
                                            skip_group_check=True)
            last.then_inc(k.u_lg, 1)
            for g in range(NT // 2):
                if g >= 6:
                    pe.wait_ge(k.u_row, g - 5)
                for t in range(2):
                    for f in range(EB):
                        last = nc.tensor.transpose(ps[:, 2 + g % 6, t * E + f * P:t * E + (f + 1) * P],
                                                   cT[:, f, (2 * g + t) * P:(2 * g + t + 1) * P], k.const("ident"))
                last.then_inc(k.u_tr, 1)
            pe.wait_ge(k.u_oh, 1)
            o = oh[:, :, :].rearrange("p i e -> p (i e)")
            nc.tensor.matmul(ps[:, CUM, 0:P], k.const("lt"), o, start=True, stop=True)
            nc.tensor.matmul(ps[:, CUM, P:2 * P], k.const("ones"), o, start=True, stop=True).then_inc(k.u_cum, 1)

        @block.scalar
        def _(act):
            for w in range(NW):
                for f in range(EB):
                    act.wait_ge(k.u_mm, EB * w + f + 1)
                    nc.scalar.activation(cT[:, f, w * W:(w + 1) * W], ps[:, EB * w + f, :], ACT.Identity,
                                         bias=bs[:, w // 2, f:f + 1]).then_inc(k.u_c, 1)
            act.wait_ge(k.u_sub, 1)
            nc.scalar.activation(lg[:, :, :], lg[:, :, :], ACT.Exp).then_inc(k.u_exp, 1)
            for g in range(NT // 2):
                act.wait_ge(k.u_tr, g + 1)
                nc.scalar.copy(k.rows2[:, 2 * g:2 * g + 2, :], ps[:, 2 + g % 6, :].rearrange("p (t e) -> p t e", t=2)
                               ).then_inc(k.u_row, 1)

        @block.vector
        def _(dve):
            then = chain(k, dve, "dve")
            nc.vector.memset(zero[:, :], 0.0).then_inc(k.u_zero, 1)
            wide = [P, NT, E1]
            dve.wait_ge(k.u_lg, 1)
            then(nc.vector.tensor_copy(lg[:, :, :], ps[:, LG, 0:P].rearrange("p (i e) -> p i e", e=E1)))
            for i in range(NT):
                last = nc.vector.max(v8[:, i, :], lg[:, i, :])
            then(last)
            for i in range(NT):
                last = nc.vector.max_index(i8[:, i, :], v8[:, i, :], lg[:, i, :])
            then(last)
            nc.vector.tensor_tensor(lg[:, :, :], lg[:, :, :], v8[:, :, 0:1].to_broadcast(wide),
                                    ALU.subtract).then_inc(k.u_sub, 1)
            then(nc.vector.tensor_copy(ix[:, :], i8[:, :, 0]))
            nc.vector.tensor_tensor(oh[:, :, :], k.const("iota", 0, E1).unsqueeze(1).to_broadcast(wide),
                                    ix[:, :].unsqueeze(2).to_broadcast(wide), ALU.is_equal).then_inc(k.u_oh, 1)
            dve.wait_ge(k.u_cum, 1)
            then(nc.vector.tensor_copy(tot[:, :, :], ps[:, CUM, P:2 * P].rearrange("p (i e) -> p i e", e=E1)))
            then(nc.vector.memset(base[:, 0, :], 0.0))
            for i in range(1, NT):
                then(nc.vector.tensor_tensor(base[:, i, :], base[:, i - 1, :], tot[:, i - 1, :], ALU.add))
            then(nc.vector.tensor_tensor(base[:, :, :], base[:, :, :],
                                         ps[:, CUM, 0:P].rearrange("p (i e) -> p i e", e=E1), ALU.add))
            then(nc.vector.tensor_tensor(base[:, :, :], base[:, :, :], oh[:, :, :], ALU.mult))
            then(nc.vector.tensor_reduce(slot[:, :], base[:, :, :], AX.X, ALU.add))
            then(nc.vector.tensor_scalar(keep[:, :], slot[:, :], float(CAP), None, ALU.is_lt))
            then(nc.vector.scalar_tensor_tensor(slot[:, :], ix[:, :], float(CAP), slot[:, :], ALU.mult, ALU.add))
            then(nc.vector.tensor_tensor(tmp[:, :], slot[:, :], keep[:, :], ALU.mult))
            nc.vector.tensor_copy(k.take[:, :], tmp[:, :])
            then(nc.vector.tensor_scalar(base[:, :, 0], keep[:, :], -OUTSIDE, OUTSIDE, ALU.mult, ALU.add))
            then(nc.vector.tensor_tensor(slot[:, :], slot[:, :], base[:, :, 0], ALU.add))
            nc.vector.tensor_copy(k.put[:, :], slot[:, :])
            dve.wait_ge(k.u_exp, 1)
            then(nc.vector.tensor_reduce(tmp[:, :], lg[:, :, :], AX.X, ALU.add))
            then(nc.vector.reciprocal(tmp[:, :], tmp[:, :]))
            nc.vector.tensor_tensor(k.gate[:, :], tmp[:, :], keep[:, :], ALU.mult)


def dispatch_phase(nc, k):
    ps = k.ps
    with ExitStack() as ctx:
        xr = ctx.enter_context(nc.sbuf_tensor("xr", [P, ST, E], F32))
        block = ctx.enter_context(nc.Block())

        @block.gpsimd
        def _(pool):
            for i in range(NT):
                nc.gpsimd.indirect_dma_start(out=k.xs, out_offset=bass.IndirectOffsetOnAxis(ap=k.put[:, i:i + 1], axis=0),
                                             in_=k.rows2[:, i, :], in_offset=None, bounds_check=SLOTS - 1,
                                             oob_is_err=False).then_inc(k.s_put, 16)

        @block.sync
        def _(sp):
            for e in range(2):
                load_second_mixture(sp, k, e)
            sp.dma_start(k.b2b[:, :, :], k.d["b2b"].partition_broadcast(P)).then_inc(k.s_b2b, 16)
            sp.wait_ge(k.s_put, 16 * NT)
            for q in range(5):
                n = ST // 5
                sp.dma_start(xr[:, q * n:(q + 1) * n, :], k.xs.rearrange("(g p) e -> p g e", p=P)[:, q * n:(q + 1) * n, :]
                             ).then_inc(k.s_xr[q], 16)

        @block.tensor
        def _(pe):
            for g in range(ST // 2):
                if g % 2 == 0:
                    pe.wait_ge(k.s_xr[g // 2], 16)
                if g >= 8:
                    pe.wait_ge(k.v_lo, g - 7)
                for f in range(EB):
                    for t in range(2):
                        last = nc.tensor.transpose(ps[:, g % 8, f * 2 * P + t * P:f * 2 * P + (t + 1) * P],
                                                   xr[:, 2 * g + t, f * P:(f + 1) * P], k.const("ident"))
                last.then_inc(k.v_tr, 1)

        def bank(g):
            return ps[:, g % 8, :].rearrange("p (f t) -> p f t", f=EB)

        @block.scalar
        def _(act):
            act.wait_ge(k.s_f[0], 32)
            nc.scalar.copy(k.fp1[0][:, :, :], k.fw1[0][:, :, :]).then_inc(k.f_h1, 1)
            for g in range(ST // 2):
                act.wait_ge(k.v_tr, g + 1)
                nc.scalar.copy(k.xsT[0][:, :, g * 2 * P:(g + 1) * 2 * P], bank(g)).then_inc(k.v_hi, 1)

        @block.vector
        def _(dve):
            dve.wait_ge(k.s_f[0], 32)
            nc.vector.tensor_copy(k.fp2[0][:, :, :], k.fw2[0][:, :, :]).then_inc(k.f_h2, 1)
            dve.wait_ge(k.f_h1, 1)
            nc.vector.tensor_tensor(k.fp1[1][:, :, :], k.fw1[0][:, :, :], k.fp1[0][:, :, :],
                                    ALU.subtract).then_inc(k.f_split, 1)
            dve.wait_ge(k.f_h2, 1)
            nc.vector.tensor_tensor(k.fp2[1][:, :, :], k.fw2[0][:, :, :], k.fp2[0][:, :, :],
                                    ALU.subtract).then_inc(k.f_split, 1)
            for g in range(ST // 2):
                at = slice(g * 2 * P, (g + 1) * 2 * P)
                dve.wait_ge(k.v_hi, g + 1)
                nc.vector.tensor_tensor(k.xsT[1][:, :, at], bank(g), k.xsT[0][:, :, at],
                                        ALU.subtract).then_inc(k.v_lo, 1)


def load_second_mixture(sp, k, e):
    sp.dma_start(k.fw1[e % 2][:, :, :], k.d["fw1"][e]).then_inc(k.s_f[e % 2], 16)
    sp.dma_start(k.fw2[e % 2][:, :, :], k.d["fw2"][e]).then_inc(k.s_f[e % 2], 16)


def capacity_phase(nc, k):
    ps = k.ps
    chunks = [(0, P), (P, P), (2 * P, CAP - 2 * P)]
    NC = len(chunks)
    with ExitStack() as ctx:
        def sb(name, shape, dt=F32):
            return ctx.enter_context(nc.sbuf_tensor(name, shape, dt))

        w1 = [k.fp1, [sb(f"fw1_{part}", [P, EB, FF], F32R) for part in "hl"]]
        w2 = [k.fp2, [sb(f"fw2_{part}", [P, FB, E], F32R) for part in "hl"]]
        RING = 4
        hid = sb("fhid", [P, RING, CAP])
        hidp = [sb(f"fhid{part}", [P, FB, CAP], F32R) for part in "hl"]
        yr = sb("yr", [P, 2, NC, E])
        block = ctx.enter_context(nc.Block())
        DOWN = 4

        @block.sync
        def _(sp):
            for e in range(E1):
                if e + 2 < E1:
                    sp.wait_ge(k.f_split, 2 * (e + 1))
                    load_second_mixture(sp, k, e + 2)
                for c, (at, m) in enumerate(chunks):
                    sp.wait_ge(k.f_y, e * NC + c + 1)
                    sp.dma_start(k.ys[e * CAP + at:e * CAP + at + m, :], yr[0:m, e % 2, c, :]
                                 ).then_inc(k.s_ys[e % 2], 16)
            for q in range(2):
                sp.wait_ge(k.s_ys[q], 16 * NC * E1 // 2)

        @block.gpsimd
        def _(pool):
            for e in range(1, E1):
                q = e % 2
                pool.wait_ge(k.f_h1, e + 1)
                nc.gpsimd.tensor_tensor(w1[q][1][:, :, :], k.fw1[q][:, :, :], w1[q][0][:, :, :],
                                        ALU.subtract).then_inc(k.f_split, 1)
                pool.wait_ge(k.f_h2, e + 1)
                nc.gpsimd.tensor_tensor(w2[q][1][:, :, :], k.fw2[q][:, :, :], w2[q][0][:, :, :],
                                        ALU.subtract).then_inc(k.f_split, 1)

        @block.tensor
        def _(pe):
            for e in range(E1):
                q = e % 2
                tok = slice(e * CAP, (e + 1) * CAP)
                pe.wait_ge(k.f_split, 2 * e + 1)
                for f in range(FB):
                    g = e * FB + f
                    if g >= 4:
                        pe.wait_ge(k.f_act, g - 3)
                    for j in range(EB):
                        last = product3(nc, ps[:, g % 4, 0:CAP], [w[:, j, f * P:(f + 1) * P] for w in w1[q]],
                                        [x[:, j, tok] for x in k.xsT], j == 0, j == EB - 1)
                    last.then_inc(k.f_up, 1)
                pe.wait_ge(k.f_split, 2 * e + 2)
                for c, (at, m) in enumerate(chunks):
                    if e:
                        pe.wait_ge(k.f_y, (e - 1) * NC + c + 1)
                    for f in range(FB):
                        if c == 0:
                            pe.wait_ge(k.f_lo, e * FB + f + 1)
                        last = product3(nc, ps[0:m, DOWN + c, 0:E], [h[:, f, at:at + m] for h in hidp],
                                        [w[:, f, :] for w in w2[q]], f == 0, f == FB - 1)
                    last.then_inc(k.f_down, 1)

        def high_part(eng, copy, e, dst, src, done):
            if e >= 2:
                eng.wait_ge(k.f_down, NC * (e - 1))
            eng.wait_ge(k.s_f[e % 2], 32 * (e // 2 + 1))
            copy(dst[e % 2][0][:, :, :], src[e % 2][:, :, :]).then_inc(done, 1)

        @block.scalar
        def _(act):
            for e in range(E1):
                for f in range(FB):
                    g = e * FB + f
                    if f == (2 if e else 0) and e + 1 < E1:
                        high_part(act, nc.scalar.copy, e + 1, w1, k.fw1, k.f_h1)
                    act.wait_ge(k.f_up, g + 1)
                    if g >= RING:
                        act.wait_ge(k.f_lo, g - RING + 1)
                    nc.scalar.activation(hid[:, g % RING, :], ps[:, g % 4, 0:CAP], ACT.Relu,
                                         bias=k.col("b1b", g)).then_inc(k.f_act, 1)

        @block.vector
        def _(dve):
            for e in range(E1):
                if e + 1 < E1:
                    high_part(dve, nc.vector.tensor_copy, e + 1, w2, k.fw2, k.f_h2)
                if e:
                    dve.wait_ge(k.f_down, NC * e)
                for f in range(FB):
                    g = e * FB + f
                    dve.wait_ge(k.f_act, g + 1)
                    nc.vector.tensor_copy(hidp[0][:, f, :], hid[:, g % RING, :]).then_inc(k.f_dhi, 1)
                    dve.wait_ge(k.f_dhi, g + 1)
                    nc.vector.tensor_tensor(hidp[1][:, f, :], hid[:, g % RING, :], hidp[0][:, f, :],
                                            ALU.subtract).then_inc(k.f_lo, 1)
                for c, (at, m) in enumerate(chunks):
                    dve.wait_ge(k.f_down, e * NC + c + 1)
                    if e >= 2 and c == 0:
                        dve.wait_ge(k.s_ys[e % 2], 16 * NC * (e // 2))
                    nc.vector.tensor_tensor(yr[0:m, e % 2, c, :], ps[0:m, DOWN + c, 0:E], k.b2b[0:m, e, :],
                                            ALU.add).then_inc(k.f_y, 1)


def combine_phase(nc, k):
    with ExitStack() as ctx:
        g = ctx.enter_context(nc.sbuf_tensor("g", [P, NT, E], F32))
        block = ctx.enter_context(nc.Block())

        @block.gpsimd
        def _(pool):
            for i in range(NT):
                nc.gpsimd.indirect_dma_start(out=g[:, i, :], out_offset=None, in_=k.ys,
                                             in_offset=bass.IndirectOffsetOnAxis(ap=k.take[:, i:i + 1], axis=0)
                                             ).then_inc(k.s_take[i], 16)

        @block.vector
        def _(dve):
            for i in range(NT):
                dve.wait_ge(k.s_take[i], 16)
                nc.vector.scalar_tensor_tensor(g[:, i, :], g[:, i, :], k.gate[:, i:i + 1], k.X[:, i, 0:E], ALU.mult,
                                               ALU.add).then_inc(k.g_x, 1)

        @block.sync
        def _(sp):
            out = k.d["out"].rearrange("(i p) e -> p i e", p=P)
            for q in range(4):
                sp.wait_ge(k.g_x, 4 * (q + 1))
                sp.dma_start(out[:, 4 * q:4 * q + 4, :], g[:, 4 * q:4 * q + 4, :]).then_inc(k.s_out, 16)
            sp.wait_ge(k.s_out, 64)


def taken(nc):
    def take(names):
        handles = [nc.alloc_semaphore(name) for name in names.split()]
        take.handles += handles
        return handles
    take.handles = []
    return take


def network(nc, d):
    class Shared:
        pass

    k = Shared()
    k.d = d
    with ExitStack() as ctx:
        def sb(name, shape, dt=F32):
            return ctx.enter_context(nc.sbuf_tensor(name, shape, dt))

        k.cols = sb("cols", [P, NCOL])
        k.rows = sb("rows", [P, NROW])
        k.consts = sb("consts", [P, NCONST])
        k.eps = sb("eps", [P, 1])
        k.X = sb("X", [P, NT, E + 1])
        k.ps = ctx.enter_context(nc.psum_tensor("ps", [P, 8, W], F32))

        def piece(tensor, table, name, at, n):
            return tensor[:, table[name][0] + at:table[name][0] + at + n]

        k.col = lambda name, at, n=1: piece(k.cols, COL_AT, name, at, n)
        k.row = lambda name, at, n=1: piece(k.rows, ROW_AT, name, at, n)
        k.const = lambda name, at=0, n=P: piece(k.consts, CONST_AT, name, at, n)

        k.s_out, k.s_it1, k.s_wC = taken(nc)("s_out s_it1 s_wC")
        k.chains = {n: (ctx.enter_context(nc.semaphore(f"own_{n}")), [0]) for n in ("dve", "act", "pool")}
        first = taken(nc)
        k.s_small, k.s_rows, k.s_wA, k.s_wB, k.s_x, k.s_xT_0, k.s_xT_1 = first("s_small s_rows s_wA s_wB s_x s_xT_0 s_xT_1")
        k.s_xT_2, k.s_xT_3, k.c_mm, k.c_evac, k.c_ctx, k.c_w2b, k.c_blend = first("s_xT_2 s_xT_3 c_mm c_evac c_ctx c_w2b c_blend")
        k.c_sg, k.c_out, k.c_tau, k.c_bdiff, k.c_bexp, k.c_var, k.c_sd = first("c_sg c_out c_tau c_bdiff c_bexp c_var c_sd")
        k.c_dve, k.c_init, k.c_norm, k.c_aff, k.c_hn = first("c_dve c_init c_norm c_aff c_hn")
        k.i_dt, k.i_evac, k.i_mm, k.i_dtA, k.i_sp, k.i_cs, k.i_expA = first("i_dt i_evac i_mm i_dtA i_sp i_cs i_expA")
        k.i_abs, k.i_ln, k.i_conv, k.i_pad, k.i_silu, k.s_ct, k.s_mw = first("i_abs i_ln i_conv i_pad i_silu s_ct s_mw")
        k.m_xst, k.m_xt, k.m_bcu, k.m_bc, k.m_G, k.m_E, k.m_seg = first("m_xst m_xt m_bcu m_bc m_G m_E m_seg")
        k.m_sz, k.m_z, k.m_M, k.m_xdt, k.m_y2, k.m_yd, k.m_h = first("m_sz m_z m_M m_xdt m_y2 m_yd m_h")
        k.m_y1, k.m_yo, k.m_xdd, k.m_S, k.m_yg, k.m_ss, k.m_xD = first("m_y1 m_yo m_xdd m_S m_yg m_ss m_xD")
        k.o_evac, k.o_tr, k.o_x, k.o_mm, k.o_var, k.o_sd, k.o_add = first("o_evac o_tr o_x o_mm o_var o_sd o_add")
        k.p_act, k.p_up, k.p_x, k.p_down = first("p_act p_up p_x p_down")
        k.r_k2, k.r_kk, k.r_G, k.r_lg, k.r_wd, k.r_cnt, k.r_tr = first("r_k2 r_kk r_G r_lg r_wd r_cnt r_tr")
        k.r_wT, k.r_b2, k.r_bo, k.r_v, k.r_exp, k.r_sel, k.e_y = first("r_wT r_b2 r_bo r_v r_exp r_sel e_y")
        k.e_act, k.e_up, k.e_down, k.s_e_0, k.s_e_1, k.r_hi = first("e_act e_up e_down s_e_0 s_e_1 r_hi")
        k.e_split, k.e_h1, k.e_h2, k.e_lo, k.e_dhi = first("e_split e_h1 e_h2 e_lo e_dhi")
        k.t_1, k.t_2, k.t_3, k.t_4, k.s_it = first("t_1 t_2 t_3 t_4 s_it")
        k.q_tanh, k.q_a, k.q_vb, k.q_srow, k.q_row, k.q_col, k.q_e8 = first("q_tanh q_a q_vb q_srow q_row q_col q_e8")
        k.q_U, k.q_sum, k.q_D, k.q_out, k.q_pool, k.q_ex, k.q_exp = first("q_U q_sum q_D q_out q_pool q_ex q_exp")
        k.q_dex, k.m_tz, k.s_mw2, k.p_w, k.p_wh = first("q_dex m_tz s_mw2 p_w p_wh")
        k.p_in, k.p_inh, k.p_hi, k.p_lo = first("p_in p_inh p_hi p_lo")
        k.s_xT = [k.s_xT_0, k.s_xT_1, k.s_xT_2, k.s_xT_3]
        k.s_e = [k.s_e_0, k.s_e_1]
        with ExitStack() as layer0:
            def arena(name, shape, dt=F32):
                return layer0.enter_context(nc.sbuf_tensor(name, shape, dt))

            k.win = arena("win", [P, EB, 1160])
            k.wop = arena("wop", [P, 4, E])
            k.c2w = arena("c2w", [P, EB, HID])
            k.keysT, k.rwT = (arena(n, [P, EB, E0]) for n in ("keysT", "rwT"))
            k.b2a = arena("b2a", [E0, E])
            k.hT = arena("hT", [P, EB, N])
            stream = layer0.enter_context(ExitStack())
            k.res0, k.hn = (stream.enter_context(nc.sbuf_tensor(n, [P, NT, E], F32)) for n in ("res0", "hn"))
            cond_phase(nc, k)
            with ExitStack() as mamba:
                def inner(name, shape, dt=F32):
                    return mamba.enter_context(nc.sbuf_tensor(name, shape, dt))

                k.post = inner("post", [P, CB, N])
                k.CT = inner("CT", [DS, N])
                k.rms = inner("rms", [P, NT])
                k.dt, k.dtA, k.ecs = (inner(n, [P, P]) for n in ("dt", "dtA", "ecs"))
                k.etot = inner("etot", [DS, P])
                k.expA = inner("expA", [P, NH])
                transpose_phase(nc, k, k.hn, k.hT, "ln1w", "ln1b", {"mm": k.t_1})
                inproj_phase(nc, k)
                ygB = inner("ygB", [P, NT // 2, DI])
                ygA = k.hn[:, :, :].rearrange("p i e -> p (i e)").rearrange("p (i e) -> p i e", e=DI)
                k.yg = lambda i: ygA[:, i, :] if i < NT // 2 else ygB[:, i - NT // 2, :]
                ssd_phase(nc, k)
                outproj_phase(nc, k)
            with ExitStack() as mlp:
                k.mw1 = mlp.enter_context(nc.sbuf_tensor("mw1", [P, EB, FF], F32))
                k.mw2 = mlp.enter_context(nc.sbuf_tensor("mw2", [P, FB, E], F32))
                transpose_phase(nc, k, k.hn, k.hT, "ln2w", "ln2b", {"mm": k.t_2}, load_mlp(k))
                mlp_phase(nc, k)
            transpose_phase(nc, k, k.X, k.hT, None, None, {"mm": k.t_3})
            stream.close()
            k.hTh, k.hTl = (arena(n, [P, EB, N], F32R) for n in ("hTh", "hTl"))
            pooled = layer0.enter_context(ExitStack())
            k.pooled = pooled.enter_context(nc.sbuf_tensor("pooled", [P, NT, E], F32))
            pool_phase(nc, k)
            transpose_phase(nc, k, k.pooled, k.hT, None, None, {"mm": k.t_4})
            pooled.close()
            k.wE = arena("wE", [P, E0, NT])
            k.wT = k.win[:, :, :].rearrange("p j n -> p (j n)")[0:E0, 0:N]
            k.w1s = [arena(f"ew1s_{q}", [P, EB, FF]) for q in range(2)]
            k.w2s = [arena(f"ew2s_{q}", [P, FB, E]) for q in range(2)]
            k.b1s = [arena(f"eb1s_{q}", [P, FB]) for q in range(2)]
            k.jobs = arena("jobs", [1, JT["blk"] + E0 * NB], I32)
            route_phase(nc, k)
            experts_phase(nc, k)
        nc.clear_and_free_semaphores(first.handles)
        nc.all_engine_barrier()
        second = taken(nc)
        k.t_5, k.t_6, k.t_7, k.l_mm, k.l_qk, k.l_vm, k.l_du = second("t_5 t_6 t_7 l_mm l_qk l_vm l_du")
        k.l_q, k.l_k, k.l_v, k.l_nb, k.l_zero = second("l_q l_k l_v l_nb l_zero")
        k.a_exp, k.a_qk, k.a_d, k.a_ev, k.a_tr, k.a_att, k.a_pv = second("a_exp a_qk a_d a_ev a_tr a_att a_pv")
        k.a_mask, k.a_lam, k.a_lexp, k.a_max, k.n_sd, k.n_1, k.n_mm = second("a_mask a_lam a_lexp a_max n_sd n_1 n_mm")
        [k.n_x] = second("n_x")
        k.s_wgt, k.s_xz, k.s_put, k.s_b2b, k.u_zero, k.u_mm, k.u_c = second("s_wgt s_xz s_put s_b2b u_zero u_mm u_c")
        k.u_lg, k.u_row, k.u_tr, k.u_oh, k.u_cum, k.u_sub, k.u_exp = second("u_lg u_row u_tr u_oh u_cum u_sub u_exp")
        k.v_tr, k.f_y, k.f_act, k.f_up, k.f_down, k.g_x = second("v_tr f_y f_act f_up f_down g_x")
        k.f_h1, k.f_h2, k.f_split, k.f_dhi, k.f_lo, k.v_hi, k.v_lo = second("f_h1 f_h2 f_split f_dhi f_lo v_hi v_lo")
        k.s_ws, k.s_f, k.s_ys = ([nc.alloc_semaphore(f"{n}{q}") for q in range(2)] for n in ("s_ws", "s_f", "s_ys"))
        k.s_xr = [nc.alloc_semaphore(f"s_xr{q}") for q in range(5)]
        k.s_take = [nc.alloc_semaphore(f"s_take{q}") for q in range(NT)]
        with ExitStack() as layer1:
            def arena(name, shape, dt=F32):
                return layer1.enter_context(nc.sbuf_tensor(name, shape, dt))

            with ExitStack() as attn:
                def inner(name, shape, dt=F32):
                    return attn.enter_context(nc.sbuf_tensor(name, shape, dt))

                k.hT = inner("hT1", [P, EB, N])
                k.wq, k.wk, k.wv, k.wo = (inner(n, [P, EB, E]) for n in ("wq", "wk", "wv", "wo"))
                k.qT, k.kT = inner("qT", [P, 8, N]), inner("kT", [P, EB, N])
                k.v, k.att = inner("v", [P, NT, E]), inner("att", [P, NT, E])
                k.ms = inner("ms", [P, NT, HEADS])
                transpose_phase(nc, k, k.X, k.hT, None, None, {"mm": k.t_5})
                laplace_phase(nc, k)
                attention_phase(nc, k)
                attention_norm_phase(nc, k)
                transpose_phase(nc, k, k.att, k.hT, "gam", None, {"mm": k.t_6})
                attention_out_phase(nc, k)
            k.xs = nc.dram_tensor("slot_rows", (SLOTS, E), F32, kind="Internal").ap()
            k.ys = nc.dram_tensor("slot_results", (SLOTS, E), F32, kind="Internal").ap()
            k.put, k.take = arena("put", [P, NT], U32), arena("take", [P, NT], U32)
            k.gate = arena("gate", [P, NT])
            k.fw1 = [arena(f"fw1s_{q}", [P, EB, FF]) for q in range(2)]
            k.fw2 = [arena(f"fw2s_{q}", [P, FB, E]) for q in range(2)]
            k.fp1 = [arena(f"fp1_{part}", [P, EB, FF], F32R) for part in "hl"]
            k.fp2 = [arena(f"fp2_{part}", [P, FB, E], F32R) for part in "hl"]
            k.b2b = arena("b2b", [P, E1, E])
            k.xsT = [arena(f"xsT{part}", [P, EB, SLOTS], F32R) for part in "hl"]
            with nc.sbuf_tensor("rows2", [P, NT, E], F32) as k.rows2, nc.sbuf_tensor("hT2", [P, EB, N], F32) as k.hT:
                transpose_phase(nc, k, k.X, k.hT, None, None, {"mm": k.t_7})
                subject_phase(nc, k)
                dispatch_phase(nc, k)
            capacity_phase(nc, k)
            combine_phase(nc, k)


def blocks(w):
    return w.reshape(w.shape[0] // P, P, w.shape[1]).transpose(1, 0, 2)


def layout(v):
    a = {}
    x = v["x"].reshape(N, E)
    a["x"], a["xT"] = x, x.T
    for n, w in (("wsoma", "L0_cond_Wsoma"), ("wtemp", "L0_cond_Wtemp"), ("wout", "L0_cond_Wout"),
                 ("wn1", "L0_cond_Wn1"), ("wg", "L0_cond_Wg"), ("win", "L0_attn_in_proj_w"),
                 ("wop", "L0_attn_out_proj_w"), ("mw1", "L0_attn_mlp_w1"), ("mw2", "L0_attn_mlp_w2"),
                 ("keysT", "L0_ffn_keys"), ("rwT", "L0_ffn_rw"), ("wq", "L1_attn_Wq"), ("wk", "L1_attn_Wk"),
                 ("wv", "L1_attn_Wv"), ("wo", "L1_attn_Wo")):
        a[n] = blocks(v[w].T)
    a["c2w"] = blocks(v["L0_cond2_W1"])
    a["b2a"] = v["L0_ffn_b2"]
    a["itok0"] = v["itok_B_0_2"]
    a["itok1"] = v["itok_B_0_7"]
    a["subw"] = v["L1_cond2_weight"].transpose(0, 2, 1).reshape(NSUB, EB, P, E).transpose(0, 2, 1, 3)
    a["subb"] = v["L1_cond2_bias"].reshape(NSUB, EB, P).transpose(0, 2, 1)
    a["wgt"] = blocks(v["L1_ffn_wg"])
    a["fw1"] = v["L1_ffn_w1"].reshape(E1, EB, P, FF).transpose(0, 2, 1, 3)
    a["fw2"] = v["L1_ffn_w2"].reshape(E1, FB, P, E).transpose(0, 2, 1, 3)
    a["b2b"] = v["L1_ffn_b2"]
    a["ew1"] = v["L0_ffn_w1"].transpose(0, 2, 1).reshape(E0, EB, P, FF).transpose(0, 2, 1, 3)
    a["ew2"] = v["L0_ffn_w2"].transpose(0, 2, 1).reshape(E0, FB, P, E).transpose(0, 2, 1, 3)
    a["eb1"] = v["L0_ffn_b1"].reshape(E0, FB, P).transpose(0, 2, 1)

    def column(x):
        x = x.reshape(-1)
        if x.size < P:
            return np.concatenate([x, np.zeros(P - x.size, x.dtype)])[:, None]
        return x.reshape(x.size // P, P).T

    cols = {"bg": v["L0_cond_bg"], "bn1": v["L0_cond_bn1"], "bsoma": v["L0_cond_bsoma"], "btemp": v["L0_cond_btemp"],
            "ln1w": v["L0_attn_ln1_w"], "ln1b": v["L0_attn_ln1_b"], "convb": v["L0_attn_conv_b"],
            "normw": v["L0_attn_norm_w"], "ln2w": v["L0_attn_ln2_w"], "ln2b": v["L0_attn_ln2_b"],
            "mlpb1": v["L0_attn_mlp_b1"], "c2b1": v["L0_cond2_b1"], "c2v": v["L0_cond2_v"]}
    cols = {n: column(x) for n, x in cols.items()}
    cols["blend"] = v["cond_1024"].reshape(2, EB, P).transpose(2, 1, 0).reshape(P, 4)
    cols["wn2"] = np.concatenate([column(v["cond_256"][0]), column(v["cond_256"][1])], 1)
    cols["convw"] = v["L0_attn_conv_w"].reshape(CB, P, 4).transpose(1, 0, 2).reshape(P, 20)
    cols["gam"] = column(np.concatenate([v["L1_attn_gamma"]] * 4))
    cols["b1a"] = v["L0_ffn_b1"].reshape(E0, FB, P).transpose(2, 0, 1).reshape(P, E0 * FB)
    cols["b1b"] = v["L1_ffn_b1"].reshape(E1, FB, P).transpose(2, 0, 1).reshape(P, E1 * FB)
    a["cols"] = np.concatenate([cols[n] for n, _ in COLS], 1)
    rows = {"tau": [v["condB_tauraws"], v["L0_cond_tau_ctx"]], "bn2": [v["condB_bn2"]], "gamma": [v["L0_cond_gamma"]],
            "beta": [v["L0_cond_beta"]], "dtb": [v["L0_attn_dt_bias"]], "alog": [v["L0_attn_A_log"]],
            "dskip": [v["L0_attn_D"]], "mlpb2": [v["L0_attn_mlp_b2"]], "rb": [v["L0_ffn_rb"]],
            "zx": [v["condB_zX"]], "zy": [v["condB_zY"]], "zr": [v["condB_zR"]],
            "lam": [v["L1_attn_lambda_q1"], v["L1_attn_lambda_k1"], v["L1_attn_lambda_q2"], v["L1_attn_lambda_k2"]]}
    a["rows"] = np.concatenate([x.reshape(-1) for n, _ in ROWS for x in rows[n]])
    a["consts"] = shape_constants()
    return a


def kernel(**inputs):
    import concourse.bacc as _bacc
    from concourse import mybir as _mybir
    from concourse.bass_utils import run_bass_kernel_spmd as _run

    nc = _bacc.Bacc("TRN2", target_bir_lowering=False, num_devices=1)
    arrays, d = {}, {}
    for name, a in layout({n: np.asarray(x) for n, x in inputs.items()}).items():
        a = np.ascontiguousarray(a)
        arrays[f"in_{name}_dram"] = a
        d[name] = nc.dram_tensor(f"in_{name}_dram", a.shape, _mybir.dt.from_np(a.dtype), kind="ExternalInput").ap()
    d["out"] = nc.dram_tensor("out_0_dram", (N, E), F32, kind="ExternalOutput").ap()
    network(nc, d)
    r = _run(nc, [arrays], core_ids=[0])
    return r.results[0]["out_0_dram"].reshape(B, T, E)
```
